# Optimizing a Trainium2 kernel written in Bass

```python
import numpy as np
import jax
import jax.numpy as jnp

def _softmax(x, axis=-1):
    return jax.nn.softmax(x, axis=axis)

def _gelu(x):
    return jax.nn.gelu(x, approximate=True)

def _silu(x):
    return jax.nn.silu(x)

def _sigmoid(x):
    return jax.nn.sigmoid(x)

def _layernorm(x, axis=-1, eps=1e-05):
    m = jnp.mean(x, axis=axis, keepdims=True)
    v = jnp.var(x, axis=axis, keepdims=True)
    return (x - m) / jnp.sqrt(v + eps)

def _scatter_add(tgt, idx, src, axis=0):
    return tgt.at[idx].add(src)

def _segment_sum(src, seg, n):
    return jax.ops.segment_sum(src, seg, n)
kernel_name = 'mk_xattn_ffn_d2_seqx_r8_bcc443'

def setup_inputs(seed: int=0):
    np.random.seed(seed)
    _w = jnp.asarray

    def _rec_inputs():
        import jax
        import jax.numpy as jnp
        _rk = jax.random.key(seed)
        x = -0.000125 + 0.9999 * jax.random.normal(jax.random.fold_in(_rk, 1), (2, 256, 512), jnp.float32)
        _lenS = 256 - jax.random.randint(jax.random.fold_in(_rk, 7), (2,), 0, max(1, 256 // 4) + 1, jnp.int32)
        _lenS2 = 512 - jax.random.randint(jax.random.fold_in(_rk, 8), (2,), 0, max(1, 512 // 4) + 1, jnp.int32)
        _ctx_4096P = jax.random.normal(jax.random.fold_in(_rk, 11), (2, 16, 512), jnp.float32)
        _ctx_4096c = jax.random.dirichlet(jax.random.fold_in(_rk, 511), 0.3 * jnp.ones((16,), jnp.float32), (2, 512))
        _ctx_4096t = jnp.einsum('bsk,bkd->bsd', _ctx_4096c, _ctx_4096P)
        _ctx_4096t = _ctx_4096t * jax.lax.rsqrt(jnp.mean(jnp.square(_ctx_4096t)) + 1e-12) * 0.953939
        ctx_4096 = -5.72187e-05 + 0.999849 * (_ctx_4096t + 0.3 * jax.random.normal(jax.random.fold_in(_rk, 611), (2, 512, 512), jnp.float32))
        _validS = jnp.arange(256)[None, :] < _lenS[:, None]
        _validS2 = jnp.arange(512)[None, :] < _lenS2[:, None]
        _causal = jnp.tril(jnp.ones((256, 256), dtype=bool))
        mask_1x1xSxS2_ff0 = jnp.where(jnp.ones((1, 1, 256, 512), dtype=bool), 0.0, -1000000000.0).astype(jnp.float32)
        return (x, ctx_4096, mask_1x1xSxS2_ff0)
    x, ctx_4096, mask_1x1xSxS2_ff0 = _rec_inputs()

    def _L0_xattn_setup():
        import jax, jax.numpy as jnp
        import numpy as np
        QMIN = 0.0
        QMAX = 255.0

        def fake_quant(x, scale, zp):
            s = scale.reshape(())
            z = zp.reshape(())
            q = jnp.clip(jnp.round(x / s + z), QMIN, QMAX)
            return (q - z) * s
        key = jax.random.key(seed)
        k1, k2 = jax.random.split(key)
        B, M, K, N = (4, 256, 512, 512)
        x1 = jax.random.normal(k1, (B, M, K), dtype=jnp.float32)
        x2 = jax.random.normal(k2, (B, K, N), dtype=jnp.float32)
        x1_scale = jnp.full((1,), 8.0 / 255.0, dtype=jnp.float32)
        x1_zp = jnp.full((1,), 128.0, dtype=jnp.float32)
        x2_scale = jnp.full((1,), 8.0 / 255.0, dtype=jnp.float32)
        x2_zp = jnp.full((1,), 128.0, dtype=jnp.float32)
        return {'x1': x1, 'x2': x2, 'x1_scale': x1_scale, 'x1_zp': x1_zp, 'x2_scale': x2_scale, 'x2_zp': x2_zp}
    _L0_xattn_all = _L0_xattn_setup()
    _L0_xattn_in = {k: v for k, v in _L0_xattn_all.items() if k in ('x1_scale', 'x1_zp', 'x2_scale', 'x2_zp')}
    del _L0_xattn_all

    def _L0_ffn_setup():
        import jax, jax.numpy as jnp
        import numpy as np
        DIM = 512
        INTER = 128
        E = 16
        GROUPS = 4
        LIM = 2
        K = 2
        SHARED_INTER = 2 * INTER
        SCALE = 1.0
        key = jax.random.key(seed)
        ks = jax.random.split(key, 16)

        def n(k, shape, s=0.02):
            return jax.random.normal(k, shape, jnp.float32) * s
        return {'x': jax.random.normal(ks[0], (1, 256, DIM), jnp.float32), 'router_w': n(ks[1], (DIM, E)), 'router_b': n(ks[2], (E,)), 'router_bias': n(ks[3], (E,), 1.0), 'ew1': n(ks[4], (E, DIM, INTER)), 'eb1': n(ks[5], (E, INTER)), 'ew2': n(ks[6], (E, DIM, INTER)), 'eb2': n(ks[7], (E, INTER)), 'ew3': n(ks[8], (E, INTER, DIM)), 'eb3': n(ks[9], (E, DIM)), 'sw1': n(ks[10], (DIM, SHARED_INTER)), 'sb1': n(ks[11], (SHARED_INTER,)), 'sw2': n(ks[12], (DIM, SHARED_INTER)), 'sb2': n(ks[13], (SHARED_INTER,)), 'sw3': n(ks[14], (SHARED_INTER, DIM)), 'sb3': n(ks[15], (DIM,))}
    _L0_ffn_all = _L0_ffn_setup()
    _L0_ffn_in = {k: v for k, v in _L0_ffn_all.items() if k in ('router_w', 'router_b', 'router_bias', 'ew1', 'eb1', 'ew2', 'eb2', 'ew3', 'eb3', 'sw1', 'sb1', 'sw2', 'sb2', 'sw3', 'sb3')}
    del _L0_ffn_all

    def _L1_xattn_setup():
        import jax, jax.numpy as jnp
        import numpy as np
        NUM_HEADS = 32
        NUM_KV_HEADS = 8
        HEAD_DIM = 128
        HIDDEN = 512
        EPS = 1e-05

        def rmsnorm(x, w, eps=EPS):
            xf = x.astype(jnp.float32)
            var = jnp.mean(xf * xf, axis=-1, keepdims=True)
            return w * (xf * jax.lax.rsqrt(var + eps)).astype(x.dtype)
        key = jax.random.key(seed)
        ks = jax.random.split(key, 10)
        B, Q, KV = (1, 128, 6404)
        s = 1.0 / np.sqrt(HIDDEN)
        return {'hidden_states': jax.random.normal(ks[0], (B, Q, HIDDEN), jnp.float32), 'cross_attention_states': jax.random.normal(ks[1], (B, KV, HIDDEN), jnp.float32), 'attention_mask': jnp.zeros((B, 1, Q, KV), jnp.float32), 'q_proj_w': jax.random.normal(ks[2], (NUM_HEADS * HEAD_DIM, HIDDEN), jnp.float32) * s, 'k_proj_w': jax.random.normal(ks[3], (NUM_KV_HEADS * HEAD_DIM, HIDDEN), jnp.float32) * s, 'v_proj_w': jax.random.normal(ks[4], (NUM_KV_HEADS * HEAD_DIM, HIDDEN), jnp.float32) * s, 'o_proj_w': jax.random.normal(ks[5], (HIDDEN, NUM_HEADS * HEAD_DIM), jnp.float32) * s, 'q_norm_w': jnp.ones((HEAD_DIM,), jnp.float32), 'k_norm_w': jnp.ones((HEAD_DIM,), jnp.float32)}
    _L1_xattn_all = _L1_xattn_setup()
    _L1_xattn_in = {k: v for k, v in _L1_xattn_all.items() if k in ('q_proj_w', 'k_proj_w', 'v_proj_w', 'o_proj_w', 'q_norm_w', 'k_norm_w')}
    del _L1_xattn_all

    def _L1_ffn_setup():
        import jax, jax.numpy as jnp
        import numpy as np
        IN_F = 512
        OUT_F = 512
        RANK = 8
        NUM_EXPERTS = 64
        TOP_K = 16
        ROUTER_DIM = 16
        ALPHA = 32
        SCALING = ALPHA / TOP_K
        BOTTLENECK = NUM_EXPERTS * RANK
        key = jax.random.key(seed)
        ks = jax.random.split(key, 5)
        x = jax.random.normal(ks[0], (4, 512, IN_F), dtype=jnp.float32)
        bound_a = float(np.sqrt(6.0 / IN_F))
        A_w = jax.random.uniform(ks[1], (BOTTLENECK, IN_F), jnp.float32, -bound_a, bound_a)
        B_w = jax.random.normal(ks[2], (OUT_F, BOTTLENECK), dtype=jnp.float32) * 0.02
        Wq_w = jax.random.normal(ks[3], (ROUTER_DIM, IN_F), dtype=jnp.float32) * 0.02
        keys = jax.random.normal(ks[4], (NUM_EXPERTS, ROUTER_DIM), dtype=jnp.float32) * 0.01
        return {'x': x, 'A_w': A_w, 'B_w': B_w, 'Wq_w': Wq_w, 'keys': keys}
    _L1_ffn_all = _L1_ffn_setup()
    _L1_ffn_in = {k: v for k, v in _L1_ffn_all.items() if k in ('A_w', 'B_w', 'Wq_w', 'keys')}
    del _L1_ffn_all
    return {'x': x, 'ctx_4096': ctx_4096, 'mask_1x1xSxS2_ff0': mask_1x1xSxS2_ff0, 'L0_xattn_x1_scale': _L0_xattn_in['x1_scale'], 'L0_xattn_x1_zp': _L0_xattn_in['x1_zp'], 'L0_xattn_x2_scale': _L0_xattn_in['x2_scale'], 'L0_xattn_x2_zp': _L0_xattn_in['x2_zp'], 'L0_ffn_router_w': _L0_ffn_in['router_w'], 'L0_ffn_router_b': _L0_ffn_in['router_b'], 'L0_ffn_router_bias': _L0_ffn_in['router_bias'], 'L0_ffn_ew1': _L0_ffn_in['ew1'], 'L0_ffn_eb1': _L0_ffn_in['eb1'], 'L0_ffn_ew2': _L0_ffn_in['ew2'], 'L0_ffn_eb2': _L0_ffn_in['eb2'], 'L0_ffn_ew3': _L0_ffn_in['ew3'], 'L0_ffn_eb3': _L0_ffn_in['eb3'], 'L0_ffn_sw1': _L0_ffn_in['sw1'], 'L0_ffn_sb1': _L0_ffn_in['sb1'], 'L0_ffn_sw2': _L0_ffn_in['sw2'], 'L0_ffn_sb2': _L0_ffn_in['sb2'], 'L0_ffn_sw3': _L0_ffn_in['sw3'], 'L0_ffn_sb3': _L0_ffn_in['sb3'], 'L1_xattn_q_proj_w': _L1_xattn_in['q_proj_w'], 'L1_xattn_k_proj_w': _L1_xattn_in['k_proj_w'], 'L1_xattn_v_proj_w': _L1_xattn_in['v_proj_w'], 'L1_xattn_o_proj_w': _L1_xattn_in['o_proj_w'], 'L1_xattn_q_norm_w': _L1_xattn_in['q_norm_w'], 'L1_xattn_k_norm_w': _L1_xattn_in['k_norm_w'], 'L1_ffn_A_w': _L1_ffn_in['A_w'], 'L1_ffn_B_w': _L1_ffn_in['B_w'], 'L1_ffn_Wq_w': _L1_ffn_in['Wq_w'], 'L1_ffn_keys': _L1_ffn_in['keys']}

def reference(x, ctx_4096, mask_1x1xSxS2_ff0, L0_xattn_x1_scale, L0_xattn_x1_zp, L0_xattn_x2_scale, L0_xattn_x2_zp, L0_ffn_router_w, L0_ffn_router_b, L0_ffn_router_bias, L0_ffn_ew1, L0_ffn_eb1, L0_ffn_ew2, L0_ffn_eb2, L0_ffn_ew3, L0_ffn_eb3, L0_ffn_sw1, L0_ffn_sb1, L0_ffn_sw2, L0_ffn_sb2, L0_ffn_sw3, L0_ffn_sb3, L1_xattn_q_proj_w, L1_xattn_k_proj_w, L1_xattn_v_proj_w, L1_xattn_o_proj_w, L1_xattn_q_norm_w, L1_xattn_k_norm_w, L1_ffn_A_w, L1_ffn_B_w, L1_ffn_Wq_w, L1_ffn_keys):
    import jax
    import jax.numpy as jnp

    def _L0_xattn_ref(x1, x2, x1_scale, x1_zp, x2_scale, x2_zp):
        import jax, jax.numpy as jnp
        import numpy as np
        QMIN = 0.0
        QMAX = 255.0

        def fake_quant(x, scale, zp):
            s = scale.reshape(())
            z = zp.reshape(())
            q = jnp.clip(jnp.round(x / s + z), QMIN, QMAX)
            return (q - z) * s
        q1 = fake_quant(x1, x1_scale, x1_zp)
        q2 = fake_quant(x2, x2_scale, x2_zp)
        return jnp.matmul(q1, q2)

    def _L0_ffn_ref(x, router_w, router_b, router_bias, ew1, eb1, ew2, eb2, ew3, eb3, sw1, sb1, sw2, sb2, sw3, sb3):
        import jax, jax.numpy as jnp
        import numpy as np
        DIM = 512
        INTER = 128
        E = 16
        GROUPS = 4
        LIM = 2
        K = 2
        SHARED_INTER = 2 * INTER
        SCALE = 1.0
        shape = x.shape
        xt = x.reshape(-1, DIM)
        T = xt.shape[0]
        logits = xt @ router_w + router_b
        scores = jax.nn.softmax(logits.astype(jnp.float32), axis=-1) + router_bias
        g = scores.reshape(T, GROUPS, E // GROUPS)
        _, gidx = jax.lax.top_k(g.max(axis=-1), LIM)
        keep = jnp.zeros((T, GROUPS), bool).at[jnp.arange(T)[:, None], gidx].set(True)
        masked = jnp.where(keep[:, :, None], g, -jnp.inf).reshape(T, E)
        _, idx = jax.lax.top_k(masked, K)
        vals = (jnp.take_along_axis(scores, idx, axis=1) * SCALE).astype(x.dtype)
        gate = jnp.zeros((T, E), x.dtype).at[jnp.arange(T)[:, None], idx].add(vals)

        def step(y, p):
            w1, b1, w2, b2, w3, b3, ge = p
            h = jax.nn.silu(xt @ w1 + b1) * (xt @ w2 + b2)
            return (y + ge[:, None] * (h @ w3 + b3), None)
        y, _ = jax.lax.scan(step, jnp.zeros_like(xt), (ew1, eb1, ew2, eb2, ew3, eb3, gate.T))
        z = jax.nn.silu(xt @ sw1 + sb1) * (xt @ sw2 + sb2) @ sw3 + sb3
        return (y + z).reshape(shape)

    def _L1_xattn_ref(hidden_states, cross_attention_states, attention_mask, q_proj_w, k_proj_w, v_proj_w, o_proj_w, q_norm_w, k_norm_w):
        import jax, jax.numpy as jnp
        import numpy as np
        NUM_HEADS = 32
        NUM_KV_HEADS = 8
        HEAD_DIM = 128
        HIDDEN = 512
        EPS = 1e-05

        def rmsnorm(x, w, eps=EPS):
            xf = x.astype(jnp.float32)
            var = jnp.mean(xf * xf, axis=-1, keepdims=True)
            return w * (xf * jax.lax.rsqrt(var + eps)).astype(x.dtype)
        B, Q, _ = hidden_states.shape
        KV = cross_attention_states.shape[1]
        n_rep = NUM_HEADS // NUM_KV_HEADS
        q = (hidden_states @ q_proj_w.T).reshape(B, Q, NUM_HEADS, HEAD_DIM).transpose(0, 2, 1, 3)
        k = (cross_attention_states @ k_proj_w.T).reshape(B, KV, NUM_KV_HEADS, HEAD_DIM).transpose(0, 2, 1, 3)
        v = (cross_attention_states @ v_proj_w.T).reshape(B, KV, NUM_KV_HEADS, HEAD_DIM).transpose(0, 2, 1, 3)
        q = rmsnorm(q, q_norm_w)
        k = jnp.repeat(k, n_rep, axis=1)
        v = jnp.repeat(v, n_rep, axis=1)
        k = rmsnorm(k, k_norm_w)
        scale = 1.0 / np.sqrt(HEAD_DIM)
        scores = jnp.einsum('bhqd,bhkd->bhqk', q, k) * scale + attention_mask
        attn = jax.nn.softmax(scores.astype(jnp.float32), axis=-1).astype(q.dtype)
        out = jnp.einsum('bhqk,bhkd->bhqd', attn, v)
        out = out.transpose(0, 2, 1, 3).reshape(B, Q, NUM_HEADS * HEAD_DIM)
        return out @ o_proj_w.T

    def _L1_ffn_ref(x, A_w, B_w, Wq_w, keys):
        import jax, jax.numpy as jnp
        import numpy as np
        IN_F = 512
        OUT_F = 512
        RANK = 8
        NUM_EXPERTS = 64
        TOP_K = 16
        ROUTER_DIM = 16
        ALPHA = 32
        SCALING = ALPHA / TOP_K
        BOTTLENECK = NUM_EXPERTS * RANK
        q = jnp.einsum('bsd,rd->bsr', x, Wq_w)
        scores = jnp.einsum('bsr,er->bse', q, keys)
        top_vals, top_idx = jax.lax.top_k(scores, TOP_K)
        top_w = jax.nn.softmax(top_vals, axis=-1)
        gate = jnp.sum(jax.nn.one_hot(top_idx, NUM_EXPERTS, dtype=top_w.dtype) * top_w[..., None], axis=-2)
        z = jnp.einsum('bsd,nd->bsn', x, A_w)
        z = z.reshape(*z.shape[:-1], NUM_EXPERTS, RANK)
        z_gated = (z * gate[..., None]).reshape(*z.shape[:-2], BOTTLENECK)
        out = jnp.einsum('bsn,on->bso', z_gated, B_w) * SCALING
        return out
    x = x + _L0_xattn_ref(_layernorm(x, axis=-1), ctx_4096, L0_xattn_x1_scale, L0_xattn_x1_zp, L0_xattn_x2_scale, L0_xattn_x2_zp)
    x = x + _L0_ffn_ref(_layernorm(x, axis=-1), L0_ffn_router_w, L0_ffn_router_b, L0_ffn_router_bias, L0_ffn_ew1, L0_ffn_eb1, L0_ffn_ew2, L0_ffn_eb2, L0_ffn_ew3, L0_ffn_eb3, L0_ffn_sw1, L0_ffn_sb1, L0_ffn_sw2, L0_ffn_sb2, L0_ffn_sw3, L0_ffn_sb3)
    x = x + _L1_xattn_ref(_layernorm(x, axis=-1), ctx_4096, mask_1x1xSxS2_ff0, L1_xattn_q_proj_w, L1_xattn_k_proj_w, L1_xattn_v_proj_w, L1_xattn_o_proj_w, L1_xattn_q_norm_w, L1_xattn_k_norm_w)
    x = x + _L1_ffn_ref(_layernorm(x, axis=-1), L1_ffn_A_w, L1_ffn_B_w, L1_ffn_Wq_w, L1_ffn_keys)
    return x

_drawn_inputs = setup_inputs


def setup_inputs(seed=0):
    import zlib

    import numpy as np

    out = dict(_drawn_inputs(seed))
    spreads = {'L1_xattn_q_norm_w': (1.0, 0.6), 'L1_xattn_k_norm_w': (1.0, 0.6)}
    factors = {'L0_ffn_router_w': 39.626,
     'L0_ffn_router_b': 200.0,
     'L0_ffn_router_bias': 8.0,
     'L0_ffn_ew1': 8.0,
     'L0_ffn_eb1': 8.0,
     'L0_ffn_ew2': 8.0,
     'L0_ffn_eb2': 8.0,
     'L0_ffn_ew3': 8.0,
     'L0_ffn_eb3': 47.249,
     'L0_ffn_sw1': 8.0,
     'L0_ffn_sb1': 64.0,
     'L0_ffn_sw2': 8.0,
     'L0_ffn_sb2': 64.0,
     'L0_ffn_sw3': 8.0,
     'L0_ffn_sb3': 200.0,
     'L1_ffn_A_w': 51.863,
     'L1_ffn_B_w': 52.324,
     'L1_ffn_Wq_w': 56.915,
     'L1_ffn_keys': 57.274,
     'L1_xattn_q_proj_w': 8.0,
     'L1_xattn_k_proj_w': 8.0,
     'L1_xattn_v_proj_w': 8.0,
     'L1_xattn_o_proj_w': 8.0}
    for name, (base, spread) in spreads.items():
        noise = np.random.default_rng([zlib.crc32(name.encode()), seed]).standard_normal(out[name].shape)
        drawn = base * np.exp(spread * noise) if base else spread * noise
        out[name] = jnp.asarray(drawn.astype(out[name].dtype))
    for name, factor in factors.items():
        out[name] = (out[name] * factor).astype(out[name].dtype)
    return out
```

```python
from contextlib import ExitStack

import concourse.bass as bass
from concourse import mybir

P = 128
D = 512
KC = D // P
BATCH, SEQ, CTX = 2, 256, 512
TOK = BATCH * SEQ
NT = TOK // P
QT_PER_B = SEQ // P
SC = CTX // P
NST = BATCH * SC
HEADS, KVH, HD = 32, 8, 128
REP = HEADS // KVH
E_ROUTED, GROUPS, TOPG, TOPE = 16, 4, 2, 2
EPG = E_ROUTED // GROUPS
NE = 18
INTER = 128
L_EXP, RANK, RD = 64, 8, 16
GW = 512
WG = KC * GW
EG = 2 * KC * INTER + D

N_CTX, N_V0, N_K, N_V1, N_E, N_Q = 0, 2, 3, 5, 6, 6 + NE
N_O = N_Q + KVH
N_A = N_O + KVH
N_B = N_A + 1

ROUND = 12582912.0
MID = 128.0
QMAX = 255.0
EPS = 1e-5
RSQRT_MAGIC = float(0x5F3759DF)
BIG = 3.0e38
PSCALE = 16384.0
L_SCALING = 32.0 / 16.0

ALU = mybir.AluOpType
ACT = mybir.ActivationFunctionType
F16 = mybir.dt.float16
F32 = mybir.dt.float32
I32 = mybir.dt.int32
AX_X = mybir.AxisListType.X


def xattn_ffn_kernel(nc, x_rows, ctx_nat, ctx_t, mask, scal, wkv, moe, moe_b, moe_b3,
                     router_w, router_b, router_bias, wq, wo, qk_norm, a_w, b_w, l_wq, l_keys, out):
    gates_dram = nc.dram_tensor("gates_dram", (NE, TOK), F32, kind="Internal").ap()
    with ExitStack() as ctx:
        def sb(name, shape, dt):
            return ctx.enter_context(nc.sbuf_tensor(name, shape, dt))

        def sem(name):
            return ctx.enter_context(nc.semaphore(name))

        k_sb = sb("k_sb", [P, KVH, 2, BATCH * CTX], F16)
        v_sb = sb("v_sb", [P, NST, 2, KVH * HD], F16)
        q_sb = sb("q_sb", [P, KVH * NT, 2, REP * P], F16)
        x_sb = sb("x_sb", [P, NT, D], F32)
        xT = sb("xT", [P, NT, 2, D], F16)
        nmask = sb("nmask", [P, QT_PER_B, CTX], F32)
        stage = sb("stage", [P, 2, WG], F32)
        wsp = sb("wsp", [P, 2, 2, WG], F16)
        f32r = sb("f32r", [P, 4, GW], F32)
        hlr = sb("hlr", [P, 4, 2, GW], F16)
        pT1 = sb("pT1", [P, 4, 2, GW], F16)
        ident = sb("ident", [P, P], F16)
        identf = sb("identf", [P, P], F32)
        wneg = sb("wneg", [P, P], F32)
        mb = sb("mb", [P, 2, NE], F32)
        scs = sb("scs", [P, 16], F32)
        rw = sb("rw", [P, KC, E_ROUTED], F32)
        rws = sb("rws", [P, 2, KC * E_ROUTED], F16)
        ones = sb("ones", [P, 1], F16)
        st6 = sb("st6", [P, NT, 6], F32)
        mv = sb("mv", [P, NT, 2], F32)
        nw = sb("nw", [P, 4, NT], F32)
        sml = sb("sml", [P, 8, 16], F32)

        early = q_sb[:, :, :, :].rearrange("p a b c -> p (a b c)")
        ctxs = early[:, 0:2 * KC * NST * P].rearrange("p (k l s) -> p k l s", k=KC, l=2)
        wkvs = early[:, 8192:24576].rearrange("p (w l c) -> p w l c", w=4, l=2)
        cnat = early[:, 24576:32768].bitcast(F32)
        cq = xT[:, :, :, :].rearrange("p a b c -> p (a b c)")
        xqT = pT1[:, 0:2, :, :].rearrange("p a b (k t) -> p (a b) k t", k=KC)
        ones128 = pT1[:, 2, 0, 0:P]
        pT0 = xT
        pT = [pT0, pT1]
        gate_bc = [hlr[:, 2, :, :].rearrange("p a b -> p (a b)").bitcast(F32),
                   hlr[:, 3, :, :].rearrange("p a b -> p (a b)").bitcast(F32)]
        b3s = f32r[:, 2, :]
        gateT = f32r[:, 3, :]
        lg = sml[:, 0:4, :]
        gt = ctx.enter_context(nc.sbuf_tensor("gt", [P, NT, NE], F32))
        rb = ctx.enter_context(nc.sbuf_tensor("rb", [P, 2, NT * E_ROUTED], F32))
        rstat = ctx.enter_context(nc.sbuf_tensor("rstat", [P, 4, NT], F32))
        cmp_gt = pT1[:, 0, :, :].rearrange("p a b -> p (a b)")
        cmp_eq = pT1[:, 1, :, :].rearrange("p a b -> p (a b)")
        mneg = ctx.enter_context(nc.sbuf_tensor("mneg", [P, 4], F32))
        psum_col = ctx.enter_context(nc.sbuf_tensor("psum_col", [P, 4], F32))
        rinv = ctx.enter_context(nc.sbuf_tensor("rinv", [P, 2, 4], F32))
        ss = ctx.enter_context(nc.sbuf_tensor("ss", [P, 2, REP], F32))
        root = ctx.enter_context(nc.sbuf_tensor("root", [P, 2, REP], F32))
        rrt = ctx.enter_context(nc.sbuf_tensor("rrt", [P, 2, REP], F32))
        late = k_sb[:, :, :, :].rearrange("p a b c -> p (a b c)").bitcast(F32)
        lower = pT1[:, 3, 0, 0:E_ROUTED * E_ROUTED].rearrange("p (i j) -> p i j", i=E_ROUTED)
        lwq = late[:, 0:64].rearrange("p (k r) -> p k r", k=KC)
        lky = late[0:RD, 64:128]
        lwqs = late[:, 128:192].bitcast(F16).rearrange("p (l c) -> p l c", l=2)
        lkys = late[0:RD, 192:256].bitcast(F16).rearrange("p (l c) -> p l c", l=2)
        lqs = late[0:RD, 256:768].bitcast(F16).rearrange("p (l c) -> p l c", l=2)
        lsc = late[:, 1024:1280].rearrange("p (t e) -> p t e", t=NT)
        lw1 = late[:, 1280:1536].rearrange("p (t e) -> p t e", t=NT)
        lw2 = late[:, 1536:1792].rearrange("p (t e) -> p t e", t=NT)
        lex = late[:, 1792:2048].rearrange("p (t e) -> p t e", t=NT)
        lm8 = late[:, 2048:2112].rearrange("p (t a b) -> p t a b", t=NT, a=2)
        lng = late[:, 2112:2120]
        lsum = late[:, 2120:2128]
        zT = late[:, 4096:6144].bitcast(F16).rearrange("p (t l c) -> p t l c", t=NT, l=2)

        ps = [ctx.enter_context(nc.psum_tensor(f"ps{i}", [P, 512], F32)) for i in range(8)]

        s_x = sem("s_x")
        s_cn = sem("s_cn")
        s_par = sem("s_par")
        s_late = sem("s_late")
        s_mask = sem("s_mask")
        s_w = [sem("s_w0"), sem("s_w1")]
        s_whi = sem("s_whi")
        s_wlo = sem("s_wlo")
        s_w12h = sem("s_w12h")
        s_w12l = sem("s_w12l")
        s_w3h = sem("s_w3h")
        s_w3l = sem("s_w3l")
        s_wqh = sem("s_wqh")
        s_wql = sem("s_wql")
        s_gload = [sem("s_gload0"), sem("s_gload1")]
        s_b3 = sem("s_b3")
        s_gst = sem("s_gst")
        s_id = sem("s_id")
        s_dve = sem("s_dve")
        s_xq = sem("s_xq")
        s_xqT = sem("s_xqT")
        s_xqTc = sem("s_xqTc")
        s_cq = sem("s_cq")
        s_sums = sem("s_sums")
        s_sumsc = sem("s_sumsc")
        s_main = sem("s_main")
        s_ln = sem("s_ln")
        s_lnh = sem("s_lnh")
        s_lnl = sem("s_lnl")
        s_lnT = sem("s_lnT")
        s_lnTc = sem("s_lnTc")
        s_rwh = sem("s_rwh")
        s_rws = sem("s_rws")
        s_rt = sem("s_rt")
        s_lg = sem("s_lg")
        s_rex = sem("s_rex")
        s_gate = sem("s_gate")
        s_gT = sem("s_gT")
        s_gTc = sem("s_gTc")
        s_vp = sem("s_vp")
        s_vh = sem("s_vh")
        s_vfree = sem("s_vfree")
        s_pj = sem("s_pj")
        s_sq = sem("s_sq")
        s_ss = sem("s_ss")
        s_root = sem("s_root")
        s_rr = sem("s_rr")
        s_nrm = sem("s_nrm")
        s_nh = sem("s_nh")
        s_nl = sem("s_nl")
        s_tr = sem("s_tr")
        s_trc = sem("s_trc")
        s_up = sem("s_up")
        s_silu = sem("s_silu")
        s_hx = sem("s_hx")
        s_hg = sem("s_hg")
        s_hh = sem("s_hh")
        s_hl = sem("s_hl")
        s_dn = sem("s_dn")
        s_s = sem("s_s")
        s_t = sem("s_t")
        s_e = sem("s_e")
        s_r0 = sem("s_r0")
        s_r = sem("s_r")
        s_ph = sem("s_ph")
        s_pl = sem("s_pl")
        s_T = sem("s_T")
        s_Tc = sem("s_Tc")
        s_pv = sem("s_pv")
        s_oh = sem("s_oh")
        s_ol = sem("s_ol")
        s_od = sem("s_od")
        s_lw = sem("s_lw")
        s_lwl = sem("s_lwl")
        s_lq = sem("s_lq")
        s_lqh = sem("s_lqh")
        s_lqs = sem("s_lqs")
        s_lsc = sem("s_lsc")
        s_lng = sem("s_lng")
        s_lex = sem("s_lex")
        s_z = sem("s_z")
        s_zg = sem("s_zg")
        s_zh = sem("s_zh")
        s_zl = sem("s_zl")
        s_zT = sem("s_zT")
        s_zTc = sem("s_zTc")
        s_y = sem("s_y")
        s_fin = sem("s_fin")
        s_out = sem("s_out")

        def words(ap):
            return ap.bitcast(F32)

        def three_products(pe, dst, lhs, rhs, start, stop):
            pe.matmul(dst, lhs[0], rhs[1], start=start, stop=False, skip_group_check=True)
            pe.matmul(dst, lhs[1], rhs[0], start=False, stop=False, skip_group_check=True)
            return pe.matmul(dst, lhs[0], rhs[0], start=False, stop=stop, skip_group_check=True)

        block = ctx.enter_context(nc.Block())

        @block.sync
        def _(sp):
            def load(slot, src, width):
                sp.dma_start(stage[:, slot, 0:width], src).then_inc(s_w[slot], 16)

            sp.dma_start(x_sb[:, :, :], x_rows.rearrange("(t p) d -> p t d", p=P)).then_inc(s_x, 16)
            sp.dma_start(cnat, ctx_nat).then_inc(s_cn, 16)
            for n in range(2):
                load(n, ctx_t[:, n, :], WG)
            for w in range(4):
                sp.wait_ge(s_wlo, w + 1)
                load((N_V0 + w) % 2, wkv[w], WG)
            for s in range(2):
                sp.wait_ge(s_wlo, N_E - 1 + s)
                load(s, moe[s], EG)
            with sp.Fori(1, NE // 2) as i:
                for s in range(2):
                    sp.wait_ge(s_w3l, 2 * i + s - 1)
                    load(s, moe[2 * i + s], EG)
            for s in range(2):
                sp.wait_ge(s_w3l, NE - 1 + s)
                load(s, wq[s], WG)
            with sp.Fori(1, KVH // 2) as i:
                for s in range(2):
                    sp.wait_ge(s_wql, 4 * (2 * i + s - 1))
                    load(s, wq[2 * i + s], WG)
            with sp.Fori(0, KVH // 2) as i:
                for s in range(2):
                    sp.wait_ge(s_wql, 4 * (KVH + 2 * i + s - 1))
                    load(s, wo[2 * i + s], WG)
            for s, src in enumerate((a_w, b_w)):
                sp.wait_ge(s_wql, 4 * (2 * KVH + s - 1))
                load(s, src, WG)
            for t in range(NT):
                sp.wait_ge(s_fin, t + 1)
                sp.dma_start(out[t * P:(t + 1) * P, :], x_sb[:, t, :]).then_inc(s_out, 16)
            sp.wait_ge(s_out, 16 * NT)

        @block.tensor
        def _(pe):
            def transposes(src_hi_lo, dst, place):
                for l in range(2):
                    for c in range(4):
                        at = place(l, c) * P
                        last = pe.transpose(dst.bitcast(F16)[:, at:at + P], src_hi_lo[:, l, c * P:(c + 1) * P], ident[:, :])
                return last

            def hi_lo_major(l, c):
                return 4 * l + c

            def block_major(l, c):
                return 2 * c + l

            def ln_transposes(n):
                for t in range(NT):
                    pe.wait_ge(s_lnl, NT * n + t + 1)
                    transposes(hlr[:, t, :, :], ps[t][:, :], hi_lo_major).then_inc(s_lnT, 1)

            def v_half(w, hg):
                pe.wait_ge(s_wlo, (3, 6)[hg])
                with pe.Fori(0, NST // 4) as i:
                    for j in range(4):
                        pe.wait_ge(s_vfree, NST * hg + 4 * i + j + 1)
                        for c in range(KC):
                            last = three_products(
                                pe, ps[4 + j][:, :],
                                [ctxs[:, c, l, bass.ds(i * (4 * P) + j * P, P)] for l in range(2)],
                                [wkvs[:, w, l, c * GW:(c + 1) * GW] for l in range(2)], c == 0, c == KC - 1)
                        last.then_inc(s_vp, 1)

            def rms_phase(r0, iters, tiles, project, place):
                def transposed(r, j):
                    pe.wait_ge(s_nl, r + 1)
                    pe.wait_ge(s_trc, r + 1)
                    transposes(hlr[:, j % 4, :, :], ps[6 + j % 2][:, :], place).then_inc(s_tr, 1)

                def body(i, first):
                    for j in range(tiles):
                        r = r0 + tiles * i + j
                        if not first or j >= 4:
                            pe.wait_ge(s_nrm, r - 3)
                        project(i, j).then_inc(s_pj, 1)
                        if not first or j >= 4:
                            transposed(r - 4, j)

                body(0, True)
                with pe.Fori(1, iters) as i:
                    body(i, False)
                for j in range(4):
                    transposed(r0 + tiles * iters - 4 + j, j)

            def k_project(i, j):
                for c in range(KC):
                    last = three_products(
                        pe, ps[j % 4][:, :],
                        [ctxs[:, c, l, bass.ds(i * (2 * P) + (j // 2) * P, P)] for l in range(2)],
                        [wkvs[:, 1 + j % 2, l, c * GW:(c + 1) * GW] for l in range(2)], c == 0, c == KC - 1)
                return last

            def q_project(i, j):
                s, t = divmod(j, NT)
                if t == 0:
                    pe.wait_ge(s_wql, 4 * (2 * i + s + 1))
                for c in range(KC):
                    last = three_products(
                        pe, ps[j % 4][:, :],
                        [xT[:, t, l, c * P:(c + 1) * P] for l in range(2)],
                        [wsp[:, s, l, c * GW:(c + 1) * GW] for l in range(2)], c == 0, c == KC - 1)
                return last

            pe.wait_ge(s_id, 4)
            for t in range(NT):
                pe.wait_ge(s_xq, t + 1)
                for c in range(KC):
                    last = pe.transpose(ps[4 + t // 2][:, :].bitcast(F16)[:, (t % 2) * D + c * P:(t % 2) * D + (c + 1) * P],
                                        hlr[:, t, 0, c * P:(c + 1) * P], ident[:, :])
                last.then_inc(s_xqT, 1)
            pe.wait_ge(s_cq, 2)
            for b in range(BATCH):
                for c in range(KC):
                    last = pe.matmul(ps[6 + b][:, :], ones128, cq[:, (b * KC + c) * D:(b * KC + c + 1) * D],
                                     start=(c == 0), stop=(c == KC - 1))
                last.then_inc(s_sums, 1)
            pe.wait_ge(s_xqTc, 2)
            for t in range(NT):
                for c in range(KC):
                    last = pe.matmul(ps[4][:, t:t + 1], xqT[:, t, c, :], ones[:, :], start=(c == 0), stop=(c == KC - 1))
            last.then_inc(s_sums, 1)
            for t in range(NT):
                for c in range(KC):
                    last = pe.matmul(ps[t][:, :], xqT[:, t, c, :],
                                     cq[:, ((t // 2) * KC + c) * D:((t // 2) * KC + c + 1) * D],
                                     start=(c == 0), stop=(c == KC - 1))
                last.then_inc(s_main, 1)

            v_half(0, 0)
            ln_transposes(0)

            pe.wait_ge(s_lnTc, NT)
            pe.wait_ge(s_rws, 1)
            pe.wait_ge(s_vfree, 4 + NST)
            for t in range(NT):
                for c in range(KC):
                    last = three_products(
                        pe, ps[4][:, t * E_ROUTED:(t + 1) * E_ROUTED],
                        [xT[:, t, l, c * P:(c + 1) * P] for l in range(2)],
                        [rws[:, l, c * E_ROUTED:(c + 1) * E_ROUTED] for l in range(2)], c == 0, c == KC - 1)
                if t == 0:
                    last.then_inc(s_tr, 4)
                if t == 1:
                    last.then_inc(s_trc, 2)
            last.then_inc(s_rt, 1)

            pe.wait_ge(s_wlo, 5)
            rms_phase(0, 4, 4, k_project, block_major)

            def up(e, s):
                pe.wait_ge(s_w12l, e + 1)
                for u in range(2):
                    for c in range(KC):
                        at = (u * KC + c) * INTER
                        last = three_products(
                            pe, ps[4 + 2 * s + u][:, :],
                            [wsp[:, s, l, at:at + INTER] for l in range(2)],
                            [xT[:, :, l, c * P:(c + 1) * P] for l in range(2)], c == 0, c == KC - 1)
                    last.then_inc(s_up, 1)

            def down(e, s, last_expert=False):
                pe.wait_ge(s_w3l, e + 1)
                pe.wait_ge(s_hl, e + 1)
                for t in range(NT):
                    last = three_products(
                        pe, ps[t][:, :], [hlr[:, s, l, t * P:(t + 1) * P] for l in range(2)],
                        [wsp[:, s, l, 2 * KC * INTER:EG] for l in range(2)], False, last_expert)
                last.then_inc(s_dn, 1)

            pe.wait_ge(s_lg, 1)
            up(0, 0)
            pe.wait_ge(s_gate, 1)
            pe.wait_ge(s_trc, 2 + 16)
            for t in range(NT):
                last = pe.transpose(ps[7][0:NE, t * P:(t + 1) * P], gt[:, t, :], identf[:, :])
            last.then_inc(s_gT, 1)
            pe.wait_ge(s_gTc, 1)
            pe.wait_ge(s_b3, 16)
            for t in range(NT):
                pe.matmul(ps[t][:, :], gateT[0:E_ROUTED + 1, t * P:(t + 1) * P], b3s[0:E_ROUTED + 1, :],
                          start=True, stop=False, skip_group_check=True)
            up(1, 1)
            down(0, 0)
            pe.wait_ge(s_hx, 1)
            up(2, 0)
            down(1, 1)
            with pe.Fori(1, NE // 2 - 1) as i:
                pe.wait_ge(s_hx, 2 * i)
                up(2 * i + 1, 1)
                down(2 * i, 0)
                pe.wait_ge(s_hx, 2 * i + 1)
                up(2 * i + 2, 0)
                down(2 * i + 1, 1)
            pe.wait_ge(s_hx, NE - 2)
            up(NE - 1, 1)
            down(NE - 2, 0)
            down(NE - 1, 1, True)

            pe.wait_ge(s_hx, NE)
            v_half(3, 1)
            ln_transposes(1)

            pe.wait_ge(s_lnTc, 2 * NT)
            pe.wait_ge(s_vfree, 4 + 2 * NST)
            rms_phase(16, 4, 2 * NT, q_project, hi_lo_major)

            def scores(g, j, k, first):
                m, hh = divmod(j, REP)
                if not first or j >= 4:
                    pe.wait_ge(s_t, k - 3)
                b = m // QT_PER_B
                three_products(
                    pe, ps[j % 4][:, :],
                    [q_sb[:, bass.ds(4 * g + m, 1), l, hh * P:(hh + 1) * P] for l in range(2)],
                    [k_sb[:, bass.ds(g, 1), l, b * CTX:(b + 1) * CTX] for l in range(2)], True, True).then_inc(s_s, 1)

            def prob_transposes(j, k, wait_bank=True):
                pe.wait_ge(s_pl, k + 1)
                if wait_bank:
                    pe.wait_ge(s_Tc, k - 1)
                transposes(hlr[:, j % 4, :, :], ps[4 + j % 2][:, :], hi_lo_major).then_inc(s_T, 1)

            def values(w, gw, mw, c, wait_bank=True):
                if c == 0:
                    pe.wait_ge(s_Tc, 4 * w + 4)
                    if wait_bank:
                        pe.wait_ge(s_ol, w - 1)
                par = mw % 2
                last = three_products(
                    pe, ps[6 + par][:, :],
                    [v_sb[:, (mw // QT_PER_B) * SC + c, l, bass.ds(gw * HD, HD)] for l in range(2)],
                    [pT[par][:, :, l, c * P:(c + 1) * P] for l in range(2)], c == 0, c == SC - 1)
                if c == SC - 1:
                    last.then_inc(s_pv, 1)

            def attention(g, first):
                for j in range(4 * REP):
                    k = 16 * g + j
                    m, c = divmod(j, REP)
                    scores(g, j, k, first)
                    if not first or j >= 4:
                        prob_transposes(j, k - 4, not first or j >= 6)
                    if not first or m >= 2:
                        values(4 * g + m - 2, g if m >= 2 else g - 1, (m - 2) % 4, c, not first)

            attention(0, True)
            with pe.Fori(1, KVH) as g:
                attention(g, False)
            for j in range(4):
                prob_transposes(j, 16 * KVH - 4 + j)
                values(4 * KVH - 2, KVH - 1, 2, j)
            for c in range(SC):
                values(4 * KVH - 1, KVH - 1, 3, c)

            def o_group(g, s, first, last_group):
                pe.wait_ge(s_wql, 4 * (KVH + 1) + 4 * g)
                for c in range(REP):
                    for t in range(NT):
                        last = three_products(
                            pe, ps[t][:, :],
                            [q_sb[:, bass.ds(4 * g + t, 1), l, c * P:(c + 1) * P] for l in range(2)],
                            [wsp[:, s, l, c * GW:(c + 1) * GW] for l in range(2)],
                            first and c == 0, last_group and c == REP - 1)
                last.then_inc(s_od, 1)

            pe.wait_ge(s_ol, 4 * KVH)
            for s in range(2):
                o_group(s, s, s == 0, False)
            with pe.Fori(1, KVH // 2 - 1) as i:
                for s in range(2):
                    o_group(2 * i + s, s, False, False)
            for s in range(2):
                o_group(KVH - 2 + s, s, False, s == 1)
            ln_transposes(2)

            pe.wait_ge(s_lnTc, 3 * NT)
            pe.wait_ge(s_lwl, 1)
            for c in range(KC):
                last = three_products(
                    pe, ps[4][0:RD, :], [lwqs[:, l, c * RD:(c + 1) * RD] for l in range(2)],
                    [xT[:, :, l, c * P:(c + 1) * P] for l in range(2)], c == 0, c == KC - 1)
            last.then_inc(s_lq, 1)
            pe.wait_ge(s_wql, 4 * (2 * KVH + 1))
            for t in range(NT):
                for c in range(KC):
                    last = three_products(
                        pe, ps[t][:, :], [xT[:, t, l, c * P:(c + 1) * P] for l in range(2)],
                        [wsp[:, 0, l, c * GW:(c + 1) * GW] for l in range(2)], c == 0, c == KC - 1)
                last.then_inc(s_z, 1)
                if t == 0:
                    pe.wait_ge(s_lqs, 1)
                    for u in range(NT):
                        last = three_products(
                            pe, ps[5][:, u * L_EXP:(u + 1) * L_EXP],
                            [lqs[:, l, u * P:(u + 1) * P] for l in range(2)],
                            [lkys[:, l, :] for l in range(2)], True, True)
                    last.then_inc(s_lsc, 1)
            for t in range(NT):
                pe.wait_ge(s_zl, t + 1)
                if t >= 2:
                    pe.wait_ge(s_zTc, t - 1)
                transposes(hlr[:, t, :, :], ps[6 + t % 2][:, :], hi_lo_major).then_inc(s_zT, 1)
            pe.wait_ge(s_wql, 4 * (2 * KVH + 2))
            for t in range(NT):
                pe.wait_ge(s_zTc, t + 1)
                for c in range(KC):
                    last = three_products(
                        pe, ps[t][:, :], [zT[:, t, l, c * P:(c + 1) * P] for l in range(2)],
                        [wsp[:, 1, l, c * GW:(c + 1) * GW] for l in range(2)], c == 0, c == KC - 1)
                last.then_inc(s_y, 1)

        @block.scalar
        def _(act):
            for dst, src in ((scs[:, 0:4], scal), (mb[:, :, :], moe_b), (rw[:, :, :], router_w), (rb[:, 0, :], router_b),
                             (rb[:, 1, :], router_bias), (wneg[:, :], qk_norm[:, 0, :]), (identf[:, :], qk_norm[:, 1, :])):
                act.dma_start(dst, src).then_inc(s_par, 16)
            act.dma_start(nmask[:, :, :], mask.rearrange("(h p) c -> p h c", p=P)).then_inc(s_mask, 16)

            def group_hi(dst, slot, load, n):
                act.wait_ge(s_w[slot], 16 * load)
                act.copy(dst, stage[:, slot, :]).then_inc(s_whi, 1)

            for n in range(2):
                act.wait_ge(s_w[n], 16)
                act.copy(ctxs[:, 2 * n:2 * n + 2, 0, :], stage[:, n, :].rearrange("p (k s) -> p k s", k=2)).then_inc(s_whi, 1)
            for w in range(2):
                group_hi(wkvs[:, w, 0, :], w, 2, w)
            act.wait_ge(s_par, 16 * 7)
            act.copy(rws[:, 0, :], rw[:, :, :].rearrange("p k e -> p (k e)")).then_inc(s_rwh, 1)

            def ln_hi(n):
                for t in range(NT):
                    act.wait_ge(s_ln, NT * n + t + 1)
                    act.copy(hlr[:, t, 0, :], f32r[:, t, :]).then_inc(s_lnh, 1)

            def v_hi(hg):
                with act.Fori(0, NST // 4) as i:
                    for j in range(4):
                        act.wait_ge(s_vp, NST * hg + 4 * i + j + 1)
                        act.copy(v_sb[:, bass.ds(4 * i + j, 1), 0, hg * GW:(hg + 1) * GW], ps[4 + j][:, :]).then_inc(s_vh, 1)

            ln_hi(0)
            group_hi(wkvs[:, 2, 0, :], 0, 3, 2)
            v_hi(0)
            group_hi(wkvs[:, 3, 0, :], 1, 3, 3)

            act.wait_ge(s_lg, 2)
            act.activation(sml[:, 4:8, :], sml[:, 0:4, :], ACT.Exp).then_inc(s_rex, 1)

            def rms_phase(r0, iters, tiles, scale, bias, copy_out, quarter):
                def squares(r, j, first):
                    act.wait_ge(s_pj, r + 1)
                    if not first or j >= 2:
                        act.wait_ge(s_ss, r - 1)
                    act.activation(f32r[:, j % 2, :], ps[j % 4][:, :], ACT.Square).then_inc(s_sq, 1)

                def roots(r, j, first):
                    act.wait_ge(s_ss, r + 1)
                    if not first or j >= 2:
                        act.wait_ge(s_rr, r - 1)
                    act.activation(root[:, j % 2, :], ss[:, j % 2, :], ACT.Sqrt, bias=bias, scale=scale).then_inc(s_root, 1)

                def hi(r, j, first):
                    act.wait_ge(s_nrm, r + 1)
                    act.wait_ge(s_tr, r + 1)
                    act.copy(hlr[:, j % 4, 0, :], f32r[:, 2 + j % 2, :]).then_inc(s_nh, 1)

                def copied(i, j, r):
                    act.wait_ge(s_tr, r + 5)
                    copy_out(i, j, ps[6 + j % 2][:, :]).then_inc(s_trc, 1)

                def body(i, first):
                    for j in range(tiles):
                        r = r0 + tiles * i + j
                        squares(r, j, first)
                        if not first or j >= 1:
                            roots(r - 1, (j - 1) % tiles, first and j - 1 < 2)
                        if not first or j >= 2:
                            hi(r - 2, (j - 2) % tiles, first and j - 2 < 4)
                        quarter(i, j)
                        if not first or j >= 4:
                            copied(i if j >= 4 else i - 1, (j - 4) % tiles, r - 4)

                body(0, True)
                with act.Fori(1, iters) as i:
                    body(i, False)
                end = tiles * iters
                roots(r0 + end - 1, tiles - 1, False)
                for j in range(2):
                    hi(r0 + end - 2 + j, tiles - 2 + j, False)
                for j in range(4):
                    copied(iters - 1, tiles - 4 + j, r0 + end - 4 + j)

            k_words = words(k_sb[:, :, :, :])

            def k_out(i, j, bank):
                h0 = (j % 2) * 4
                return act.copy(k_words[:, h0:h0 + 4, :, bass.ds(i * P + (j // 2) * (P // 2), P // 2)],
                                bank.rearrange("p (h l w) -> p h l w", h=4, l=2))

            def q_out(i, j, bank):
                return act.copy(words(q_sb[:, bass.ds(2 * NT * i + j, 1), :, :]), bank)

            rms_phase(0, 4, 4, 1.0 / HD, scs[:, 12:13], k_out, lambda i, j: None)

            def w12_hi(e, s):
                act.wait_ge(s_w[s], 16 * ((N_E + e - s) // 2 + 1) if isinstance(e, int) else 16 * (N_E // 2 + 1) + 8 * (e - s))
                if not (isinstance(e, int) and e < 2):
                    act.wait_ge(s_up, 2 * e - 2)
                act.copy(wsp[:, s, 0, 0:2 * KC * INTER], stage[:, s, 0:2 * KC * INTER]).then_inc(s_w12h, 1)

            def w3_hi(e, s):
                if not (isinstance(e, int) and e < 2):
                    act.wait_ge(s_dn, e - 1)
                act.copy(wsp[:, s, 0, 2 * KC * INTER:EG], stage[:, s, 2 * KC * INTER:EG]).then_inc(s_w3h, 1)

            def gate_load(e, s):
                act.dma_start(gate_bc[s], gates_dram[bass.ds(e, 1), :].partition_broadcast(P)
                              .rearrange("q a t -> q (a t)")).then_inc(s_gload[s], 16)

            def silu(e, s):
                act.wait_ge(s_up, 2 * e + 1)
                if not (isinstance(e, int) and e < 2):
                    act.wait_ge(s_hl, e - 1)
                act.activation(f32r[:, s, :], ps[4 + 2 * s][:, :], ACT.Silu, bias=mb[:, 0, bass.ds(e, 1)]).then_inc(s_silu, 1)

            def hidden_hi(e, s):
                act.wait_ge(s_hg, e + 1)
                if not (isinstance(e, int) and e < 2):
                    act.wait_ge(s_dn, e - 1)
                act.copy(hlr[:, s, 0, :], f32r[:, s, :]).then_inc(s_hh, 1)

            def expert(e, s):
                silu(e, s)
                if not (isinstance(e, int) and e + 2 >= NE):
                    w12_hi(e + 2, s)
                hidden_hi(e, s)
                if not (isinstance(e, int) and e + 2 >= NE):
                    gate_load(e + 2, s)
                if not (isinstance(e, int) and e + 1 >= NE):
                    w3_hi(e + 1, 1 - s)

            w12_hi(0, 0)
            w3_hi(0, 0)
            w12_hi(1, 1)
            act.dma_start(b3s[0:E_ROUTED + 1, :], moe_b3).then_inc(s_b3, 16)
            act.wait_ge(s_gTc, 1)
            act.dma_start(gates_dram, gateT[0:NE, :]).then_inc(s_gst, 16)
            act.wait_ge(s_gst, 16)
            for s in range(2):
                gate_load(s, s)
            for s in range(2):
                expert(s, s)
            with act.Fori(1, NE // 2 - 1) as i:
                for s in range(2):
                    expert(2 * i + s, s)
            for s in range(2):
                expert(NE - 2 + s, s)

            def quarter_hi(slot, c, free=None):
                if free is not None:
                    act.wait_ge(*free)
                act.copy(wsp[:, slot, 0, c * GW:(c + 1) * GW], stage[:, slot, c * GW:(c + 1) * GW]).then_inc(s_wqh, 1)

            Q_LOADS = N_Q // 2
            act.wait_ge(s_w[0], 16 * (Q_LOADS + 1))
            for c in range(4):
                quarter_hi(0, c, (s_dn, NE - 1) if c == 0 else None)
            ln_hi(1)
            v_hi(1)
            act.wait_ge(s_lnT, 2 * NT)

            def q_quarter(i, j):
                s, c = divmod(j, 4)
                if c == 0:
                    act.wait_ge(s_w[1 - s], 16 * (Q_LOADS + 1 + s) + 16 * i)
                    act.wait_ge(s_pj, 16 + 8 * i + 4 * s)
                quarter_hi(1 - s, c)

            rms_phase(16, 4, 2 * NT, 1.0 / 64, scs[:, 13:14], q_out, q_quarter)

            def exponentials(j, k):
                act.wait_ge(s_t, k + 1)
                act.activation(f32r[:, j % 4, :], f32r[:, j % 4, :], ACT.Exp, bias=mneg[:, j % 4:j % 4 + 1], scale=-1.0,
                               accum_out=psum_col[:, j % 4:j % 4 + 1]).then_inc(s_e, 1)

            def prob_copy(j, k, u, wait_values):
                act.wait_ge(s_T, k + 1)
                if wait_values:
                    act.wait_ge(s_pv, u - 1)
                act.copy(words(pT[(j // REP) % 2][:, j % REP, :, :]), ps[4 + j % 2][:, :]
                         .rearrange("p (l w) -> p l w", l=2)).then_inc(s_Tc, 1)

            def o_hi(w, mw):
                act.wait_ge(s_pv, w + 1)
                act.activation(q_sb[:, bass.ds(w, 1), 0, :], ps[6 + mw % 2][:, :], ACT.Copy, scale=1.0 / PSCALE).then_inc(s_oh, 1)

            def attention(g, first):
                for j in range(4 * REP):
                    k = 16 * g + j
                    m, hh = divmod(j, REP)
                    exponentials(j, k)
                    if not first or j >= 4:
                        prob_copy((j - 4) % 16, k - 4, 4 * g + m - 1, hh == 0 and (not first or m >= 3))
                    if hh == 0 and (not first or m >= 3):
                        o_hi(4 * g + m - 3, (m - 3) % 4)

            attention(0, True)
            with act.Fori(1, KVH) as g:
                attention(g, False)
            o_hi(4 * KVH - 3, 1)
            for j in range(4):
                prob_copy(12 + j, 16 * KVH - 4 + j, 4 * KVH - 1, j == 0)
            for m in range(2):
                o_hi(4 * KVH - 2 + m, m)

            for c in range(4):
                act.wait_ge(s_w[1], 16 * (Q_LOADS + KVH // 2 + 1))
                quarter_hi(1, c)
            with act.Fori(0, KVH // 2 - 1) as i:
                for s in range(2):
                    act.wait_ge(s_w[s], 16 * (Q_LOADS + KVH // 2 + 2) + 16 * i)
                    act.wait_ge(s_od, 2 * i + s + 1)
                    for c in range(4):
                        quarter_hi(s, c)
            for s in range(2):
                act.wait_ge(s_w[s], 16 * (Q_LOADS + KVH + 1))
                act.wait_ge(s_od, KVH - 1 + s)
                for c in range(4):
                    quarter_hi(s, c)
            for dst, src in ((lwq, l_wq), (lky, l_keys)):
                act.dma_start(dst, src).then_inc(s_late, 16)
            act.wait_ge(s_late, 32)
            act.copy(lwqs[:, 0, :], lwq.rearrange("p k r -> p (k r)")).then_inc(s_lw, 1)
            act.copy(lkys[:, 0, :], lky).then_inc(s_lw, 1)
            ln_hi(2)

            act.wait_ge(s_lq, 1)
            act.copy(lqs[:, 0, :], ps[4][0:RD, :]).then_inc(s_lqh, 1)
            for t in range(NT):
                act.wait_ge(s_lng, t + 1)
                act.activation(lex[:, t, :], lsc[:, t, :], ACT.Exp, bias=lng[:, t:t + 1]).then_inc(s_lex, 1)
            for t in range(NT):
                act.wait_ge(s_zg, t + 1)
                act.copy(hlr[:, t, 0, :], f32r[:, t, :]).then_inc(s_zh, 1)

        @block.gpsimd
        def _(pool):
            pool.memset(ident[:, :], 0.0).then_inc(s_id, 1)
            pool.memset(lower[:, :, :], 1.0).then_inc(s_id, 1)
            pool.wait_ge(s_id, 2)
            pool.affine_select(out=ident[:, :], in_=ident[:, :], compare_op=ALU.not_equal, fill=1.0, base=0,
                               pattern=[[-1, P]], channel_multiplier=1).then_inc(s_id, 1)
            pool.affine_select(out=lower[:, :, :], in_=lower[:, :, :], compare_op=ALU.is_gt, fill=0.0, base=0,
                               pattern=[[1, E_ROUTED], [-1, E_ROUTED]], channel_multiplier=0).then_inc(s_id, 1)

            def low(dst_lo, src, dst_hi):
                return pool.tensor_tensor(dst_lo, src, dst_hi, ALU.subtract)

            for n in range(2):
                pool.wait_ge(s_whi, n + 1)
                low(ctxs[:, 2 * n:2 * n + 2, 1, :], stage[:, n, :].rearrange("p (k s) -> p k s", k=2),
                    ctxs[:, 2 * n:2 * n + 2, 0, :]).then_inc(s_wlo, 1)
            for w in range(4):
                pool.wait_ge(s_whi, 3 + w)
                low(wkvs[:, w, 1, :], stage[:, w % 2, :], wkvs[:, w, 0, :]).then_inc(s_wlo, 1)

            def rms_phase(r0, iters, tiles, quarter):
                def tile_low(r, j):
                    pool.wait_ge(s_nh, r + 1)
                    low(hlr[:, j % 4, 1, :], f32r[:, 2 + j % 2, :], hlr[:, j % 4, 0, :]).then_inc(s_nl, 1)

                def body(i, first):
                    for j in range(tiles):
                        if not first or j >= 2:
                            tile_low(r0 + tiles * i + j - 2, (j - 2) % tiles)
                        quarter(i, j)

                body(0, True)
                with pool.Fori(1, iters) as i:
                    body(i, False)
                for j in range(2):
                    tile_low(r0 + tiles * iters - 2 + j, tiles - 2 + j)

            rms_phase(0, 4, 4, lambda i, j: None)

            W12, W3 = slice(0, 2 * KC * INTER), slice(2 * KC * INTER, EG)

            def w12_lo(e, s):
                pool.wait_ge(s_w12h, e + 1)
                low(wsp[:, s, 1, W12], stage[:, s, W12], wsp[:, s, 0, W12]).then_inc(s_w12l, 1)

            def w3_lo(e, s):
                pool.wait_ge(s_w3h, e + 1)
                low(wsp[:, s, 1, W3], stage[:, s, W3], wsp[:, s, 0, W3]).then_inc(s_w3l, 1)

            w12_lo(0, 0)
            w3_lo(0, 0)
            w12_lo(1, 1)
            with pool.Fori(0, NE // 2 - 1) as i:
                for s in range(2):
                    w12_lo(2 * i + s + 2, s)
                    w3_lo(2 * i + s + 1, 1 - s)
            w3_lo(NE - 1, 1)

            def quarter_lo(slot, c, q):
                pool.wait_ge(s_wqh, q + 1)
                at = slice(c * GW, (c + 1) * GW)
                low(wsp[:, slot, 1, at], stage[:, slot, at], wsp[:, slot, 0, at]).then_inc(s_wql, 1)

            for c in range(4):
                quarter_lo(0, c, c)
            rms_phase(16, 4, 2 * NT, lambda i, j: quarter_lo(1 - j // 4, j % 4, 8 * i + 4 + j))

            def prob_hi(j, k, first):
                summed, freed = k + 1, k - 3
                if not first:
                    summed, freed = pool.to_reg(summed), pool.to_reg(freed)
                pool.wait_ge(s_nl, 16 + NT * KVH)
                pool.wait_ge(s_r, summed)
                if not first:
                    pool.wait_ge(s_T, freed)
                pool.tensor_scalar(hlr[:, j % 4, 0, :], f32r[:, j % 4, :], rinv[:, 1, j % 4:j % 4 + 1], 1.0,
                                   ALU.mult, ALU.mult).then_inc(s_ph, 1)

            for j in range(4):
                prob_hi(j, j, True)
            with pool.Fori(1, 4 * KVH) as u:
                for j in range(4):
                    prob_hi(j, 4 * u + j, False)

            for c in range(4):
                quarter_lo(1, c, 4 * (KVH + 1) + c)
            with pool.Fori(0, KVH // 2 - 1) as i:
                for s in range(2):
                    for c in range(4):
                        quarter_lo(s, c, 4 * (KVH + 2) + 8 * i + 4 * s + c)
            for s in range(2):
                for c in range(4):
                    quarter_lo(s, c, 4 * (2 * KVH + s) + c)

        @block.vector
        def _(dve):
            linked = [0]

            def link(ins):
                ins.then_inc(s_dve, 1)
                linked[0] += 1
                dve.wait_ge(s_dve, linked[0])

            def spread(ap, n):
                return ap.unsqueeze(len(ap.shape)).to_broadcast(list(ap.shape) + [n])

            def layer_norm():
                for t in range(NT):
                    last = dve.bn_stats(st6[:, t, :], x_sb[:, t, :])
                link(last)
                for t in range(NT):
                    last = dve.bn_aggr(mv[:, t, :], st6[:, t, :])
                link(last)
                var, y, tmp = nw[:, 0, :], nw[:, 1, :], nw[:, 2, :]
                link(dve.tensor_scalar(var, mv[:, :, 1], EPS, None, ALU.add))
                link(dve.tensor_scalar(y.bitcast(I32), var.bitcast(I32), 1, None, ALU.arith_shift_right))
                link(dve.tensor_scalar(y.bitcast(I32), y.bitcast(I32), -1.0, RSQRT_MAGIC, ALU.mult, ALU.add))
                for _ in range(3):
                    link(dve.scalar_tensor_tensor(out=tmp, in0=y, scalar=-0.5, in1=y, op0=ALU.mult, op1=ALU.mult))
                    link(dve.tensor_tensor(tmp, tmp, var, ALU.mult))
                    link(dve.scalar_tensor_tensor(out=y, in0=tmp, scalar=1.5, in1=y, op0=ALU.add, op1=ALU.mult))

            def normalise(t):
                return dve.tensor_scalar(f32r[:, t, :], x_sb[:, t, :], mv[:, t, 0:1], nw[:, 1, t:t + 1],
                                         ALU.subtract, ALU.mult)

            dve.wait_ge(s_par, 16 * 7)
            for c in (0, 2):
                last = dve.reciprocal(scs[:, 4 + c // 2:5 + c // 2], scs[:, c:c + 1])
            dve.tensor_tensor(scs[:, 6:7], scs[:, 0:1], scs[:, 2:3], ALU.mult)
            for c in (1, 3):
                dve.tensor_scalar(scs[:, 7 + c // 2:8 + c // 2], scs[:, c:c + 1], -1.0, MID, ALU.mult, ALU.add)
            dve.memset(scs[:, 12:13], EPS)
            dve.memset(scs[:, 13:14], 2 * EPS)
            dve.memset(ones[:, :], 1.0)
            dve.memset(ones128, 1.0)
            for t in range(NT):
                dve.memset(gt[:, t, E_ROUTED:NE], 1.0)
            link(dve.scalar_tensor_tensor(out=wneg[:, :], in0=wneg[:, :], scalar=-1.0, in1=identf[:, :],
                                          op0=ALU.mult, op1=ALU.mult))
            dve.wait_ge(s_id, 4)
            dve.tensor_copy(identf[:, :], ident[:, :])
            for c in range(2):
                last = dve.tensor_tensor(scs[:, 9 + c:10 + c], scs[:, 6:7], scs[:, 7 + c:8 + c], ALU.mult)
            link(last)
            link(dve.scalar_tensor_tensor(out=scs[:, 11:12], in0=scs[:, 9:10], scalar=float(D), in1=scs[:, 8:9],
                                          op0=ALU.mult, op1=ALU.mult))
            dve.wait_ge(s_rwh, 1)
            dve.tensor_tensor(rws[:, 1, :], rw[:, :, :].rearrange("p k e -> p (k e)"), rws[:, 0, :],
                              ALU.subtract).then_inc(s_rws, 1)

            dve.wait_ge(s_x, 16)
            layer_norm()
            for t in range(NT):
                last = normalise(t)
            link(last)
            for t in range(NT):
                last = dve.tensor_scalar(f32r[:, t, :], f32r[:, t, :], scs[:, 4:5], scs[:, 1:2], ALU.mult, ALU.add)
            link(last)
            for t in range(NT):
                last = dve.tensor_scalar(f32r[:, t, :], f32r[:, t, :], 0.0, QMAX, ALU.max, ALU.min)
            link(last)
            for t in range(NT):
                dve.tensor_scalar(hlr[:, t, 0, :], f32r[:, t, :], ROUND, ROUND + MID, ALU.add, ALU.subtract).then_inc(s_xq, 1)
            dve.wait_ge(s_cn, 16)
            half = KC * D
            for b in range(BATCH):
                c32 = cnat[:, b * half:(b + 1) * half]
                link(dve.tensor_scalar(c32, c32, scs[:, 5:6], scs[:, 3:4], ALU.mult, ALU.add))
                link(dve.tensor_scalar(c32, c32, 0.0, QMAX, ALU.max, ALU.min))
                dve.tensor_scalar(cq[:, b * half:(b + 1) * half], c32, ROUND, ROUND + MID, ALU.add, ALU.subtract)\
                   .then_inc(s_cq, 1)
            dve.wait_ge(s_xqT, NT)
            for b in range(2):
                dve.tensor_copy(words(pT1[:, b, :, :]), ps[4 + b][:, :].rearrange("p (l w) -> p l w", l=2)).then_inc(s_xqTc, 1)
            dve.wait_ge(s_sums, BATCH + 1)
            dve.tensor_scalar(nw[:, 3, :], ps[4][:, 0:NT], scs[:, 10:11], scs[:, 11:12], ALU.mult, ALU.add)
            for b in range(BATCH):
                last = dve.tensor_scalar(f32r[:, b, :], ps[6 + b][:, :], scs[:, 9:10], None, ALU.mult)
            linked[0] += 1
            last.then_inc(s_dve, 1)
            dve.wait_ge(s_dve, linked[0])
            for t in range(NT):
                last = dve.scalar_tensor_tensor(out=x_sb[:, t, :], in0=x_sb[:, t, :], scalar=nw[:, 3, t:t + 1],
                                                in1=f32r[:, t // 2, :], op0=ALU.add, op1=ALU.add)
            last.then_inc(s_vfree, 4)
            for t in range(NT):
                dve.wait_ge(s_main, t + 1)
                if t == 0:
                    dve.wait_ge(s_vfree, 4)
                last = dve.scalar_tensor_tensor(out=x_sb[:, t, :], in0=ps[t][:, :], scalar=scs[:, 6:7],
                                                in1=x_sb[:, t, :], op0=ALU.mult, op1=ALU.add)
            link(last)

            def ln_split(n):
                layer_norm()
                for t in range(NT):
                    normalise(t).then_inc(s_ln, 1)
                for t in range(NT):
                    dve.wait_ge(s_lnh, NT * n + t + 1)
                    dve.tensor_tensor(hlr[:, t, 1, :], f32r[:, t, :], hlr[:, t, 0, :], ALU.subtract).then_inc(s_lnl, 1)

            def ln_copies(n):
                for t in range(NT):
                    dve.wait_ge(s_lnT, NT * n + t + 1)
                    dve.tensor_copy(words(xT[:, t, :, :]), ps[t][:, :].rearrange("p (l w) -> p l w", l=2)).then_inc(s_lnTc, 1)

            def v_lo(hg):
                with dve.Fori(0, NST // 4) as i:
                    for j in range(4):
                        dve.wait_ge(s_vh, NST * hg + 4 * i + j + 1)
                        at = slice(hg * GW, (hg + 1) * GW)
                        dve.tensor_tensor(v_sb[:, bass.ds(4 * i + j, 1), 1, at], ps[4 + j][:, :],
                                          v_sb[:, bass.ds(4 * i + j, 1), 0, at], ALU.subtract).then_inc(s_vfree, 1)

            ln_split(0)
            v_lo(0)
            ln_copies(0)

            lg, ex = sml[:, 0:4, :], sml[:, 4:8, :]
            dve.wait_ge(s_rt, 1)
            link(dve.tensor_tensor(lg, ps[4][:, 0:NT * E_ROUTED].rearrange("p (t e) -> p t e", t=NT),
                                   rb[:, 0, :].rearrange("p (t e) -> p t e", t=NT), ALU.add))
            link(dve.tensor_reduce(rstat[:, 0, :], lg, AX_X, ALU.max))
            dve.tensor_tensor(lg, lg, spread(rstat[:, 0, :], E_ROUTED), ALU.subtract).then_inc(s_lg, 2)
            dve.wait_ge(s_rex, 1)
            link(dve.tensor_reduce(rstat[:, 1, :], ex, AX_X, ALU.add))
            link(dve.reciprocal(rstat[:, 2, :], rstat[:, 1, :]))
            link(dve.tensor_tensor(ex, ex, spread(rstat[:, 2, :], E_ROUTED), ALU.mult))
            link(dve.tensor_tensor(ex, ex, rb[:, 1, :].rearrange("p (t e) -> p t e", t=NT), ALU.add))

            def ranks(vals, n, dst):
                gt_, eq_ = (c[:, 0:NT * n * n].rearrange("p (t i j) -> p t i j", t=NT, i=n) for c in (cmp_gt, cmp_eq))
                other = vals.unsqueeze(2).to_broadcast([P, NT, n, n])
                own = spread(vals, n)
                below = lower[:, 0:n, 0:n].unsqueeze(1).to_broadcast([P, NT, n, n])
                dve.tensor_tensor(gt_, other, own, ALU.is_gt)
                link(dve.tensor_tensor(eq_, other, own, ALU.is_equal))
                link(dve.tensor_tensor(eq_, eq_, below, ALU.mult))
                link(dve.tensor_tensor(gt_, gt_, eq_, ALU.add))
                link(dve.tensor_reduce(dst, gt_, AX_X, ALU.add))

            gmax = lg[:, :, 0:GROUPS]
            grank = lg[:, :, GROUPS:2 * GROUPS]
            masked = lg[:, :, :]
            link(dve.tensor_reduce(gmax, ex.rearrange("p t (g e) -> p t g e", g=GROUPS), AX_X, ALU.max))
            ranks(gmax, GROUPS, grank)
            link(dve.tensor_scalar(rstat[:, :, :], grank, float(TOPG), -BIG, ALU.is_ge, ALU.mult))
            link(dve.tensor_tensor(masked.rearrange("p t (g e) -> p t g e", g=GROUPS), ex.rearrange("p t (g e) -> p t g e", g=GROUPS),
                                   spread(rstat[:, :, :], EPG), ALU.add))
            ranks(masked, E_ROUTED, rb[:, 0, :].rearrange("p (t e) -> p t e", t=NT))
            dve.scalar_tensor_tensor(out=gt[:, :, 0:E_ROUTED], in0=rb[:, 0, :].rearrange("p (t e) -> p t e", t=NT),
                                     scalar=float(TOPE), in1=ex, op0=ALU.is_lt, op1=ALU.mult).then_inc(s_gate, 1)
            dve.wait_ge(s_mask, 16)
            dve.tensor_scalar(nmask[:, :, :], nmask[:, :, :], -8.0, None, ALU.mult)

            def rms_phase(r0, iters, tiles, weighted):
                def sums(r, j, first):
                    dve.wait_ge(s_sq, r + 1)
                    if not first or j >= 2:
                        dve.wait_ge(s_root, r - 1)
                    dve.tensor_reduce(ss[:, j % 2, :], f32r[:, j % 2, :].rearrange("p (h d) -> p h d", h=REP),
                                      AX_X, ALU.add).then_inc(s_ss, 1)

                def normed(r, j, first):
                    dve.wait_ge(s_root, r + 1)
                    dve.reciprocal(rrt[:, j % 2, :], root[:, j % 2, :]).then_inc(s_rr, 1)
                    dve.wait_ge(s_rr, r + 1)
                    if not first or j >= 2:
                        dve.wait_ge(s_nl, r - 1)
                    dst, bank = f32r[:, 2 + j % 2, :], ps[j % 4]
                    if weighted:
                        for h in range(REP):
                            at = slice(h * HD, (h + 1) * HD)
                            last = dve.scalar_tensor_tensor(out=dst[:, at], in0=bank[:, at], scalar=rrt[:, j % 2, h:h + 1],
                                                            in1=wneg[:, :], op0=ALU.mult, op1=ALU.mult)
                    else:
                        last = dve.tensor_tensor(dst.rearrange("p (h d) -> p h d", h=REP),
                                                 bank[:, :].rearrange("p (h d) -> p h d", h=REP),
                                                 spread(rrt[:, j % 2, :], HD), ALU.mult)
                    last.then_inc(s_nrm, 1)

                def body(i, first):
                    for j in range(tiles):
                        r = r0 + tiles * i + j
                        sums(r, j, first)
                        if not first or j >= 1:
                            normed(r - 1, (j - 1) % tiles, first and j - 1 < 2)

                body(0, True)
                with dve.Fori(1, iters) as i:
                    body(i, False)
                normed(r0 + tiles * iters - 1, tiles - 1, False)

            rms_phase(0, 4, 4, True)

            dve.wait_ge(s_gT, 1)
            dve.wait_ge(s_nl, 16)
            dve.tensor_copy(gateT[0:NE, :], ps[7][0:NE, :]).then_inc(s_gTc, 1)

            def expert(e, s):
                tile, bank = f32r[:, s, :], ps[5 + 2 * s]
                dve.wait_ge(s_silu, e + 1)
                dve.wait_ge(s_up, 2 * e + 2)
                dve.scalar_tensor_tensor(out=tile, in0=bank[:, :], scalar=mb[:, 1, bass.ds(e, 1)], in1=tile,
                                         op0=ALU.add, op1=ALU.mult).then_inc(s_hx, 1)
                dve.wait_ge(s_hx, e + 1)
                dve.wait_ge(s_gload[s], 8 * (e - s) + 16)
                dve.tensor_tensor(tile, tile, gate_bc[s], ALU.mult).then_inc(s_hg, 1)
                dve.wait_ge(s_hh, e + 1)
                dve.tensor_tensor(hlr[:, s, 1, :], tile, hlr[:, s, 0, :], ALU.subtract).then_inc(s_hl, 1)

            with dve.Fori(0, NE // 2) as i:
                for s in range(2):
                    expert(2 * i + s, s)
            dve.wait_ge(s_dn, NE)
            for t in range(NT):
                last = dve.tensor_tensor(x_sb[:, t, :], ps[t][:, :], x_sb[:, t, :], ALU.add)
            link(last)
            ln_split(1)
            v_lo(1)
            ln_copies(1)
            rms_phase(16, 4, 2 * NT, False)

            def masked_scores(j, k, qt, first):
                scored, freed = k + 1, k - 3
                if not first:
                    scored, freed = dve.to_reg(scored), dve.to_reg(freed)
                dve.wait_ge(s_mask, 16)
                dve.wait_ge(s_s, scored)
                if not first or j >= 4:
                    dve.wait_ge(s_pl, freed)
                dve.tensor_tensor_reduce(f32r[:, j % 4, :], ps[j % 4][:, :], nmask[:, qt, :], 0.125, BIG,
                                         ALU.add, ALU.min, mneg[:, j % 4:j % 4 + 1]).then_inc(s_t, 1)

            def inverse_sum(j, k):
                dve.wait_ge(s_e, k + 1)
                dve.reciprocal(rinv[:, 0, j % 4:j % 4 + 1], psum_col[:, j % 4:j % 4 + 1]).then_inc(s_r0, 1)

            def scaled_inverse(j, k):
                dve.wait_ge(s_r0, k + 1)
                dve.tensor_scalar(rinv[:, 1, j % 4:j % 4 + 1], rinv[:, 0, j % 4:j % 4 + 1], PSCALE, None,
                                  ALU.mult).then_inc(s_r, 1)

            def prob_lo(j, k):
                dve.wait_ge(s_ph, k + 1)
                dve.scalar_tensor_tensor(out=hlr[:, j % 4, 1, :], in0=f32r[:, j % 4, :], scalar=rinv[:, 1, j % 4:j % 4 + 1],
                                         in1=hlr[:, j % 4, 0, :], op0=ALU.mult, op1=ALU.subtract).then_inc(s_pl, 1)

            def o_lo(w, mw):
                dve.wait_ge(s_oh, w + 1)
                dve.scalar_tensor_tensor(out=q_sb[:, bass.ds(w, 1), 1, :], in0=ps[6 + mw % 2][:, :], scalar=1.0 / PSCALE,
                                         in1=q_sb[:, bass.ds(w, 1), 0, :], op0=ALU.mult, op1=ALU.subtract).then_inc(s_ol, 1)

            def attention(g, first):
                for j in range(4 * REP):
                    k = 16 * g + j
                    m, hh = divmod(j, REP)
                    masked_scores(j, k, m % QT_PER_B, first)
                    if not first or j >= 1:
                        inverse_sum((j - 1) % 4, k - 1)
                    if not first or j >= 2:
                        prob_lo((j - 2) % 4, k - 2)
                    if not first or j >= 1:
                        scaled_inverse((j - 1) % 4, k - 1)
                    if hh == 1 and (not first or m >= 3):
                        o_lo(4 * g + m - 3, (m - 3) % 4)

            attention(0, True)
            with dve.Fori(1, KVH) as g:
                attention(g, False)
            end = 16 * KVH
            inverse_sum(3, end - 1)
            prob_lo(2, end - 2)
            scaled_inverse(3, end - 1)
            prob_lo(3, end - 1)
            for m in range(3):
                o_lo(4 * KVH - 3 + m, (m + 1) % 4)

            dve.wait_ge(s_od, KVH)
            for t in range(NT):
                last = dve.tensor_tensor(x_sb[:, t, :], ps[t][:, :], x_sb[:, t, :], ALU.add)
            link(last)
            ln_split(2)
            ln_copies(2)

            dve.wait_ge(s_lw, 2)
            dve.tensor_tensor(lwqs[:, 1, :], lwq.rearrange("p k r -> p (k r)"), lwqs[:, 0, :], ALU.subtract)
            dve.tensor_tensor(lkys[:, 1, :], lky, lkys[:, 0, :], ALU.subtract).then_inc(s_lwl, 1)
            dve.wait_ge(s_lqh, 1)
            dve.tensor_tensor(lqs[:, 1, :], ps[4][0:RD, :], lqs[:, 0, :], ALU.subtract).then_inc(s_lqs, 1)
            dve.wait_ge(s_lsc, 1)
            link(dve.tensor_copy(lsc, ps[5][:, 0:NT * L_EXP].rearrange("p (t e) -> p t e", t=NT)))
            for t in range(NT):
                last = dve.max(lm8[:, t, 0, :], lsc[:, t, :])
            link(last)
            for t in range(NT):
                dve.match_replace(lw1[:, t, :], lm8[:, t, 0, :], lsc[:, t, :], -BIG)
                last = dve.tensor_scalar(lng[:, t:t + 1], lm8[:, t, 0, 0:1], -1.0, None, ALU.mult)
                last.then_inc(s_lng, 1)
            dve.wait_ge(s_lng, NT)
            for t in range(NT):
                last = dve.max(lm8[:, t, 1, :], lw1[:, t, :])
            link(last)
            for t in range(NT):
                last = dve.match_replace(lw2[:, t, :], lm8[:, t, 1, :], lw1[:, t, :], -BIG)
            link(last)
            link(dve.tensor_tensor(lw2, lw2, lsc, ALU.not_equal))
            dve.wait_ge(s_lex, NT)
            link(dve.tensor_tensor(lex, lex, lw2, ALU.mult))
            link(dve.tensor_reduce(lsum[:, 0:NT], lex, AX_X, ALU.add))
            link(dve.reciprocal(lsum[:, NT:2 * NT], lsum[:, 0:NT]))
            link(dve.tensor_tensor(lex, lex, spread(lsum[:, NT:2 * NT], L_EXP), ALU.mult))
            for t in range(NT):
                dve.wait_ge(s_z, t + 1)
                dve.tensor_tensor(f32r[:, t, :].rearrange("p (e r) -> p e r", r=RANK),
                                  ps[t][:, :].rearrange("p (e r) -> p e r", r=RANK),
                                  spread(lex[:, t, :], RANK), ALU.mult).then_inc(s_zg, 1)
            for t in range(NT):
                dve.wait_ge(s_zh, t + 1)
                dve.tensor_tensor(hlr[:, t, 1, :], f32r[:, t, :], hlr[:, t, 0, :], ALU.subtract).then_inc(s_zl, 1)
            for t in range(NT):
                dve.wait_ge(s_zT, t + 1)
                dve.tensor_copy(words(zT[:, t, :, :]), ps[6 + t % 2][:, :].rearrange("p (l w) -> p l w", l=2)).then_inc(s_zTc, 1)
            for t in range(NT):
                dve.wait_ge(s_y, t + 1)
                dve.scalar_tensor_tensor(out=x_sb[:, t, :], in0=ps[t][:, :], scalar=L_SCALING, in1=x_sb[:, t, :],
                                         op0=ALU.mult, op1=ALU.add).then_inc(s_fin, 1)


def kernel(x, ctx_4096, mask_1x1xSxS2_ff0, L0_xattn_x1_scale, L0_xattn_x1_zp, L0_xattn_x2_scale, L0_xattn_x2_zp,
           L0_ffn_router_w, L0_ffn_router_b, L0_ffn_router_bias, L0_ffn_ew1, L0_ffn_eb1, L0_ffn_ew2, L0_ffn_eb2,
           L0_ffn_ew3, L0_ffn_eb3, L0_ffn_sw1, L0_ffn_sb1, L0_ffn_sw2, L0_ffn_sb2, L0_ffn_sw3, L0_ffn_sb3,
           L1_xattn_q_proj_w, L1_xattn_k_proj_w, L1_xattn_v_proj_w, L1_xattn_o_proj_w, L1_xattn_q_norm_w,
           L1_xattn_k_norm_w, L1_ffn_A_w, L1_ffn_B_w, L1_ffn_Wq_w, L1_ffn_keys):
    import numpy as np
    import concourse.bacc as bacc
    from concourse.bass_utils import run_bass_kernel_spmd

    def a(v):
        return np.asarray(v)

    def chunked(w):
        return w.reshape(KC, P, -1).transpose(1, 0, 2)

    def groups(w):
        return chunked(w).reshape(P, KC, -1, GW).transpose(2, 0, 1, 3).reshape(-1, P, WG)

    def rows(v, n=1):
        return np.tile(v.reshape(1, -1), (P, n))

    ctx = a(ctx_4096)
    ctx_t = ctx.transpose(2, 0, 1).reshape(D, BATCH * CTX)
    wk, wv = groups(a(L1_xattn_k_proj_w).T), groups(a(L1_xattn_v_proj_w).T)

    def experts(ew, sw):
        both = np.concatenate([ew, sw.reshape(D, 2, INTER).transpose(1, 0, 2)])
        return both.reshape(NE, KC, P, INTER).transpose(0, 2, 1, 3).reshape(NE, P, KC * INTER)

    moe = np.concatenate([experts(a(L0_ffn_ew1), a(L0_ffn_sw1)), experts(a(L0_ffn_ew2), a(L0_ffn_sw2)),
                          np.concatenate([a(L0_ffn_ew3), a(L0_ffn_sw3).reshape(2, INTER, D)])], axis=2)
    moe_b = np.stack([np.concatenate([a(L0_ffn_eb1), a(L0_ffn_sb1).reshape(2, INTER)]).T,
                      np.concatenate([a(L0_ffn_eb2), a(L0_ffn_sb2).reshape(2, INTER)]).T], axis=1)
    arrays = {
        "x_rows": a(x).reshape(TOK, D),
        "ctx_nat": ctx.reshape(BATCH * KC, P, D).transpose(1, 0, 2).reshape(P, -1),
        "ctx_t": chunked(ctx_t).reshape(P, 2, WG),
        "mask": a(mask_1x1xSxS2_ff0).reshape(SEQ, CTX),
        "scal": rows(np.concatenate([a(v).reshape(1) for v in (L0_xattn_x1_scale, L0_xattn_x1_zp,
                                                               L0_xattn_x2_scale, L0_xattn_x2_zp)])),
        "wkv": np.stack([wv[0], wk[0], wk[1], wv[1]]),
        "moe": moe,
        "moe_b": moe_b,
        "moe_b3": np.concatenate([a(L0_ffn_eb3), a(L0_ffn_sb3).reshape(1, D)]),
        "router_w": chunked(a(L0_ffn_router_w)),
        "router_b": rows(a(L0_ffn_router_b), NT),
        "router_bias": rows(a(L0_ffn_router_bias), NT),
        "wq": groups(a(L1_xattn_q_proj_w).T),
        "wo": a(L1_xattn_o_proj_w).T.reshape(KVH, REP, P, D).transpose(0, 2, 1, 3).reshape(KVH, P, WG),
        "qk_norm": np.stack([rows(a(L1_xattn_q_norm_w)), rows(a(L1_xattn_k_norm_w))], axis=1),
        "a_w": chunked(a(L1_ffn_A_w).T).reshape(P, WG),
        "b_w": chunked(a(L1_ffn_B_w).T).reshape(P, WG),
        "l_wq": chunked(a(L1_ffn_Wq_w).T),
        "l_keys": a(L1_ffn_keys).T,
    }
    nc = bacc.Bacc("TRN2", target_bir_lowering=False, num_devices=1)
    sent, args = {}, {}
    for name, v in arrays.items():
        v = np.ascontiguousarray(v)
        sent["in_" + name] = v
        args[name] = nc.dram_tensor("in_" + name, v.shape, mybir.dt.from_np(v.dtype), kind="ExternalInput").ap()
    out = nc.dram_tensor("out_x", (TOK, D), F32, kind="ExternalOutput").ap()
    xattn_ffn_kernel(nc, out=out, **args)
    r = run_bass_kernel_spmd(nc, [sent], core_ids=[0])
    return r.results[0]["out_x"].reshape(BATCH, SEQ, D)
```

```python
from contextlib import ExitStack

import concourse.bass as bass
from concourse import mybir

P = 128
D = 512
KC = D // P
BATCH, SEQ, CTX = 2, 256, 512
TOK = BATCH * SEQ
NT = TOK // P
QT_PER_B = SEQ // P
SC = CTX // P
NST = BATCH * SC
HEADS, KVH, HD = 32, 8, 128
REP = HEADS // KVH
E_ROUTED, GROUPS, TOPG, TOPE = 16, 4, 2, 2
EPG = E_ROUTED // GROUPS
NE = 18
INTER = 128
L_EXP, RANK, RD = 64, 8, 16
GW = 512
WG = KC * GW
EG = 2 * KC * INTER + D

QUARTERS = ((0, 1), (2,), (3,), ())

PAR_QN, PAR_KN, PAR_MB = 0, HD, 2 * HD
PAR_RW = PAR_MB + 2 * NE
PAR_RB = PAR_RW + KC * E_ROUTED
PAR_SC = PAR_RB + 2 * NT * E_ROUTED
PAR_END = PAR_SC + 16

ROUND = 12582912.0
MID = 128.0
QMAX = 255.0
EPS = 1e-5
RSQRT_MAGIC = float(0x5F3759DF)
BIG = 3.0e38
PSCALE = 16384.0
L_SCALING = 32.0 / 16.0

ALU = mybir.AluOpType
ACT = mybir.ActivationFunctionType
F16 = mybir.dt.float16
F32 = mybir.dt.float32
I32 = mybir.dt.int32
AX_X = mybir.AxisListType.X


def xattn_ffn_kernel(nc, x_rows, ctx_nat, ctx_t, mask, params, wkv, moe, moe_b3, wq, wo, a_w, b_w, l_wq, l_keys, out):
    gates_dram = nc.dram_tensor("gates_dram", (NE, TOK), F32, kind="Internal").ap()
    with ExitStack() as ctx:
        def sb(name, shape, dt):
            return ctx.enter_context(nc.sbuf_tensor(name, shape, dt))

        def sem(name):
            return ctx.enter_context(nc.semaphore(name))

        k_sb = sb("k_sb", [P, KVH, 2, BATCH * CTX], F16)
        v_sb = sb("v_sb", [P, NST, 2, KVH * HD], F16)
        q_sb = sb("q_sb", [P, KVH * NT, 2, REP * P], F16)
        x_sb = sb("x_sb", [P, NT, D], F32)
        xT = sb("xT", [P, NT, 2, D], F16)
        nmask = sb("nmask", [P, QT_PER_B, CTX], F32)
        stage = sb("stage", [P, 2, WG], F32)
        wsp = sb("wsp", [P, 2, 2, WG], F16)
        f32r = sb("f32r", [P, 4, GW], F32)
        hlr = sb("hlr", [P, 4, 2, GW], F16)
        pT1 = sb("pT1", [P, 4, 2, GW], F16)
        ident = sb("ident", [P, P], F16)
        par = sb("par", [P, PAR_END], F32)
        wneg = par[:, PAR_QN:PAR_KN]
        identf = par[:, PAR_KN:PAR_MB]
        mb = par[:, PAR_MB:PAR_RW].rearrange("p (a e) -> p a e", a=2)
        rw = par[:, PAR_RW:PAR_RB]
        rb = par[:, PAR_RB:PAR_SC].rearrange("p (a n) -> p a n", a=2)
        scs = par[:, PAR_SC:PAR_END]
        rws = sb("rws", [P, 2, KC * E_ROUTED], F16)
        ones = sb("ones", [P, 1], F16)
        st6 = sb("st6", [P, NT, 6], F32)
        mv = sb("mv", [P, NT, 2], F32)
        nw = sb("nw", [P, 4, NT], F32)
        sml = sb("sml", [P, 8, 16], F32)

        early = q_sb[:, :, :, :].rearrange("p a b c -> p (a b c)")
        ctxs = early[:, 0:2 * KC * NST * P].rearrange("p (k l s) -> p k l s", k=KC, l=2)
        wkvs = early[:, 8192:24576].rearrange("p (w l c) -> p w l c", w=4, l=2)
        cnat = early[:, 24576:32768].bitcast(F32)
        cq = xT[:, :, :, :].rearrange("p a b c -> p (a b c)")
        xqT = pT1[:, 0:2, :, :].rearrange("p a b (k t) -> p (a b) k t", k=KC)
        ones128 = pT1[:, 2, 0, 0:P]
        pT0 = xT
        pT = [pT0, pT1]
        gate_bc = [hlr[:, 2, :, :].rearrange("p a b -> p (a b)").bitcast(F32),
                   hlr[:, 3, :, :].rearrange("p a b -> p (a b)").bitcast(F32)]
        b3s = stage[:, 1, EG:WG]
        gateT = stage[:, 0, EG:WG]
        kv_land = k_sb[:, :, :, :].rearrange("p a b c -> p (a b c)").bitcast(F32).rearrange("p (w c) -> p w c", w=4)
        gt = ctx.enter_context(nc.sbuf_tensor("gt", [P, NT, NE], F32))
        rstat = ctx.enter_context(nc.sbuf_tensor("rstat", [P, 4, NT], F32))
        cmp_gt = pT1[:, 0, :, :].rearrange("p a b -> p (a b)")
        cmp_eq = pT1[:, 1, :, :].rearrange("p a b -> p (a b)")
        mneg = ctx.enter_context(nc.sbuf_tensor("mneg", [P, 4], F32))
        psum_col = ctx.enter_context(nc.sbuf_tensor("psum_col", [P, 4], F32))
        rinv = ctx.enter_context(nc.sbuf_tensor("rinv", [P, 2, 4], F32))
        ss = ctx.enter_context(nc.sbuf_tensor("ss", [P, 2, REP], F32))
        root = ctx.enter_context(nc.sbuf_tensor("root", [P, 2, REP], F32))
        rrt = ctx.enter_context(nc.sbuf_tensor("rrt", [P, 2, REP], F32))
        late = k_sb[:, :, :, :].rearrange("p a b c -> p (a b c)").bitcast(F32)
        lower = pT1[:, 3, 0, 0:E_ROUTED * E_ROUTED].rearrange("p (i j) -> p i j", i=E_ROUTED)
        lwq = late[:, 0:64].rearrange("p (k r) -> p k r", k=KC)
        lky = late[0:RD, 64:128]
        lwqs = late[:, 128:192].bitcast(F16).rearrange("p (l c) -> p l c", l=2)
        lkys = late[0:RD, 192:256].bitcast(F16).rearrange("p (l c) -> p l c", l=2)
        lqs = late[0:RD, 256:768].bitcast(F16).rearrange("p (l c) -> p l c", l=2)
        lsc = late[:, 1024:1280].rearrange("p (t e) -> p t e", t=NT)
        lw1 = late[:, 1280:1536].rearrange("p (t e) -> p t e", t=NT)
        lw2 = late[:, 1536:1792].rearrange("p (t e) -> p t e", t=NT)
        lex = late[:, 1792:2048].rearrange("p (t e) -> p t e", t=NT)
        lm8 = late[:, 2048:2112].rearrange("p (t a b) -> p t a b", t=NT, a=2)
        lng = late[:, 2112:2120]
        lsum = late[:, 2120:2128]
        zT = late[:, 4096:6144].bitcast(F16).rearrange("p (t l c) -> p t l c", t=NT, l=2)

        ps = [ctx.enter_context(nc.psum_tensor(f"ps{i}", [P, 512], F32)) for i in range(8)]

        s_x = sem("s_x")
        s_cn = sem("s_cn")
        s_par = sem("s_par")
        s_late = sem("s_late")
        s_mask = sem("s_mask")
        s_w = [sem("s_w0"), sem("s_w1")]
        s_e12 = [sem("s_e12_0"), sem("s_e12_1")]
        s_e3 = [sem("s_e3_0"), sem("s_e3_1")]
        s_ctx = [sem("s_ctx0"), sem("s_ctx1")]
        s_kv = [sem(f"s_kv{w}") for w in range(4)]
        s_firsth = sem("s_firsth")
        s_firstl = sem("s_firstl")
        s_v0l = sem("s_v0l")
        s_whi = sem("s_whi")
        s_wlo = sem("s_wlo")
        s_w12h = sem("s_w12h")
        s_w12l = sem("s_w12l")
        s_w3h = sem("s_w3h")
        s_w3l = sem("s_w3l")
        s_wqh = sem("s_wqh")
        s_wql = sem("s_wql")
        s_gload = [sem("s_gload0"), sem("s_gload1")]
        s_b3 = sem("s_b3")
        s_gst = sem("s_gst")
        s_id = sem("s_id")
        s_dve = sem("s_dve")
        s_xq = sem("s_xq")
        s_xqT = sem("s_xqT")
        s_xqTc = sem("s_xqTc")
        s_cq = sem("s_cq")
        s_sums = sem("s_sums")
        s_sumsc = sem("s_sumsc")
        s_main = sem("s_main")
        s_ln = sem("s_ln")
        s_lnh = sem("s_lnh")
        s_lnl = sem("s_lnl")
        s_lnT = sem("s_lnT")
        s_lnTc = sem("s_lnTc")
        s_rwh = sem("s_rwh")
        s_rws = sem("s_rws")
        s_rt = sem("s_rt")
        s_lg = sem("s_lg")
        s_rex = sem("s_rex")
        s_gate = sem("s_gate")
        s_gT = sem("s_gT")
        s_gTc = sem("s_gTc")
        s_vp = sem("s_vp")
        s_vh = sem("s_vh")
        s_vfree = sem("s_vfree")
        s_pj = sem("s_pj")
        s_sq = sem("s_sq")
        s_ss = sem("s_ss")
        s_root = sem("s_root")
        s_rr = sem("s_rr")
        s_nrm = sem("s_nrm")
        s_nh = sem("s_nh")
        s_nl = sem("s_nl")
        s_tr = sem("s_tr")
        s_trc = sem("s_trc")
        s_up = sem("s_up")
        s_silu = sem("s_silu")
        s_hx = sem("s_hx")
        s_hg = sem("s_hg")
        s_hh = sem("s_hh")
        s_hl = sem("s_hl")
        s_dn = sem("s_dn")
        s_s = sem("s_s")
        s_t = sem("s_t")
        s_e = sem("s_e")
        s_r0 = sem("s_r0")
        s_r = sem("s_r")
        s_ph = sem("s_ph")
        s_pl = sem("s_pl")
        s_T = sem("s_T")
        s_Tc = sem("s_Tc")
        s_pv = sem("s_pv")
        s_oh = sem("s_oh")
        s_ol = sem("s_ol")
        s_od = sem("s_od")
        s_lw = sem("s_lw")
        s_lwl = sem("s_lwl")
        s_lq = sem("s_lq")
        s_lqh = sem("s_lqh")
        s_lqs = sem("s_lqs")
        s_lsc = sem("s_lsc")
        s_lng = sem("s_lng")
        s_lex = sem("s_lex")
        s_z = sem("s_z")
        s_zg = sem("s_zg")
        s_zh = sem("s_zh")
        s_zl = sem("s_zl")
        s_zT = sem("s_zT")
        s_zTc = sem("s_zTc")
        s_y = sem("s_y")
        s_fin = sem("s_fin")
        s_out = sem("s_out")

        def words(ap):
            return ap.bitcast(F32)

        def three_products(pe, dst, lhs, rhs, start, stop):
            pe.matmul(dst, lhs[0], rhs[1], start=start, stop=False, skip_group_check=True)
            pe.matmul(dst, lhs[1], rhs[0], start=False, stop=False, skip_group_check=True)
            return pe.matmul(dst, lhs[0], rhs[0], start=False, stop=stop, skip_group_check=True)

        W12, W3 = slice(0, 2 * KC * INTER), slice(2 * KC * INTER, EG)

        block = ctx.enter_context(nc.Block())

        @block.sync
        def _(sp):
            def load(slot, src, width):
                sp.dma_start(stage[:, slot, 0:width], src).then_inc(s_w[slot], 16)

            sp.dma_start(stage[:, 0, :], ctx_t[:, 0, :]).then_inc(s_ctx[0], 16)
            sp.dma_start(kv_land[:, 0, :], wkv[0]).then_inc(s_kv[0], 16)
            sp.dma_start(par[:, 0:PAR_SC + 4], params).then_inc(s_par, 16)
            sp.dma_start(x_sb[:, :, :], x_rows.rearrange("(t p) d -> p t d", p=P)).then_inc(s_x, 16)
            sp.dma_start(stage[:, 1, :], ctx_t[:, 1, :]).then_inc(s_ctx[1], 16)
            sp.dma_start(cnat, ctx_nat).then_inc(s_cn, 16)
            for w in (3, 1, 2):
                sp.dma_start(kv_land[:, w, :], wkv[w]).then_inc(s_kv[w], 16)

            def load_w12(e, s):
                sp.dma_start(stage[:, s, W12], moe[e][:, W12]).then_inc(s_e12[s], 16)

            def load_w3(e, s):
                sp.dma_start(stage[:, s, W3], moe[e][:, W3]).then_inc(s_e3[s], 16)

            sp.wait_ge(s_firstl, 4)
            load_w12(0, 0)
            load_w3(0, 0)
            sp.wait_ge(s_wlo, 1)
            load_w12(1, 1)
            load_w3(1, 1)
            sp.dma_start(b3s[0:E_ROUTED + 1, :], moe_b3).then_inc(s_b3, 16)
            sp.dma_start(nmask[:, :, :], mask.rearrange("(h p) c -> p h c", p=P)).then_inc(s_mask, 16)
            sp.wait_ge(s_w12l, 1)
            load_w12(2, 0)
            sp.wait_ge(s_w12l, 2)
            load_w12(3, 1)
            sp.wait_ge(s_w3l, 1)
            load_w3(2, 0)
            with sp.Fori(2, NE // 2) as i:
                for s in range(2):
                    sp.wait_ge(s_w12l, 2 * i + s - 1)
                    load_w12(2 * i + s, s)
                    sp.wait_ge(s_w3l, 2 * i + s - 2)
                    load_w3(2 * i + s - 1, 1 - s)
            sp.wait_ge(s_w3l, NE - 2)
            load_w3(NE - 1, 1)
            for s in range(2):
                sp.wait_ge(s_w3l, NE - 1 + s)
                load(s, wq[s], WG)
            with sp.Fori(1, KVH // 2) as i:
                for s in range(2):
                    sp.wait_ge(s_wql, 4 * (2 * i + s - 1))
                    load(s, wq[2 * i + s], WG)
            with sp.Fori(0, KVH // 2) as i:
                for s in range(2):
                    sp.wait_ge(s_wql, 4 * (KVH + 2 * i + s - 1))
                    load(s, wo[2 * i + s], WG)
            for s, src in enumerate((a_w, b_w)):
                sp.wait_ge(s_wql, 4 * (2 * KVH + s - 1))
                load(s, src, WG)
            for t in range(NT):
                sp.wait_ge(s_fin, t + 1)
                sp.dma_start(out[t * P:(t + 1) * P, :], x_sb[:, t, :]).then_inc(s_out, 16)
            sp.wait_ge(s_out, 16 * NT)

        @block.tensor
        def _(pe):
            def transposes(src_hi_lo, dst, place):
                for l in range(2):
                    for c in range(4):
                        at = place(l, c) * P
                        last = pe.transpose(dst.bitcast(F16)[:, at:at + P], src_hi_lo[:, l, c * P:(c + 1) * P], ident[:, :])
                return last

            def hi_lo_major(l, c):
                return 4 * l + c

            def block_major(l, c):
                return 2 * c + l

            def ln_transposes(n):
                for t in range(NT):
                    pe.wait_ge(s_lnl, NT * n + t + 1)
                    transposes(hlr[:, t, :, :], ps[t][:, :], hi_lo_major).then_inc(s_lnT, 1)

            def v_rows(hg, b):
                w = (0, 3)[hg]
                if b == 1:
                    pe.wait_ge(s_wlo, 1)
                if hg == 1:
                    pe.wait_ge(s_wlo, 2)
                for j in range(SC):
                    if hg == 0 and b == 1:
                        pe.wait_ge(s_vfree, j + 1)
                    for c in range(KC):
                        if hg == 0 and b == 0 and j == 0:
                            pe.wait_ge(s_firstl if c < 2 else s_v0l, 5 + c if c < 2 else c - 1)
                        last = three_products(
                            pe, ps[4 + j][:, :],
                            [ctxs[:, c, l, b * CTX + j * P:b * CTX + (j + 1) * P] for l in range(2)],
                            [wkvs[:, w, l, c * GW:(c + 1) * GW] for l in range(2)], c == 0, c == KC - 1)
                    last.then_inc(s_vp, 1)

            def rms_phase(r0, iters, tiles, project, place, before_last=None):
                def transposed(r, j):
                    pe.wait_ge(s_nl, r + 1)
                    pe.wait_ge(s_trc, r + 1)
                    transposes(hlr[:, j % 4, :, :], ps[6 + j % 2][:, :], place).then_inc(s_tr, 1)

                def body(i, first):
                    for j in range(tiles):
                        r = r0 + tiles * i + j
                        if not first or j >= 4:
                            pe.wait_ge(s_nrm, r - 3)
                        project(i, j).then_inc(s_pj, 1)
                        if not first or j >= 4:
                            transposed(r - 4, j)

                body(0, True)
                with pe.Fori(1, iters) as i:
                    body(i, False)
                if before_last:
                    before_last()
                for j in range(4):
                    transposed(r0 + tiles * iters - 4 + j, j)

            def k_project(i, j):
                for c in range(KC):
                    last = three_products(
                        pe, ps[j % 4][:, :],
                        [ctxs[:, c, l, bass.ds(i * (2 * P) + (j // 2) * P, P)] for l in range(2)],
                        [wkvs[:, 1 + j % 2, l, c * GW:(c + 1) * GW] for l in range(2)], c == 0, c == KC - 1)
                return last

            def q_project(i, j):
                s, t = divmod(j, NT)
                if t == 0:
                    pe.wait_ge(s_wql, 4 * (2 * i + s + 1))
                for c in range(KC):
                    last = three_products(
                        pe, ps[j % 4][:, :],
                        [xT[:, t, l, c * P:(c + 1) * P] for l in range(2)],
                        [wsp[:, s, l, c * GW:(c + 1) * GW] for l in range(2)], c == 0, c == KC - 1)
                return last

            v_rows(0, 0)
            v_rows(0, 1)

            def up(e, s, which=(0, 1)):
                pe.wait_ge(s_w12l, e + 1)
                for u in which:
                    for c in range(KC):
                        at = (u * KC + c) * INTER
                        last = three_products(
                            pe, ps[4 + 2 * s + u][:, :],
                            [wsp[:, s, l, at:at + INTER] for l in range(2)],
                            [xT[:, :, l, c * P:(c + 1) * P] for l in range(2)], c == 0, c == KC - 1)
                    last.then_inc(s_up, 1)

            def down(e, s, last_expert=False):
                pe.wait_ge(s_w3l, e + 1)
                pe.wait_ge(s_hl, e + 1)
                for t in range(NT):
                    last = three_products(
                        pe, ps[t][:, :], [hlr[:, s, l, t * P:(t + 1) * P] for l in range(2)],
                        [wsp[:, s, l, 2 * KC * INTER:EG] for l in range(2)], False, last_expert)
                last.then_inc(s_dn, 1)

            def first_expert():
                pe.wait_ge(s_gate, 1)
                for t in range(NT):
                    last = pe.transpose(ps[5][0:NE, t * P:(t + 1) * P], gt[:, t, :], identf)
                last.then_inc(s_gT, 1)
                up(0, 0, (0,))

            pe.wait_ge(s_id, 4)
            pe.wait_ge(s_vfree, 6)
            for t in range(NT):
                pe.wait_ge(s_xq, t + 1)
                for c in range(KC):
                    last = pe.transpose(ps[4 + t // 2][:, :].bitcast(F16)[:, (t % 2) * D + c * P:(t % 2) * D + (c + 1) * P],
                                        hlr[:, t, 0, c * P:(c + 1) * P], ident[:, :])
                last.then_inc(s_xqT, 1)
            pe.wait_ge(s_vfree, NST)
            for b in range(BATCH):
                pe.wait_ge(s_cq, b + 1)
                for c in range(KC):
                    last = pe.matmul(ps[6 + b][:, :], ones128, cq[:, (b * KC + c) * D:(b * KC + c + 1) * D],
                                     start=(c == 0), stop=(c == KC - 1))
                last.then_inc(s_sums, 1)
            pe.wait_ge(s_xqTc, 2)
            for t in range(NT):
                for c in range(KC):
                    last = pe.matmul(ps[4][:, t:t + 1], xqT[:, t, c, :], ones[:, :], start=(c == 0), stop=(c == KC - 1))
            last.then_inc(s_sums, 1)
            for t in range(NT):
                for c in range(KC):
                    last = pe.matmul(ps[t][:, :], xqT[:, t, c, :],
                                     cq[:, ((t // 2) * KC + c) * D:((t // 2) * KC + c + 1) * D],
                                     start=(c == 0), stop=(c == KC - 1))
                last.then_inc(s_main, 1)

            pe.wait_ge(s_vfree, NST + 4)
            v_rows(1, 0)
            ln_transposes(0)

            pe.wait_ge(s_lnTc, NT)
            pe.wait_ge(s_rws, 1)
            pe.wait_ge(s_vfree, NST + 8)
            for t in range(NT):
                for c in range(KC):
                    last = three_products(
                        pe, ps[4][:, t * E_ROUTED:(t + 1) * E_ROUTED],
                        [xT[:, t, l, c * P:(c + 1) * P] for l in range(2)],
                        [rws[:, l, c * E_ROUTED:(c + 1) * E_ROUTED] for l in range(2)], c == 0, c == KC - 1)
                if t == 0:
                    last.then_inc(s_tr, 4)
                if t == 1:
                    last.then_inc(s_trc, 2)
            last.then_inc(s_rt, 1)

            pe.wait_ge(s_wlo, 4)
            rms_phase(0, 4, 4, k_project, block_major, first_expert)

            pe.wait_ge(s_gTc, 1)
            up(0, 0, (1,))
            pe.wait_ge(s_b3, 16)
            for t in range(NT):
                pe.matmul(ps[t][:, :], gateT[0:E_ROUTED + 1, t * P:(t + 1) * P], b3s[0:E_ROUTED + 1, :],
                          start=True, stop=False, skip_group_check=True)
            pe.wait_ge(s_trc, 2 + 16)
            up(1, 1)
            down(0, 0)
            pe.wait_ge(s_hx, 1)
            up(2, 0)
            down(1, 1)
            with pe.Fori(1, NE // 2 - 1) as i:
                pe.wait_ge(s_hx, 2 * i)
                up(2 * i + 1, 1)
                down(2 * i, 0)
                pe.wait_ge(s_hx, 2 * i + 1)
                up(2 * i + 2, 0)
                down(2 * i + 1, 1)
            pe.wait_ge(s_hx, NE - 2)
            up(NE - 1, 1)
            down(NE - 2, 0)
            down(NE - 1, 1, True)

            pe.wait_ge(s_hx, NE)
            v_rows(1, 1)
            ln_transposes(1)

            pe.wait_ge(s_lnTc, 2 * NT)
            pe.wait_ge(s_vfree, 4 + 2 * NST)
            rms_phase(16, 4, 2 * NT, q_project, hi_lo_major)

            def scores(g, j, k, first):
                m, hh = divmod(j, REP)
                if not first or j >= 4:
                    pe.wait_ge(s_t, k - 3)
                b = m // QT_PER_B
                three_products(
                    pe, ps[j % 4][:, :],
                    [q_sb[:, bass.ds(4 * g + m, 1), l, hh * P:(hh + 1) * P] for l in range(2)],
                    [k_sb[:, bass.ds(g, 1), l, b * CTX:(b + 1) * CTX] for l in range(2)], True, True).then_inc(s_s, 1)

            def prob_transposes(j, k, wait_bank=True):
                pe.wait_ge(s_pl, k + 1)
                if wait_bank:
                    pe.wait_ge(s_Tc, k - 1)
                transposes(hlr[:, j % 4, :, :], ps[4 + j % 2][:, :], hi_lo_major).then_inc(s_T, 1)

            def values(w, gw, mw, c, wait_bank=True):
                if c == 0:
                    pe.wait_ge(s_Tc, 4 * w + 4)
                    if wait_bank:
                        pe.wait_ge(s_ol, w - 1)
                par = mw % 2
                last = three_products(
                    pe, ps[6 + par][:, :],
                    [v_sb[:, (mw // QT_PER_B) * SC + c, l, bass.ds(gw * HD, HD)] for l in range(2)],
                    [pT[par][:, :, l, c * P:(c + 1) * P] for l in range(2)], c == 0, c == SC - 1)
                if c == SC - 1:
                    last.then_inc(s_pv, 1)

            def attention(g, first):
                for j in range(4 * REP):
                    k = 16 * g + j
                    m, c = divmod(j, REP)
                    scores(g, j, k, first)
                    if not first or j >= 4:
                        prob_transposes(j, k - 4, not first or j >= 6)
                    if not first or m >= 2:
                        values(4 * g + m - 2, g if m >= 2 else g - 1, (m - 2) % 4, c, not first)

            attention(0, True)
            with pe.Fori(1, KVH) as g:
                attention(g, False)
            for j in range(4):
                prob_transposes(j, 16 * KVH - 4 + j)
                values(4 * KVH - 2, KVH - 1, 2, j)
            for c in range(SC):
                values(4 * KVH - 1, KVH - 1, 3, c)

            def o_group(g, s, first, last_group):
                pe.wait_ge(s_wql, 4 * (KVH + 1) + 4 * g)
                for c in range(REP):
                    for t in range(NT):
                        last = three_products(
                            pe, ps[t][:, :],
                            [q_sb[:, bass.ds(4 * g + t, 1), l, c * P:(c + 1) * P] for l in range(2)],
                            [wsp[:, s, l, c * GW:(c + 1) * GW] for l in range(2)],
                            first and c == 0, last_group and c == REP - 1)
                last.then_inc(s_od, 1)

            pe.wait_ge(s_ol, 4 * KVH)
            for s in range(2):
                o_group(s, s, s == 0, False)
            with pe.Fori(1, KVH // 2 - 1) as i:
                for s in range(2):
                    o_group(2 * i + s, s, False, False)
            for s in range(2):
                o_group(KVH - 2 + s, s, False, s == 1)
            ln_transposes(2)

            pe.wait_ge(s_lnTc, 3 * NT)
            pe.wait_ge(s_lwl, 1)
            for c in range(KC):
                last = three_products(
                    pe, ps[4][0:RD, :], [lwqs[:, l, c * RD:(c + 1) * RD] for l in range(2)],
                    [xT[:, :, l, c * P:(c + 1) * P] for l in range(2)], c == 0, c == KC - 1)
            last.then_inc(s_lq, 1)
            pe.wait_ge(s_wql, 4 * (2 * KVH + 1))
            for t in range(NT):
                for c in range(KC):
                    last = three_products(
                        pe, ps[t][:, :], [xT[:, t, l, c * P:(c + 1) * P] for l in range(2)],
                        [wsp[:, 0, l, c * GW:(c + 1) * GW] for l in range(2)], c == 0, c == KC - 1)
                last.then_inc(s_z, 1)
                if t == 0:
                    pe.wait_ge(s_lqs, 1)
                    for u in range(NT):
                        last = three_products(
                            pe, ps[5][:, u * L_EXP:(u + 1) * L_EXP],
                            [lqs[:, l, u * P:(u + 1) * P] for l in range(2)],
                            [lkys[:, l, :] for l in range(2)], True, True)
                    last.then_inc(s_lsc, 1)
            for t in range(NT):
                pe.wait_ge(s_zl, t + 1)
                if t >= 2:
                    pe.wait_ge(s_zTc, t - 1)
                transposes(hlr[:, t, :, :], ps[6 + t % 2][:, :], hi_lo_major).then_inc(s_zT, 1)
            pe.wait_ge(s_wql, 4 * (2 * KVH + 2))
            for t in range(NT):
                pe.wait_ge(s_zTc, t + 1)
                for c in range(KC):
                    last = three_products(
                        pe, ps[t][:, :], [zT[:, t, l, c * P:(c + 1) * P] for l in range(2)],
                        [wsp[:, 1, l, c * GW:(c + 1) * GW] for l in range(2)], c == 0, c == KC - 1)
                last.then_inc(s_y, 1)

        @block.scalar
        def _(act):
            act.wait_ge(s_ctx[0], 16)
            for c in range(KC):
                act.copy(ctxs[:, c, 0, 0:CTX], stage[:, 0, c * CTX:(c + 1) * CTX]).then_inc(s_firsth, 1)
            act.wait_ge(s_kv[0], 16)
            for c in range(KC):
                act.copy(wkvs[:, 0, 0, c * GW:(c + 1) * GW], kv_land[:, 0, c * GW:(c + 1) * GW]).then_inc(s_firsth, 1)
            act.wait_ge(s_ctx[1], 16)
            act.copy(ctxs[:, :, 0, CTX:2 * CTX], stage[:, 1, :].rearrange("p (k s) -> p k s", k=KC)).then_inc(s_whi, 1)
            act.wait_ge(s_par, 16)
            act.copy(rws[:, 0, :], rw).then_inc(s_rwh, 1)

            def group_hi(w):
                act.wait_ge(s_kv[w], 16)
                act.copy(wkvs[:, w, 0, :], kv_land[:, w, :]).then_inc(s_whi, 1)

            def ln_hi(n):
                for t in range(NT):
                    act.wait_ge(s_ln, NT * n + t + 1)
                    act.copy(hlr[:, t, 0, :], f32r[:, t, :]).then_inc(s_lnh, 1)

            def v_hi(hg, tiles):
                for n in tiles:
                    act.wait_ge(s_vp, NST * hg + n + 1)
                    act.copy(v_sb[:, n, 0, hg * GW:(hg + 1) * GW], ps[4 + n % 4][:, :]).then_inc(s_vh, 1)

            def w12_hi(e, s):
                act.wait_ge(s_e12[s], 8 * (e - s) + 16)
                if not (isinstance(e, int) and e < 2):
                    act.wait_ge(s_up, 2 * e - 2)
                act.copy(wsp[:, s, 0, W12], stage[:, s, W12]).then_inc(s_w12h, 1)

            def w3_hi(e, s):
                act.wait_ge(s_e3[s], 8 * (e - s) + 16)
                if not (isinstance(e, int) and e < 2):
                    act.wait_ge(s_dn, e - 1)
                act.copy(wsp[:, s, 0, W3], stage[:, s, W3]).then_inc(s_w3h, 1)

            v_hi(0, (0, 1))
            group_hi(3)
            v_hi(0, (2, 3))
            group_hi(1)
            v_hi(0, (4, 5))
            group_hi(2)
            v_hi(0, (6, 7))
            w12_hi(0, 0)
            w3_hi(0, 0)
            w12_hi(1, 1)
            ln_hi(0)
            v_hi(1, (0, 1, 2, 3))

            act.wait_ge(s_lg, 2)
            act.activation(sml[:, 4:8, :], sml[:, 0:4, :], ACT.Exp).then_inc(s_rex, 1)

            def rms_phase(r0, iters, tiles, scale, bias, copy_out, quarter):
                def squares(r, j, first):
                    act.wait_ge(s_pj, r + 1)
                    if not first or j >= 2:
                        act.wait_ge(s_ss, r - 1)
                    act.activation(f32r[:, j % 2, :], ps[j % 4][:, :], ACT.Square).then_inc(s_sq, 1)

                def roots(r, j, first):
                    act.wait_ge(s_ss, r + 1)
                    if not first or j >= 2:
                        act.wait_ge(s_rr, r - 1)
                    act.activation(root[:, j % 2, :], ss[:, j % 2, :], ACT.Sqrt, bias=bias, scale=scale).then_inc(s_root, 1)

                def hi(r, j, first):
                    act.wait_ge(s_nrm, r + 1)
                    act.wait_ge(s_tr, r + 1)
                    act.copy(hlr[:, j % 4, 0, :], f32r[:, 2 + j % 2, :]).then_inc(s_nh, 1)

                def copied(i, j, r):
                    act.wait_ge(s_tr, r + 5)
                    copy_out(i, j, ps[6 + j % 2][:, :]).then_inc(s_trc, 1)

                def body(i, first):
                    for j in range(tiles):
                        r = r0 + tiles * i + j
                        squares(r, j, first)
                        if not first or j >= 1:
                            roots(r - 1, (j - 1) % tiles, first and j - 1 < 2)
                        if not first or j >= 2:
                            hi(r - 2, (j - 2) % tiles, first and j - 2 < 4)
                        for c in QUARTERS[j % 4]:
                            quarter(i, j // 4, c)
                        if not first or j >= 4:
                            copied(i if j >= 4 else i - 1, (j - 4) % tiles, r - 4)

                body(0, True)
                with act.Fori(1, iters) as i:
                    body(i, False)
                end = tiles * iters
                roots(r0 + end - 1, tiles - 1, False)
                for j in range(2):
                    hi(r0 + end - 2 + j, tiles - 2 + j, False)
                for j in range(4):
                    copied(iters - 1, tiles - 4 + j, r0 + end - 4 + j)

            k_words = words(k_sb[:, :, :, :])

            def k_out(i, j, bank):
                h0 = (j % 2) * 4
                return act.copy(k_words[:, h0:h0 + 4, :, bass.ds(i * P + (j // 2) * (P // 2), P // 2)],
                                bank.rearrange("p (h l w) -> p h l w", h=4, l=2))

            def q_out(i, j, bank):
                return act.copy(words(q_sb[:, bass.ds(2 * NT * i + j, 1), :, :]), bank)

            rms_phase(0, 4, 4, 1.0 / HD, scs[:, 12:13], k_out, lambda i, g, c: None)

            def gate_load(e, s):
                act.dma_start(gate_bc[s], gates_dram[bass.ds(e, 1), :].partition_broadcast(P)
                              .rearrange("q a t -> q (a t)")).then_inc(s_gload[s], 16)

            def silu(e, s):
                act.wait_ge(s_up, 2 * e + 1)
                if not (isinstance(e, int) and e < 2):
                    act.wait_ge(s_hl, e - 1)
                act.activation(f32r[:, s, :], ps[4 + 2 * s][:, :], ACT.Silu, bias=mb[:, 0, bass.ds(e, 1)]).then_inc(s_silu, 1)

            def hidden_hi(e, s):
                act.wait_ge(s_hg, e + 1)
                if not (isinstance(e, int) and e < 2):
                    act.wait_ge(s_dn, e - 1)
                act.copy(hlr[:, s, 0, :], f32r[:, s, :]).then_inc(s_hh, 1)

            def expert(e, s):
                silu(e, s)
                if not (isinstance(e, int) and e + 2 >= NE):
                    w12_hi(e + 2, s)
                hidden_hi(e, s)
                if not (isinstance(e, int) and e + 2 >= NE):
                    gate_load(e + 2, s)
                if not (isinstance(e, int) and e + 1 >= NE):
                    w3_hi(e + 1, 1 - s)

            act.wait_ge(s_gTc, 1)
            act.dma_start(gates_dram, gateT[0:NE, :]).then_inc(s_gst, 16)
            act.wait_ge(s_gst, 16)
            for s in range(2):
                gate_load(s, s)
            for s in range(2):
                expert(s, s)
            with act.Fori(1, NE // 2 - 1) as i:
                for s in range(2):
                    expert(2 * i + s, s)
            for s in range(2):
                expert(NE - 2 + s, s)

            def quarter_hi(slot, c, free=None):
                if free is not None:
                    act.wait_ge(*free)
                act.copy(wsp[:, slot, 0, c * GW:(c + 1) * GW], stage[:, slot, c * GW:(c + 1) * GW]).then_inc(s_wqh, 1)

            act.wait_ge(s_w[0], 16)
            for c in range(4):
                quarter_hi(0, c, (s_dn, NE - 1) if c == 0 else None)
            ln_hi(1)
            v_hi(1, (4, 5, 6, 7))
            act.wait_ge(s_lnT, 2 * NT)

            def q_quarter(i, s, c):
                if c == 0:
                    act.wait_ge(s_w[1 - s], 16 * (1 + s) + 16 * i)
                    act.wait_ge(s_pj, 16 + 8 * i + 4 * s)
                quarter_hi(1 - s, c)

            rms_phase(16, 4, 2 * NT, 1.0 / 64, scs[:, 13:14], q_out, q_quarter)

            def exponentials(j, k):
                act.wait_ge(s_t, k + 1)
                act.activation(f32r[:, j % 4, :], f32r[:, j % 4, :], ACT.Exp, bias=mneg[:, j % 4:j % 4 + 1], scale=-1.0,
                               accum_out=psum_col[:, j % 4:j % 4 + 1]).then_inc(s_e, 1)

            def prob_copy(j, k, u, wait_values):
                act.wait_ge(s_T, k + 1)
                if wait_values:
                    act.wait_ge(s_pv, u - 1)
                act.copy(words(pT[(j // REP) % 2][:, j % REP, :, :]), ps[4 + j % 2][:, :]
                         .rearrange("p (l w) -> p l w", l=2)).then_inc(s_Tc, 1)

            def o_hi(w, mw):
                act.wait_ge(s_pv, w + 1)
                act.activation(q_sb[:, bass.ds(w, 1), 0, :], ps[6 + mw % 2][:, :], ACT.Copy, scale=1.0 / PSCALE).then_inc(s_oh, 1)

            def attention(g, first):
                for j in range(4 * REP):
                    k = 16 * g + j
                    m, hh = divmod(j, REP)
                    exponentials(j, k)
                    if not first or j >= 4:
                        prob_copy((j - 4) % 16, k - 4, 4 * g + m - 1, hh == 0 and (not first or m >= 3))
                    if hh == 0 and (not first or m >= 3):
                        o_hi(4 * g + m - 3, (m - 3) % 4)

            attention(0, True)
            with act.Fori(1, KVH) as g:
                attention(g, False)
            o_hi(4 * KVH - 3, 1)
            for j in range(4):
                prob_copy(12 + j, 16 * KVH - 4 + j, 4 * KVH - 1, j == 0)
            for m in range(2):
                o_hi(4 * KVH - 2 + m, m)

            for c in range(4):
                act.wait_ge(s_w[1], 16 * (KVH // 2 + 1))
                quarter_hi(1, c)
            with act.Fori(0, KVH // 2 - 1) as i:
                for s in range(2):
                    act.wait_ge(s_w[s], 16 * (KVH // 2 + 2) + 16 * i)
                    act.wait_ge(s_od, 2 * i + s + 1)
                    for c in range(4):
                        quarter_hi(s, c)
            for s in range(2):
                act.wait_ge(s_w[s], 16 * (KVH + 1))
                act.wait_ge(s_od, KVH - 1 + s)
                for c in range(4):
                    quarter_hi(s, c)
            for dst, src in ((lwq, l_wq), (lky, l_keys)):
                act.dma_start(dst, src).then_inc(s_late, 16)
            act.wait_ge(s_late, 32)
            act.copy(lwqs[:, 0, :], lwq.rearrange("p k r -> p (k r)")).then_inc(s_lw, 1)
            act.copy(lkys[:, 0, :], lky).then_inc(s_lw, 1)
            ln_hi(2)

            act.wait_ge(s_lq, 1)
            act.copy(lqs[:, 0, :], ps[4][0:RD, :]).then_inc(s_lqh, 1)
            for t in range(NT):
                act.wait_ge(s_lng, t + 1)
                act.activation(lex[:, t, :], lsc[:, t, :], ACT.Exp, bias=lng[:, t:t + 1]).then_inc(s_lex, 1)
            for t in range(NT):
                act.wait_ge(s_zg, t + 1)
                act.copy(hlr[:, t, 0, :], f32r[:, t, :]).then_inc(s_zh, 1)

        @block.gpsimd
        def _(pool):
            pool.memset(ident[:, :], 0.0).then_inc(s_id, 1)
            pool.memset(lower[:, :, :], 1.0).then_inc(s_id, 1)
            pool.wait_ge(s_id, 2)
            pool.affine_select(out=ident[:, :], in_=ident[:, :], compare_op=ALU.not_equal, fill=1.0, base=0,
                               pattern=[[-1, P]], channel_multiplier=1).then_inc(s_id, 1)
            pool.affine_select(out=lower[:, :, :], in_=lower[:, :, :], compare_op=ALU.is_gt, fill=0.0, base=0,
                               pattern=[[1, E_ROUTED], [-1, E_ROUTED]], channel_multiplier=0).then_inc(s_id, 1)

            def low(dst_lo, src, dst_hi):
                return pool.tensor_tensor(dst_lo, src, dst_hi, ALU.subtract)

            for c in range(2, KC):
                pool.wait_ge(s_firsth, 5 + c)
                at = slice(c * GW, (c + 1) * GW)
                low(wkvs[:, 0, 1, at], kv_land[:, 0, at], wkvs[:, 0, 0, at]).then_inc(s_v0l, 1)
            pool.wait_ge(s_whi, 1)
            low(ctxs[:, :, 1, CTX:2 * CTX], stage[:, 1, :].rearrange("p (k s) -> p k s", k=KC),
                ctxs[:, :, 0, CTX:2 * CTX]).then_inc(s_wlo, 1)
            for n, w in enumerate((3, 1, 2)):
                pool.wait_ge(s_whi, n + 2)
                low(wkvs[:, w, 1, :], kv_land[:, w, :], wkvs[:, w, 0, :]).then_inc(s_wlo, 1)

            def w12_lo(e, s):
                pool.wait_ge(s_w12h, e + 1)
                low(wsp[:, s, 1, W12], stage[:, s, W12], wsp[:, s, 0, W12]).then_inc(s_w12l, 1)

            def w3_lo(e, s):
                pool.wait_ge(s_w3h, e + 1)
                low(wsp[:, s, 1, W3], stage[:, s, W3], wsp[:, s, 0, W3]).then_inc(s_w3l, 1)

            w12_lo(0, 0)
            w3_lo(0, 0)
            w12_lo(1, 1)

            def rms_phase(r0, iters, tiles, quarter):
                def tile_low(r, j):
                    pool.wait_ge(s_nh, r + 1)
                    low(hlr[:, j % 4, 1, :], f32r[:, 2 + j % 2, :], hlr[:, j % 4, 0, :]).then_inc(s_nl, 1)

                def body(i, first):
                    for j in range(tiles):
                        if not first or j >= 2:
                            tile_low(r0 + tiles * i + j - 2, (j - 2) % tiles)
                        for c in QUARTERS[j % 4]:
                            quarter(i, j // 4, c)

                body(0, True)
                with pool.Fori(1, iters) as i:
                    body(i, False)
                for j in range(2):
                    tile_low(r0 + tiles * iters - 2 + j, tiles - 2 + j)

            rms_phase(0, 4, 4, lambda i, g, c: None)

            with pool.Fori(0, NE // 2 - 1) as i:
                for s in range(2):
                    w12_lo(2 * i + s + 2, s)
                    w3_lo(2 * i + s + 1, 1 - s)
            w3_lo(NE - 1, 1)

            def quarter_lo(slot, c, q):
                pool.wait_ge(s_wqh, q + 1)
                at = slice(c * GW, (c + 1) * GW)
                low(wsp[:, slot, 1, at], stage[:, slot, at], wsp[:, slot, 0, at]).then_inc(s_wql, 1)

            for c in range(4):
                quarter_lo(0, c, c)
            rms_phase(16, 4, 2 * NT, lambda i, s, c: quarter_lo(1 - s, c, 8 * i + 4 + 4 * s + c))

            def prob_hi(j, k, first):
                summed, freed = k + 1, k - 3
                if not first:
                    summed, freed = pool.to_reg(summed), pool.to_reg(freed)
                pool.wait_ge(s_nl, 16 + NT * KVH)
                pool.wait_ge(s_r, summed)
                if not first:
                    pool.wait_ge(s_T, freed)
                pool.tensor_scalar(hlr[:, j % 4, 0, :], f32r[:, j % 4, :], rinv[:, 1, j % 4:j % 4 + 1], 1.0,
                                   ALU.mult, ALU.mult).then_inc(s_ph, 1)

            for j in range(4):
                prob_hi(j, j, True)
            with pool.Fori(1, 4 * KVH) as u:
                for j in range(4):
                    prob_hi(j, 4 * u + j, False)

            for c in range(4):
                quarter_lo(1, c, 4 * (KVH + 1) + c)
            with pool.Fori(0, KVH // 2 - 1) as i:
                for s in range(2):
                    for c in range(4):
                        quarter_lo(s, c, 4 * (KVH + 2) + 8 * i + 4 * s + c)
            for s in range(2):
                for c in range(4):
                    quarter_lo(s, c, 4 * (2 * KVH + s) + c)

        @block.vector
        def _(dve):
            linked = [0]

            def link(ins):
                ins.then_inc(s_dve, 1)
                linked[0] += 1
                dve.wait_ge(s_dve, linked[0])

            def spread(ap, n):
                return ap.unsqueeze(len(ap.shape)).to_broadcast(list(ap.shape) + [n])

            def layer_norm():
                for t in range(NT):
                    last = dve.bn_stats(st6[:, t, :], x_sb[:, t, :])
                link(last)
                for t in range(NT):
                    last = dve.bn_aggr(mv[:, t, :], st6[:, t, :])
                link(last)
                var, y, tmp = nw[:, 0, :], nw[:, 1, :], nw[:, 2, :]
                link(dve.tensor_scalar(var, mv[:, :, 1], EPS, None, ALU.add))
                link(dve.tensor_scalar(y.bitcast(I32), var.bitcast(I32), 1, None, ALU.arith_shift_right))
                link(dve.tensor_scalar(y.bitcast(I32), y.bitcast(I32), -1.0, RSQRT_MAGIC, ALU.mult, ALU.add))
                for _ in range(3):
                    link(dve.scalar_tensor_tensor(out=tmp, in0=y, scalar=-0.5, in1=y, op0=ALU.mult, op1=ALU.mult))
                    link(dve.tensor_tensor(tmp, tmp, var, ALU.mult))
                    link(dve.scalar_tensor_tensor(out=y, in0=tmp, scalar=1.5, in1=y, op0=ALU.add, op1=ALU.mult))

            def normalise(t):
                return dve.tensor_scalar(f32r[:, t, :], x_sb[:, t, :], mv[:, t, 0:1], nw[:, 1, t:t + 1],
                                         ALU.subtract, ALU.mult)

            for c in range(KC):
                dve.wait_ge(s_firsth, c + 1)
                dve.tensor_tensor(ctxs[:, c, 1, 0:CTX], stage[:, 0, c * CTX:(c + 1) * CTX], ctxs[:, c, 0, 0:CTX],
                                  ALU.subtract).then_inc(s_firstl, 1)
            for c in range(2):
                dve.wait_ge(s_firsth, 5 + c)
                at = slice(c * GW, (c + 1) * GW)
                dve.tensor_tensor(wkvs[:, 0, 1, at], kv_land[:, 0, at], wkvs[:, 0, 0, at], ALU.subtract).then_inc(s_firstl, 1)

            dve.wait_ge(s_par, 16)
            for c in (0, 2):
                last = dve.reciprocal(scs[:, 4 + c // 2:5 + c // 2], scs[:, c:c + 1])
            dve.tensor_tensor(scs[:, 6:7], scs[:, 0:1], scs[:, 2:3], ALU.mult)
            for c in (1, 3):
                dve.tensor_scalar(scs[:, 7 + c // 2:8 + c // 2], scs[:, c:c + 1], -1.0, MID, ALU.mult, ALU.add)
            dve.memset(scs[:, 12:13], EPS)
            dve.memset(scs[:, 13:14], 2 * EPS)
            dve.memset(ones[:, :], 1.0)
            dve.memset(ones128, 1.0)
            for t in range(NT):
                dve.memset(gt[:, t, E_ROUTED:NE], 1.0)
            link(dve.scalar_tensor_tensor(out=wneg, in0=wneg, scalar=-1.0, in1=identf,
                                          op0=ALU.mult, op1=ALU.mult))
            dve.wait_ge(s_id, 4)
            dve.tensor_copy(identf, ident[:, :])
            for c in range(2):
                last = dve.tensor_tensor(scs[:, 9 + c:10 + c], scs[:, 6:7], scs[:, 7 + c:8 + c], ALU.mult)
            link(last)
            link(dve.scalar_tensor_tensor(out=scs[:, 11:12], in0=scs[:, 9:10], scalar=float(D), in1=scs[:, 8:9],
                                          op0=ALU.mult, op1=ALU.mult))
            dve.wait_ge(s_rwh, 1)
            dve.tensor_tensor(rws[:, 1, :], rw, rws[:, 0, :], ALU.subtract).then_inc(s_rws, 1)

            def v_lo(hg, tiles):
                at = slice(hg * GW, (hg + 1) * GW)
                for n in tiles:
                    dve.wait_ge(s_vh, NST * hg + n + 1)
                    dve.tensor_tensor(v_sb[:, n, 1, at], ps[4 + n % 4][:, :], v_sb[:, n, 0, at],
                                      ALU.subtract).then_inc(s_vfree, 1)

            dve.wait_ge(s_x, 16)
            layer_norm()
            for t in range(NT):
                last = normalise(t)
            v_lo(0, (0, 1))
            link(last)
            for t in range(NT):
                last = dve.tensor_scalar(f32r[:, t, :], f32r[:, t, :], scs[:, 4:5], scs[:, 1:2], ALU.mult, ALU.add)
            link(last)
            for t in range(NT):
                last = dve.tensor_scalar(f32r[:, t, :], f32r[:, t, :], 0.0, QMAX, ALU.max, ALU.min)
            link(last)
            for t in range(NT):
                dve.tensor_scalar(hlr[:, t, 0, :], f32r[:, t, :], ROUND, ROUND + MID, ALU.add, ALU.subtract).then_inc(s_xq, 1)
            v_lo(0, (2, 3))
            dve.wait_ge(s_cn, 16)
            half = KC * D
            for b in range(BATCH):
                c32 = cnat[:, b * half:(b + 1) * half]
                link(dve.tensor_scalar(c32, c32, scs[:, 5:6], scs[:, 3:4], ALU.mult, ALU.add))
                link(dve.tensor_scalar(c32, c32, 0.0, QMAX, ALU.max, ALU.min))
                dve.tensor_scalar(cq[:, b * half:(b + 1) * half], c32, ROUND, ROUND + MID, ALU.add, ALU.subtract)\
                   .then_inc(s_cq, 1)
                v_lo(0, (4 + 2 * b, 5 + 2 * b))
            dve.wait_ge(s_xqT, NT)
            for b in range(2):
                dve.tensor_copy(words(pT1[:, b, :, :]), ps[4 + b][:, :].rearrange("p (l w) -> p l w", l=2)).then_inc(s_xqTc, 1)
            dve.wait_ge(s_sums, BATCH + 1)
            dve.tensor_scalar(nw[:, 3, :], ps[4][:, 0:NT], scs[:, 10:11], scs[:, 11:12], ALU.mult, ALU.add)
            for b in range(BATCH):
                last = dve.tensor_scalar(f32r[:, b, :], ps[6 + b][:, :], scs[:, 9:10], None, ALU.mult)
            linked[0] += 1
            last.then_inc(s_dve, 1)
            dve.wait_ge(s_dve, linked[0])
            for t in range(NT):
                last = dve.scalar_tensor_tensor(out=x_sb[:, t, :], in0=x_sb[:, t, :], scalar=nw[:, 3, t:t + 1],
                                                in1=f32r[:, t // 2, :], op0=ALU.add, op1=ALU.add)
            last.then_inc(s_vfree, 4)
            for t in range(NT):
                dve.wait_ge(s_main, t + 1)
                if t == 0:
                    dve.wait_ge(s_vfree, NST + 4)
                last = dve.scalar_tensor_tensor(out=x_sb[:, t, :], in0=ps[t][:, :], scalar=scs[:, 6:7],
                                                in1=x_sb[:, t, :], op0=ALU.mult, op1=ALU.add)
            link(last)

            def ln_split(n):
                layer_norm()
                for t in range(NT):
                    normalise(t).then_inc(s_ln, 1)
                for t in range(NT):
                    dve.wait_ge(s_lnh, NT * n + t + 1)
                    dve.tensor_tensor(hlr[:, t, 1, :], f32r[:, t, :], hlr[:, t, 0, :], ALU.subtract).then_inc(s_lnl, 1)

            def ln_copies(n):
                for t in range(NT):
                    dve.wait_ge(s_lnT, NT * n + t + 1)
                    dve.tensor_copy(words(xT[:, t, :, :]), ps[t][:, :].rearrange("p (l w) -> p l w", l=2)).then_inc(s_lnTc, 1)

            ln_split(0)
            v_lo(1, (0, 1, 2, 3))
            ln_copies(0)

            lg, ex = sml[:, 0:4, :], sml[:, 4:8, :]
            dve.wait_ge(s_rt, 1)
            link(dve.tensor_tensor(lg, ps[4][:, 0:NT * E_ROUTED].rearrange("p (t e) -> p t e", t=NT),
                                   rb[:, 0, :].rearrange("p (t e) -> p t e", t=NT), ALU.add))
            link(dve.tensor_reduce(rstat[:, 0, :], lg, AX_X, ALU.max))
            dve.tensor_tensor(lg, lg, spread(rstat[:, 0, :], E_ROUTED), ALU.subtract).then_inc(s_lg, 2)
            dve.wait_ge(s_rex, 1)
            link(dve.tensor_reduce(rstat[:, 1, :], ex, AX_X, ALU.add))
            link(dve.reciprocal(rstat[:, 2, :], rstat[:, 1, :]))
            link(dve.tensor_tensor(ex, ex, spread(rstat[:, 2, :], E_ROUTED), ALU.mult))
            link(dve.tensor_tensor(ex, ex, rb[:, 1, :].rearrange("p (t e) -> p t e", t=NT), ALU.add))

            def ranks(vals, n, dst):
                gt_, eq_ = (c[:, 0:NT * n * n].rearrange("p (t i j) -> p t i j", t=NT, i=n) for c in (cmp_gt, cmp_eq))
                other = vals.unsqueeze(2).to_broadcast([P, NT, n, n])
                own = spread(vals, n)
                below = lower[:, 0:n, 0:n].unsqueeze(1).to_broadcast([P, NT, n, n])
                dve.tensor_tensor(gt_, other, own, ALU.is_gt)
                link(dve.tensor_tensor(eq_, other, own, ALU.is_equal))
                link(dve.tensor_tensor(eq_, eq_, below, ALU.mult))
                link(dve.tensor_tensor(gt_, gt_, eq_, ALU.add))
                link(dve.tensor_reduce(dst, gt_, AX_X, ALU.add))

            gmax = lg[:, :, 0:GROUPS]
            grank = lg[:, :, GROUPS:2 * GROUPS]
            masked = lg[:, :, :]
            link(dve.tensor_reduce(gmax, ex.rearrange("p t (g e) -> p t g e", g=GROUPS), AX_X, ALU.max))
            ranks(gmax, GROUPS, grank)
            link(dve.tensor_scalar(rstat[:, :, :], grank, float(TOPG), -BIG, ALU.is_ge, ALU.mult))
            link(dve.tensor_tensor(masked.rearrange("p t (g e) -> p t g e", g=GROUPS), ex.rearrange("p t (g e) -> p t g e", g=GROUPS),
                                   spread(rstat[:, :, :], EPG), ALU.add))
            ranks(masked, E_ROUTED, rb[:, 0, :].rearrange("p (t e) -> p t e", t=NT))
            dve.scalar_tensor_tensor(out=gt[:, :, 0:E_ROUTED], in0=rb[:, 0, :].rearrange("p (t e) -> p t e", t=NT),
                                     scalar=float(TOPE), in1=ex, op0=ALU.is_lt, op1=ALU.mult).then_inc(s_gate, 1)
            dve.wait_ge(s_mask, 16)
            dve.tensor_scalar(nmask[:, :, :], nmask[:, :, :], -8.0, None, ALU.mult)

            def rms_phase(r0, iters, tiles, weighted):
                def sums(r, j, first):
                    dve.wait_ge(s_sq, r + 1)
                    if not first or j >= 2:
                        dve.wait_ge(s_root, r - 1)
                    dve.tensor_reduce(ss[:, j % 2, :], f32r[:, j % 2, :].rearrange("p (h d) -> p h d", h=REP),
                                      AX_X, ALU.add).then_inc(s_ss, 1)

                def normed(r, j, first):
                    dve.wait_ge(s_root, r + 1)
                    dve.reciprocal(rrt[:, j % 2, :], root[:, j % 2, :]).then_inc(s_rr, 1)
                    dve.wait_ge(s_rr, r + 1)
                    if not first or j >= 2:
                        dve.wait_ge(s_nl, r - 1)
                    dst, bank = f32r[:, 2 + j % 2, :], ps[j % 4]
                    if weighted:
                        for h in range(REP):
                            at = slice(h * HD, (h + 1) * HD)
                            last = dve.scalar_tensor_tensor(out=dst[:, at], in0=bank[:, at], scalar=rrt[:, j % 2, h:h + 1],
                                                            in1=wneg, op0=ALU.mult, op1=ALU.mult)
                    else:
                        last = dve.tensor_tensor(dst.rearrange("p (h d) -> p h d", h=REP),
                                                 bank[:, :].rearrange("p (h d) -> p h d", h=REP),
                                                 spread(rrt[:, j % 2, :], HD), ALU.mult)
                    last.then_inc(s_nrm, 1)

                def body(i, first):
                    for j in range(tiles):
                        r = r0 + tiles * i + j
                        sums(r, j, first)
                        if not first or j >= 1:
                            normed(r - 1, (j - 1) % tiles, first and j - 1 < 2)

                body(0, True)
                with dve.Fori(1, iters) as i:
                    body(i, False)
                normed(r0 + tiles * iters - 1, tiles - 1, False)

            rms_phase(0, 4, 4, True)

            dve.wait_ge(s_gT, 1)
            dve.tensor_copy(gateT[0:NE, :], ps[5][0:NE, :]).then_inc(s_gTc, 1)

            def expert(e, s):
                tile, bank = f32r[:, s, :], ps[5 + 2 * s]
                dve.wait_ge(s_silu, e + 1)
                dve.wait_ge(s_up, 2 * e + 2)
                dve.scalar_tensor_tensor(out=tile, in0=bank[:, :], scalar=mb[:, 1, bass.ds(e, 1)], in1=tile,
                                         op0=ALU.add, op1=ALU.mult).then_inc(s_hx, 1)
                dve.wait_ge(s_hx, e + 1)
                dve.wait_ge(s_gload[s], 8 * (e - s) + 16)
                dve.tensor_tensor(tile, tile, gate_bc[s], ALU.mult).then_inc(s_hg, 1)
                dve.wait_ge(s_hh, e + 1)
                dve.tensor_tensor(hlr[:, s, 1, :], tile, hlr[:, s, 0, :], ALU.subtract).then_inc(s_hl, 1)

            with dve.Fori(0, NE // 2) as i:
                for s in range(2):
                    expert(2 * i + s, s)
            dve.wait_ge(s_dn, NE)
            for t in range(NT):
                last = dve.tensor_tensor(x_sb[:, t, :], ps[t][:, :], x_sb[:, t, :], ALU.add)
            link(last)
            ln_split(1)
            v_lo(1, (4, 5, 6, 7))
            ln_copies(1)
            rms_phase(16, 4, 2 * NT, False)

            def masked_scores(j, k, qt, first):
                scored, freed = k + 1, k - 3
                if not first:
                    scored, freed = dve.to_reg(scored), dve.to_reg(freed)
                dve.wait_ge(s_mask, 16)
                dve.wait_ge(s_s, scored)
                if not first or j >= 4:
                    dve.wait_ge(s_pl, freed)
                dve.tensor_tensor_reduce(f32r[:, j % 4, :], ps[j % 4][:, :], nmask[:, qt, :], 0.125, BIG,
                                         ALU.add, ALU.min, mneg[:, j % 4:j % 4 + 1]).then_inc(s_t, 1)

            def inverse_sum(j, k):
                dve.wait_ge(s_e, k + 1)
                dve.reciprocal(rinv[:, 0, j % 4:j % 4 + 1], psum_col[:, j % 4:j % 4 + 1]).then_inc(s_r0, 1)

            def scaled_inverse(j, k):
                dve.wait_ge(s_r0, k + 1)
                dve.tensor_scalar(rinv[:, 1, j % 4:j % 4 + 1], rinv[:, 0, j % 4:j % 4 + 1], PSCALE, None,
                                  ALU.mult).then_inc(s_r, 1)

            def prob_lo(j, k):
                dve.wait_ge(s_ph, k + 1)
                dve.scalar_tensor_tensor(out=hlr[:, j % 4, 1, :], in0=f32r[:, j % 4, :], scalar=rinv[:, 1, j % 4:j % 4 + 1],
                                         in1=hlr[:, j % 4, 0, :], op0=ALU.mult, op1=ALU.subtract).then_inc(s_pl, 1)

            def o_lo(w, mw):
                dve.wait_ge(s_oh, w + 1)
                dve.scalar_tensor_tensor(out=q_sb[:, bass.ds(w, 1), 1, :], in0=ps[6 + mw % 2][:, :], scalar=1.0 / PSCALE,
                                         in1=q_sb[:, bass.ds(w, 1), 0, :], op0=ALU.mult, op1=ALU.subtract).then_inc(s_ol, 1)

            def attention(g, first):
                for j in range(4 * REP):
                    k = 16 * g + j
                    m, hh = divmod(j, REP)
                    masked_scores(j, k, m % QT_PER_B, first)
                    if not first or j >= 1:
                        inverse_sum((j - 1) % 4, k - 1)
                    if not first or j >= 2:
                        prob_lo((j - 2) % 4, k - 2)
                    if not first or j >= 1:
                        scaled_inverse((j - 1) % 4, k - 1)
                    if hh == 1 and (not first or m >= 3):
                        o_lo(4 * g + m - 3, (m - 3) % 4)

            attention(0, True)
            with dve.Fori(1, KVH) as g:
                attention(g, False)
            end = 16 * KVH
            inverse_sum(3, end - 1)
            prob_lo(2, end - 2)
            scaled_inverse(3, end - 1)
            prob_lo(3, end - 1)
            for m in range(3):
                o_lo(4 * KVH - 3 + m, (m + 1) % 4)

            dve.wait_ge(s_od, KVH)
            for t in range(NT):
                last = dve.tensor_tensor(x_sb[:, t, :], ps[t][:, :], x_sb[:, t, :], ALU.add)
            link(last)
            ln_split(2)
            ln_copies(2)

            dve.wait_ge(s_lw, 2)
            dve.tensor_tensor(lwqs[:, 1, :], lwq.rearrange("p k r -> p (k r)"), lwqs[:, 0, :], ALU.subtract)
            dve.tensor_tensor(lkys[:, 1, :], lky, lkys[:, 0, :], ALU.subtract).then_inc(s_lwl, 1)
            dve.wait_ge(s_lqh, 1)
            dve.tensor_tensor(lqs[:, 1, :], ps[4][0:RD, :], lqs[:, 0, :], ALU.subtract).then_inc(s_lqs, 1)
            dve.wait_ge(s_lsc, 1)
            link(dve.tensor_copy(lsc, ps[5][:, 0:NT * L_EXP].rearrange("p (t e) -> p t e", t=NT)))
            for t in range(NT):
                last = dve.max(lm8[:, t, 0, :], lsc[:, t, :])
            link(last)
            for t in range(NT):
                dve.match_replace(lw1[:, t, :], lm8[:, t, 0, :], lsc[:, t, :], -BIG)
                last = dve.tensor_scalar(lng[:, t:t + 1], lm8[:, t, 0, 0:1], -1.0, None, ALU.mult)
                last.then_inc(s_lng, 1)
            dve.wait_ge(s_lng, NT)
            for t in range(NT):
                last = dve.max(lm8[:, t, 1, :], lw1[:, t, :])
            link(last)
            for t in range(NT):
                last = dve.match_replace(lw2[:, t, :], lm8[:, t, 1, :], lw1[:, t, :], -BIG)
            link(last)
            link(dve.tensor_tensor(lw2, lw2, lsc, ALU.not_equal))
            dve.wait_ge(s_lex, NT)
            link(dve.tensor_tensor(lex, lex, lw2, ALU.mult))
            link(dve.tensor_reduce(lsum[:, 0:NT], lex, AX_X, ALU.add))
            link(dve.reciprocal(lsum[:, NT:2 * NT], lsum[:, 0:NT]))
            link(dve.tensor_tensor(lex, lex, spread(lsum[:, NT:2 * NT], L_EXP), ALU.mult))
            for t in range(NT):
                dve.wait_ge(s_z, t + 1)
                dve.tensor_tensor(f32r[:, t, :].rearrange("p (e r) -> p e r", r=RANK),
                                  ps[t][:, :].rearrange("p (e r) -> p e r", r=RANK),
                                  spread(lex[:, t, :], RANK), ALU.mult).then_inc(s_zg, 1)
            for t in range(NT):
                dve.wait_ge(s_zh, t + 1)
                dve.tensor_tensor(hlr[:, t, 1, :], f32r[:, t, :], hlr[:, t, 0, :], ALU.subtract).then_inc(s_zl, 1)
            for t in range(NT):
                dve.wait_ge(s_zT, t + 1)
                dve.tensor_copy(words(zT[:, t, :, :]), ps[6 + t % 2][:, :].rearrange("p (l w) -> p l w", l=2)).then_inc(s_zTc, 1)
            for t in range(NT):
                dve.wait_ge(s_y, t + 1)
                dve.scalar_tensor_tensor(out=x_sb[:, t, :], in0=ps[t][:, :], scalar=L_SCALING, in1=x_sb[:, t, :],
                                         op0=ALU.mult, op1=ALU.add).then_inc(s_fin, 1)


def kernel(x, ctx_4096, mask_1x1xSxS2_ff0, L0_xattn_x1_scale, L0_xattn_x1_zp, L0_xattn_x2_scale, L0_xattn_x2_zp,
           L0_ffn_router_w, L0_ffn_router_b, L0_ffn_router_bias, L0_ffn_ew1, L0_ffn_eb1, L0_ffn_ew2, L0_ffn_eb2,
           L0_ffn_ew3, L0_ffn_eb3, L0_ffn_sw1, L0_ffn_sb1, L0_ffn_sw2, L0_ffn_sb2, L0_ffn_sw3, L0_ffn_sb3,
           L1_xattn_q_proj_w, L1_xattn_k_proj_w, L1_xattn_v_proj_w, L1_xattn_o_proj_w, L1_xattn_q_norm_w,
           L1_xattn_k_norm_w, L1_ffn_A_w, L1_ffn_B_w, L1_ffn_Wq_w, L1_ffn_keys):
    import numpy as np
    import concourse.bacc as bacc
    from concourse.bass_utils import run_bass_kernel_spmd

    def a(v):
        return np.asarray(v)

    def chunked(w):
        return w.reshape(KC, P, -1).transpose(1, 0, 2)

    def groups(w):
        return chunked(w).reshape(P, KC, -1, GW).transpose(2, 0, 1, 3).reshape(-1, P, WG)

    def rows(v, n=1):
        return np.tile(v.reshape(1, -1), (P, n))

    ctx = a(ctx_4096)
    ctx_t = ctx.transpose(2, 0, 1).reshape(D, BATCH * CTX)
    wk, wv = groups(a(L1_xattn_k_proj_w).T), groups(a(L1_xattn_v_proj_w).T)

    def experts(ew, sw):
        both = np.concatenate([ew, sw.reshape(D, 2, INTER).transpose(1, 0, 2)])
        return both.reshape(NE, KC, P, INTER).transpose(0, 2, 1, 3).reshape(NE, P, KC * INTER)

    moe = np.concatenate([experts(a(L0_ffn_ew1), a(L0_ffn_sw1)), experts(a(L0_ffn_ew2), a(L0_ffn_sw2)),
                          np.concatenate([a(L0_ffn_ew3), a(L0_ffn_sw3).reshape(2, INTER, D)])], axis=2)
    moe_b = np.stack([np.concatenate([a(L0_ffn_eb1), a(L0_ffn_sb1).reshape(2, INTER)]).T,
                      np.concatenate([a(L0_ffn_eb2), a(L0_ffn_sb2).reshape(2, INTER)]).T], axis=1)
    params = np.concatenate([rows(a(L1_xattn_q_norm_w)), rows(a(L1_xattn_k_norm_w)), moe_b.reshape(P, -1),
                             chunked(a(L0_ffn_router_w)).reshape(P, -1), rows(a(L0_ffn_router_b), NT),
                             rows(a(L0_ffn_router_bias), NT)]
                            + [rows(a(v)) for v in (L0_xattn_x1_scale, L0_xattn_x1_zp, L0_xattn_x2_scale,
                                                    L0_xattn_x2_zp)], axis=1)
    arrays = {
        "x_rows": a(x).reshape(TOK, D),
        "ctx_nat": ctx.reshape(BATCH * KC, P, D).transpose(1, 0, 2).reshape(P, -1),
        "ctx_t": chunked(ctx_t).reshape(P, KC, BATCH, CTX).transpose(0, 2, 1, 3).reshape(P, BATCH, WG),
        "params": params,
        "mask": a(mask_1x1xSxS2_ff0).reshape(SEQ, CTX),
        "wkv": np.stack([wv[0], wk[0], wk[1], wv[1]]),
        "moe": moe,
        "moe_b3": np.concatenate([a(L0_ffn_eb3), a(L0_ffn_sb3).reshape(1, D)]),
        "wq": groups(a(L1_xattn_q_proj_w).T),
        "wo": a(L1_xattn_o_proj_w).T.reshape(KVH, REP, P, D).transpose(0, 2, 1, 3).reshape(KVH, P, WG),
        "a_w": chunked(a(L1_ffn_A_w).T).reshape(P, WG),
        "b_w": chunked(a(L1_ffn_B_w).T).reshape(P, WG),
        "l_wq": chunked(a(L1_ffn_Wq_w).T),
        "l_keys": a(L1_ffn_keys).T,
    }
    nc = bacc.Bacc("TRN2", target_bir_lowering=False, num_devices=1)
    sent, args = {}, {}
    for name, v in arrays.items():
        v = np.ascontiguousarray(v)
        sent["in_" + name] = v
        args[name] = nc.dram_tensor("in_" + name, v.shape, mybir.dt.from_np(v.dtype), kind="ExternalInput").ap()
    out = nc.dram_tensor("out_x", (TOK, D), F32, kind="ExternalOutput").ap()
    xattn_ffn_kernel(nc, out=out, **args)
    r = run_bass_kernel_spmd(nc, [sent], core_ids=[0])
    return r.results[0]["out_x"].reshape(BATCH, SEQ, D)
```

```python
from contextlib import ExitStack

import concourse.bass as bass
from concourse import mybir

P = 128
D = 512
KC = D // P
BATCH, SEQ, CTX = 2, 256, 512
TOK = BATCH * SEQ
NT = TOK // P
QT_PER_B = SEQ // P
SC = CTX // P
NST = BATCH * SC
HEADS, KVH, HD = 32, 8, 128
REP = HEADS // KVH
E_ROUTED, GROUPS, TOPG, TOPE = 16, 4, 2, 2
EPG = E_ROUTED // GROUPS
NE = 18
INTER = 128
L_EXP, RANK, RD = 64, 8, 16
GW = 512
WG = KC * GW
EG = 2 * KC * INTER + D

QUARTERS = ((0, 1), (2, 3), (), ())

PAR_QN, PAR_KN, PAR_MB = 0, HD, 2 * HD
PAR_RW = PAR_MB + 2 * NE
PAR_RB = PAR_RW + KC * E_ROUTED
PAR_SC = PAR_RB + 2 * NT * E_ROUTED
PAR_END = PAR_SC + 16

ROUND = 12582912.0
MID = 128.0
QMAX = 255.0
EPS = 1e-5
RSQRT_MAGIC = float(0x5F3759DF)
BIG = 3.0e38
PSCALE = 16384.0
L_SCALING = 32.0 / 16.0

ALU = mybir.AluOpType
ACT = mybir.ActivationFunctionType
F16 = mybir.dt.float16
F32 = mybir.dt.float32
I32 = mybir.dt.int32
AX_X = mybir.AxisListType.X


def xattn_ffn_kernel(nc, x_rows, ctx_nat, first_chunks, ctx_t, mask, params, wkv, moe, moe_b3, wq, wo, a_w, b_w, l_wq, l_keys, out):
    gates_dram = nc.dram_tensor("gates_dram", (NE, TOK), F32, kind="Internal").ap()
    with ExitStack() as ctx:
        def sb(name, shape, dt):
            return ctx.enter_context(nc.sbuf_tensor(name, shape, dt))

        def sem(name):
            return ctx.enter_context(nc.semaphore(name))

        k_sb = sb("k_sb", [P, KVH, 2, BATCH * CTX], F16)
        v_sb = sb("v_sb", [P, NST, 2, KVH * HD], F16)
        q_sb = sb("q_sb", [P, KVH * NT, 2, REP * P], F16)
        x_sb = sb("x_sb", [P, NT, D], F32)
        xT = sb("xT", [P, NT, 2, D], F16)
        nmask = sb("nmask", [P, QT_PER_B, CTX], F32)
        stage = sb("stage", [P, 2, WG], F32)
        wsp = sb("wsp", [P, 2, 2, WG], F16)
        f32r = sb("f32r", [P, 4, GW], F32)
        hlr = sb("hlr", [P, 4, 2, GW], F16)
        pT1 = sb("pT1", [P, 4, 2, GW], F16)
        ident = sb("ident", [P, P], F16)
        par = sb("par", [P, PAR_END], F32)
        wneg = par[:, PAR_QN:PAR_KN]
        identf = par[:, PAR_KN:PAR_MB]
        mb = par[:, PAR_MB:PAR_RW].rearrange("p (a e) -> p a e", a=2)
        rw = par[:, PAR_RW:PAR_RB]
        rb = par[:, PAR_RB:PAR_SC].rearrange("p (a n) -> p a n", a=2)
        scs = par[:, PAR_SC:PAR_END]
        rws = sb("rws", [P, 2, KC * E_ROUTED], F16)
        ones = sb("ones", [P, 1], F16)
        st6 = sb("st6", [P, NT, 6], F32)
        mv = sb("mv", [P, NT, 2], F32)
        nw = sb("nw", [P, 4, NT], F32)
        sml = sb("sml", [P, 8, 16], F32)

        early = q_sb[:, :, :, :].rearrange("p a b c -> p (a b c)")
        ctxs = early[:, 0:2 * KC * NST * P].rearrange("p (k l s) -> p k l s", k=KC, l=2)
        wkvs = early[:, 8192:24576].rearrange("p (w l c) -> p w l c", w=4, l=2)
        cnat = early[:, 24576:32768].bitcast(F32)
        cq = xT[:, :, :, :].rearrange("p a b c -> p (a b c)")
        xqT = pT1[:, 0:2, :, :].rearrange("p a b (k t) -> p (a b) k t", k=KC)
        ones128 = pT1[:, 2, 0, 0:P]
        pT0 = xT
        pT = [pT0, pT1]
        gate_bc = [hlr[:, 2, :, :].rearrange("p a b -> p (a b)").bitcast(F32),
                   hlr[:, 3, :, :].rearrange("p a b -> p (a b)").bitcast(F32)]
        b3s = stage[:, 1, EG:WG]
        gateT = stage[:, 0, EG:WG]
        gatesT = [wsp[0:E_ROUTED + 1, 0, l, EG:WG] for l in range(2)]
        b3 = [wsp[0:E_ROUTED + 1, 1, l, EG:WG] for l in range(2)]
        kv_land = k_sb[:, :, :, :].rearrange("p a b c -> p (a b c)").bitcast(F32).rearrange("p (w c) -> p w c", w=4)
        gt = ctx.enter_context(nc.sbuf_tensor("gt", [P, NT, NE], F32))
        rstat = ctx.enter_context(nc.sbuf_tensor("rstat", [P, 4, NT], F32))
        cmp_gt = pT1[:, 0, :, :].rearrange("p a b -> p (a b)")
        cmp_eq = pT1[:, 1, :, :].rearrange("p a b -> p (a b)")
        mneg = ctx.enter_context(nc.sbuf_tensor("mneg", [P, 4], F32))
        psum_col = ctx.enter_context(nc.sbuf_tensor("psum_col", [P, 4], F32))
        rinv = ctx.enter_context(nc.sbuf_tensor("rinv", [P, 2, 4], F32))
        ss = ctx.enter_context(nc.sbuf_tensor("ss", [P, 2, REP], F32))
        root = ctx.enter_context(nc.sbuf_tensor("root", [P, 2, REP], F32))
        rrt = ctx.enter_context(nc.sbuf_tensor("rrt", [P, 2, REP], F32))
        late = k_sb[:, :, :, :].rearrange("p a b c -> p (a b c)").bitcast(F32)
        lower = pT1[:, 3, 0, 0:E_ROUTED * E_ROUTED].rearrange("p (i j) -> p i j", i=E_ROUTED)
        lwq = late[:, 0:64].rearrange("p (k r) -> p k r", k=KC)
        lky = late[0:RD, 64:128]
        lwqs = late[:, 128:192].bitcast(F16).rearrange("p (l c) -> p l c", l=2)
        lkys = late[0:RD, 192:256].bitcast(F16).rearrange("p (l c) -> p l c", l=2)
        lqs = late[0:RD, 256:768].bitcast(F16).rearrange("p (l c) -> p l c", l=2)
        lsc = late[:, 1024:1280].rearrange("p (t e) -> p t e", t=NT)
        lw1 = late[:, 1280:1536].rearrange("p (t e) -> p t e", t=NT)
        lw2 = late[:, 1536:1792].rearrange("p (t e) -> p t e", t=NT)
        lex = late[:, 1792:2048].rearrange("p (t e) -> p t e", t=NT)
        lm8 = late[:, 2048:2112].rearrange("p (t a b) -> p t a b", t=NT, a=2)
        lng = late[:, 2112:2120]
        lsum = late[:, 2120:2128]
        zT = late[:, 4096:6144].bitcast(F16).rearrange("p (t l c) -> p t l c", t=NT, l=2)

        tail = v_sb[:, :, :, :].rearrange("p a b c -> p (a b c)").rearrange("p (w l c) -> p w l c", w=4, l=2)
        A, B = 2, 3

        ps = [ctx.enter_context(nc.psum_tensor(f"ps{i}", [P, 512], F32)) for i in range(8)]

        s_x = sem("s_x")
        s_cn = sem("s_cn")
        s_par = sem("s_par")
        s_late = sem("s_late")
        s_mask = sem("s_mask")
        s_w = [sem("s_w0"), sem("s_w1")]
        s_e12 = [sem("s_e12_0"), sem("s_e12_1")]
        s_e3 = [sem("s_e3_0"), sem("s_e3_1")]
        s_first = [sem(f"s_first{c}") for c in range(KC)]
        s_ctx = sem("s_ctx")
        s_kv = [sem(f"s_kv{w}") for w in range(3)]
        s_c0h = sem("s_c0h")
        s_c0l = sem("s_c0l")
        s_v0h = sem("s_v0h")
        s_v0l = sem("s_v0l")
        s_whi = sem("s_whi")
        s_wlo = sem("s_wlo")
        s_w12h = sem("s_w12h")
        s_w12l = sem("s_w12l")
        s_w3h = sem("s_w3h")
        s_w3l = sem("s_w3l")
        s_wqh = sem("s_wqh")
        s_wql = sem("s_wql")
        s_gload = [sem("s_gload0"), sem("s_gload1")]
        s_b3 = sem("s_b3")
        s_b3h = sem("s_b3h")
        s_b3l = sem("s_b3l")
        s_gh = sem("s_gh")
        s_gl = sem("s_gl")
        s_gst = sem("s_gst")
        s_id = sem("s_id")
        s_dve = sem("s_dve")
        s_xq = sem("s_xq")
        s_xqT = sem("s_xqT")
        s_xqTc = sem("s_xqTc")
        s_cq = sem("s_cq")
        s_sums = sem("s_sums")
        s_sumsc = sem("s_sumsc")
        s_main = sem("s_main")
        s_ln = sem("s_ln")
        s_lnh = sem("s_lnh")
        s_lnl = sem("s_lnl")
        s_lnT = sem("s_lnT")
        s_lnTc = [sem("s_lnTc_dve"), sem("s_lnTc_act")]
        s_c1 = sem("s_c1")
        s_rwh = sem("s_rwh")
        s_rws = sem("s_rws")
        s_rt = sem("s_rt")
        s_lg = sem("s_lg")
        s_rex = sem("s_rex")
        s_gate = sem("s_gate")
        s_gT = sem("s_gT")
        s_gTc = sem("s_gTc")
        s_vp = sem("s_vp")
        s_vh = sem("s_vh")
        s_vfree = sem("s_vfree")
        s_nw3 = sem("s_nw3")
        s_corr = sem("s_corr")
        s_pj = sem("s_pj")
        s_sq = sem("s_sq")
        s_ss = sem("s_ss")
        s_root = sem("s_root")
        s_rr = sem("s_rr")
        s_nrm = sem("s_nrm")
        s_nh = sem("s_nh")
        s_nl = sem("s_nl")
        s_tr = sem("s_tr")
        s_trc = sem("s_trc")
        s_up = sem("s_up")
        s_silu = sem("s_silu")
        s_hx = sem("s_hx")
        s_hg = sem("s_hg")
        s_hh = sem("s_hh")
        s_hl = sem("s_hl")
        s_dn = sem("s_dn")
        s_s = sem("s_s")
        s_t = sem("s_t")
        s_e = sem("s_e")
        s_r0 = sem("s_r0")
        s_ph = sem("s_ph")
        s_pl = sem("s_pl")
        s_T = sem("s_T")
        s_Tc = sem("s_Tc")
        s_pv = sem("s_pv")
        s_oh = sem("s_oh")
        s_ol = sem("s_ol")
        s_od = sem("s_od")
        s_ot = sem("s_ot")
        s_lw = sem("s_lw")
        s_lwl = sem("s_lwl")
        s_lq = sem("s_lq")
        s_lqh = sem("s_lqh")
        s_lqs = sem("s_lqs")
        s_lsc = sem("s_lsc")
        s_lng = sem("s_lng")
        s_lex = sem("s_lex")
        s_z = sem("s_z")
        s_zg = sem("s_zg")
        s_zh = sem("s_zh")
        s_zl = sem("s_zl")
        s_zT = sem("s_zT")
        s_zTc = sem("s_zTc")
        s_y = sem("s_y")
        s_fin = sem("s_fin")
        s_out = sem("s_out")

        def v_bank(hg, n):
            return ps[n - SC] if hg == 0 and n >= SC else ps[4 + n % SC]

        def words(ap):
            return ap.bitcast(F32)

        def three_products(pe, dst, lhs, rhs, start, stop):
            pe.matmul(dst, lhs[0], rhs[1], start=start, stop=False, skip_group_check=True)
            pe.matmul(dst, lhs[1], rhs[0], start=False, stop=False, skip_group_check=True)
            return pe.matmul(dst, lhs[0], rhs[0], start=False, stop=stop, skip_group_check=True)

        W12, W3 = slice(0, 2 * KC * INTER), slice(2 * KC * INTER, EG)

        block = ctx.enter_context(nc.Block())

        @block.sync
        def _(sp):
            def load(slot, src, width):
                sp.dma_start(stage[:, slot, 0:width], src).then_inc(s_w[slot], 16)

            for c in range(KC):
                sp.dma_start(stage[:, :, c * GW:(c + 1) * GW], first_chunks[c]).then_inc(s_first[c], 16)
            sp.dma_start(par[:, 0:PAR_SC + 4], params).then_inc(s_par, 16)
            sp.dma_start(x_sb[:, :, :], x_rows.rearrange("(t p) d -> p t d", p=P)).then_inc(s_x, 16)
            sp.dma_start(kv_land[:, 0, :], ctx_t).then_inc(s_ctx, 16)
            sp.dma_start(cnat, ctx_nat).then_inc(s_cn, 16)
            for w in (3, 1, 2):
                sp.dma_start(kv_land[:, w, :], wkv[w - 1]).then_inc(s_kv[w - 1], 16)

            def load_w12(e, s):
                sp.dma_start(stage[:, s, W12], moe[e][:, W12]).then_inc(s_e12[s], 16)

            def load_w3(e, s):
                sp.dma_start(stage[:, s, W3], moe[e][:, W3]).then_inc(s_e3[s], 16)

            sp.wait_ge(s_c0l, KC)
            load_w12(0, 0)
            load_w3(0, 0)
            sp.wait_ge(s_v0l, KC)
            load_w12(1, 1)
            load_w3(1, 1)
            sp.dma_start(b3s[0:E_ROUTED + 1, :], moe_b3).then_inc(s_b3, 16)
            sp.dma_start(nmask[:, :, :], mask.rearrange("(h p) c -> p h c", p=P)).then_inc(s_mask, 16)
            sp.wait_ge(s_w12l, 1)
            load_w12(2, 0)
            sp.wait_ge(s_w12l, 2)
            load_w12(3, 1)
            sp.wait_ge(s_w3l, 1)
            load_w3(2, 0)
            with sp.Fori(2, NE // 2) as i:
                for s in range(2):
                    sp.wait_ge(s_w12l, 2 * i + s - 1)
                    load_w12(2 * i + s, s)
                    sp.wait_ge(s_w3l, 2 * i + s - 2)
                    load_w3(2 * i + s - 1, 1 - s)
            sp.wait_ge(s_w3l, NE - 2)
            load_w3(NE - 1, 1)
            for s in range(2):
                sp.wait_ge(s_w3l, NE - 1 + s)
                load(s, wq[s], WG)
            with sp.Fori(1, KVH // 2) as i:
                for s in range(2):
                    sp.wait_ge(s_wql, 4 * (2 * i + s - 1))
                    load(s, wq[2 * i + s], WG)
            with sp.Fori(0, KVH // 2) as i:
                for s in range(2):
                    sp.wait_ge(s_wql, 4 * (KVH + 2 * i + s - 1))
                    load(s, wo[2 * i + s], WG)
            for s, src in enumerate((a_w, b_w)):
                sp.wait_ge(s_wql, 4 * (2 * KVH + s - 1))
                load(s, src, WG)
            for t in range(NT):
                sp.wait_ge(s_fin, t + 1)
                sp.dma_start(out[t * P:(t + 1) * P, :], x_sb[:, t, :]).then_inc(s_out, 16)
            sp.wait_ge(s_out, 16 * NT)

        @block.tensor
        def _(pe):
            def transposes(src_hi_lo, dst, place):
                for l in range(2):
                    for c in range(4):
                        at = place(l, c) * P
                        last = pe.transpose(dst.bitcast(F16)[:, at:at + P], src_hi_lo[:, l, c * P:(c + 1) * P], ident[:, :])
                return last

            def hi_lo_major(l, c):
                return 4 * l + c

            def block_major(l, c):
                return 2 * c + l

            def ln_transpose(n, t):
                pe.wait_ge(s_lnl, NT * n + t + 1)
                transposes(hlr[:, t, :, :], ps[t][:, :], hi_lo_major).then_inc(s_lnT, 1)

            def ln_transposes(n):
                for t in range(NT):
                    ln_transpose(n, t)

            def ln_transposed(n, t):
                if n < 2:
                    pe.wait_ge(s_lnTc[t % 2], NT // 2 * n + t // 2 + 1)
                else:
                    pe.wait_ge(s_lnTc[1], NT + t + 1)

            def v_products(hg, b, j, c):
                w = (0, 3)[hg]
                return three_products(
                    pe, v_bank(hg, SC * b + j)[:, :],
                    [ctxs[:, c, l, b * CTX + j * P:b * CTX + (j + 1) * P] for l in range(2)],
                    [wkvs[:, w, l, c * GW:(c + 1) * GW] for l in range(2)], c == 0, c == KC - 1)

            def v_rows(hg, b):
                for j in range(SC):
                    for c in range(KC):
                        last = v_products(hg, b, j, c)
                    last.then_inc(s_vp, 1)

            def rms_phase(r0, iters, tiles, project, place, after_first=None, before_last=None, beside_last=None):
                def transposed(r, j):
                    pe.wait_ge(s_nl, r + 1)
                    pe.wait_ge(s_trc, r + 1)
                    transposes(hlr[:, j % 4, :, :], ps[6 + j % 2][:, :], place).then_inc(s_tr, 1)

                def body(i, first):
                    for j in range(tiles):
                        r = r0 + tiles * i + j
                        if not first or j >= 4:
                            pe.wait_ge(s_nrm, r - 3)
                        project(i, j).then_inc(s_pj, 1)
                        if not first or j >= 4:
                            transposed(r - 4, j)

                body(0, True)
                if after_first:
                    after_first()
                with pe.Fori(1, iters) as i:
                    body(i, False)
                if before_last:
                    before_last()
                for j in range(4):
                    transposed(r0 + tiles * iters - 4 + j, j)
                    if beside_last:
                        for k in ((0, 1), (2, 3), (), ())[j]:
                            beside_last(k)

            def k_project(i, j):
                for c in range(KC):
                    last = three_products(
                        pe, ps[j % 4][:, :],
                        [ctxs[:, c, l, bass.ds(i * (2 * P) + (j // 2) * P, P)] for l in range(2)],
                        [wkvs[:, 1 + j % 2, l, c * GW:(c + 1) * GW] for l in range(2)], c == 0, c == KC - 1)
                return last

            def q_project(i, j):
                s, t = divmod(j, NT)
                if t == 0:
                    pe.wait_ge(s_wql, 4 * (2 * i + s + 1))
                if isinstance(i, int) and s == 0:
                    ln_transposed(1, t)
                if isinstance(i, int) and j == 3:
                    pe.wait_ge(s_vfree, 2 * NST)
                for c in range(KC):
                    last = three_products(
                        pe, ps[j % 4][:, :],
                        [xT[:, t, l, c * P:(c + 1) * P] for l in range(2)],
                        [wsp[:, s, l, c * GW:(c + 1) * GW] for l in range(2)], c == 0, c == KC - 1)
                return last

            for b in range(BATCH):
                for c in range(KC):
                    if b == 0:
                        pe.wait_ge(s_c0l, c + 1)
                        pe.wait_ge(s_v0l, c + 1)
                    else:
                        pe.wait_ge(s_wlo, c + 1)
                    for j in range(SC):
                        last = v_products(0, b, j, c)
                        if c == KC - 1:
                            last.then_inc(s_vp, 1)

            def up(e, s, which=(0, 1)):
                pe.wait_ge(s_w12l, e + 1)
                for u in which:
                    for c in range(KC):
                        at = (u * KC + c) * INTER
                        last = three_products(
                            pe, ps[4 + 2 * s + u][:, :],
                            [wsp[:, s, l, at:at + INTER] for l in range(2)],
                            [xT[:, :, l, c * P:(c + 1) * P] for l in range(2)], c == 0, c == KC - 1)
                    last.then_inc(s_up, 1)

            def down(e, s, last_expert=False):
                pe.wait_ge(s_w3l, e + 1)
                pe.wait_ge(s_hl, e + 1)
                for t in range(NT):
                    last = three_products(
                        pe, ps[t][:, :], [hlr[:, s, l, t * P:(t + 1) * P] for l in range(2)],
                        [wsp[:, s, l, 2 * KC * INTER:EG] for l in range(2)], False, last_expert)
                last.then_inc(s_dn, 1)

            def first_expert():
                pe.wait_ge(s_gate, 1)
                for t in range(NT):
                    last = pe.transpose(ps[5][0:NE, t * P:(t + 1) * P], gt[:, t, :], identf)
                last.then_inc(s_gT, 1)
                up(0, 0, (0,))

            pe.wait_ge(s_id, 4)
            pe.wait_ge(s_vfree, 2)
            for t in range(NT):
                pe.wait_ge(s_xq, t + 1)
                for c in range(KC):
                    last = pe.transpose(ps[4 + t // 2][:, :].bitcast(F16)[:, (t % 2) * D + c * P:(t % 2) * D + (c + 1) * P],
                                        hlr[:, t, 0, c * P:(c + 1) * P], ident[:, :])
                last.then_inc(s_xqT, 1)
            for b in range(BATCH):
                pe.wait_ge(s_vfree, 3 + b)
                pe.wait_ge(s_cq, b + 1)
                for c in range(KC):
                    last = pe.matmul(ps[6 + b][:, :], ones128, cq[:, (b * KC + c) * D:(b * KC + c + 1) * D],
                                     start=(c == 0), stop=(c == KC - 1))
                last.then_inc(s_sums, 1)
            pe.wait_ge(s_xqTc, 2)
            for t in range(NT):
                for c in range(KC):
                    last = pe.matmul(ps[4][:, t:t + 1], xqT[:, t, c, :], ones[:, :], start=(c == 0), stop=(c == KC - 1))
            last.then_inc(s_sums, 1)
            for t in range(NT):
                pe.wait_ge(s_vfree, SC + t + 1)
                for c in range(KC):
                    last = pe.matmul(ps[t][:, :], xqT[:, t, c, :],
                                     cq[:, ((t // 2) * KC + c) * D:((t // 2) * KC + c + 1) * D],
                                     start=(c == 0), stop=(c == KC - 1))
                last.then_inc(s_main, 1)

            pe.wait_ge(s_corr, NT)
            pe.wait_ge(s_wlo, KC + 1)
            v_rows(1, 0)
            ln_transposes(0)

            pe.wait_ge(s_rws, 1)
            pe.wait_ge(s_vfree, NST + 1)
            for t in range(NT):
                ln_transposed(0, t)
                for c in range(KC):
                    last = three_products(
                        pe, ps[4][:, t * E_ROUTED:(t + 1) * E_ROUTED],
                        [xT[:, t, l, c * P:(c + 1) * P] for l in range(2)],
                        [rws[:, l, c * E_ROUTED:(c + 1) * E_ROUTED] for l in range(2)], c == 0, c == KC - 1)
                if t == 0:
                    last.then_inc(s_tr, 4)
                if t == 1:
                    last.then_inc(s_trc, 2)
            last.then_inc(s_rt, 1)

            pe.wait_ge(s_wlo, KC + 3)
            rms_phase(0, 4, 4, k_project, block_major,
                      lambda: pe.wait_ge(s_vfree, NST + 4),
                      first_expert)

            pe.wait_ge(s_gTc, 1)
            up(0, 0, (1,))
            pe.wait_ge(s_b3l, 1)
            pe.wait_ge(s_gl, 1)
            for t in range(NT):
                three_products(pe, ps[t][:, :], [g[:, t * P:(t + 1) * P] for g in gatesT], b3, True, False)
            pe.wait_ge(s_trc, 2 + 16)
            up(1, 1)
            down(0, 0)
            pe.wait_ge(s_hx, 1)
            up(2, 0)
            down(1, 1)
            with pe.Fori(1, NE // 2 - 1) as i:
                pe.wait_ge(s_hx, 2 * i)
                up(2 * i + 1, 1)
                down(2 * i, 0)
                pe.wait_ge(s_hx, 2 * i + 1)
                up(2 * i + 2, 0)
                down(2 * i + 1, 1)
            pe.wait_ge(s_hx, NE - 2)
            up(NE - 1, 1)
            down(NE - 2, 0)
            down(NE - 1, 1, True)

            pe.wait_ge(s_hx, NE)
            v_rows(1, 1)
            ln_transposes(1)
            def scores(g, j, k, first):
                m, hh = divmod(j, REP)
                if first and j < 4:
                    pe.wait_ge(s_nrm, 16 + NT * KVH - 3 + j)
                if not first or j >= 4:
                    pe.wait_ge(s_t, k - 3)
                b = m // QT_PER_B
                three_products(
                    pe, ps[j % 4][:, :],
                    [q_sb[:, bass.ds(4 * g + m, 1), l, hh * P:(hh + 1) * P] for l in range(2)],
                    [k_sb[:, bass.ds(g, 1), l, b * CTX:(b + 1) * CTX] for l in range(2)], True, True).then_inc(s_s, 1)

            def prob_transposes(j, k, wait_bank=True):
                pe.wait_ge(s_pl, k + 1)
                if wait_bank:
                    pe.wait_ge(s_Tc, k - 1)
                transposes(hlr[:, j % 4, :, :], ps[4 + j % 2][:, :], hi_lo_major).then_inc(s_T, 1)

            def values(w, gw, mw, c, wait_bank=True):
                if c == 0:
                    pe.wait_ge(s_Tc, 4 * w + 4)
                    if wait_bank:
                        pe.wait_ge(s_ol, w - 1)
                par = mw % 2
                last = three_products(
                    pe, ps[6 + par][:, :],
                    [v_sb[:, (mw // QT_PER_B) * SC + c, l, bass.ds(gw * HD, HD)] for l in range(2)],
                    [pT[par][:, :, l, c * P:(c + 1) * P] for l in range(2)], c == 0, c == SC - 1)
                if c == SC - 1:
                    last.then_inc(s_pv, 1)

            def attention(g, first):
                for j in range(4 * REP):
                    k = 16 * g + j
                    m, c = divmod(j, REP)
                    if not first or j >= 4:
                        scores(g, j, k, first)
                        prob_transposes(j, k - 4, not first or j >= 6)
                    if not first or m >= 2:
                        values(4 * g + m - 2, g if m >= 2 else g - 1, (m - 2) % 4, c, not first)

            def o_products(g, w, t, first, last_group):
                for c in range(REP):
                    last = three_products(
                        pe, ps[t][:, :],
                        [q_sb[:, bass.ds(4 * g + t, 1), l, c * P:(c + 1) * P] for l in range(2)],
                        [w[:, l, c * GW:(c + 1) * GW] for l in range(2)],
                        first and c == 0, last_group and c == REP - 1)
                return last

            def o_group(g, s, first):
                pe.wait_ge(s_wql, 4 * (KVH + 1) + 4 * g)
                for t in range(NT):
                    last = o_products(g, wsp[:, s], t, first, False)
                last.then_inc(s_od, 1)

            rms_phase(16, 4, 2 * NT, q_project, hi_lo_major, beside_last=lambda j: scores(0, j, j, True))
            attention(0, True)
            pe.wait_ge(s_trc, 2 + 16 + NT * KVH)
            with pe.Fori(1, KVH) as g:
                attention(g, False)
            for j in range(4):
                prob_transposes(j, 16 * KVH - 4 + j)
                values(4 * KVH - 2, KVH - 1, 2, j)
            o_group(0, 0, True)
            for c in range(SC):
                values(4 * KVH - 1, KVH - 1, 3, c)

            o_group(1, 1, False)
            with pe.Fori(1, KVH // 2 - 1) as i:
                for s in range(2):
                    o_group(2 * i + s, s, False)
            pe.wait_ge(s_wql, 4 * (2 * KVH))
            pe.wait_ge(s_ol, 4 * KVH)
            for t in range(NT):
                o_products(KVH - 2, tail[:, 0], t, False, False)
                if t >= 2:
                    ln_transpose(2, t - 2)
                o_products(KVH - 1, tail[:, 1], t, False, True).then_inc(s_ot, 1)

            def queries(t):
                ln_transposed(2, t)
                pe.wait_ge(s_lwl, 1)
                for c in range(KC):
                    last = three_products(
                        pe, ps[4][0:RD, t * P:(t + 1) * P], [lwqs[:, l, c * RD:(c + 1) * RD] for l in range(2)],
                        [xT[:, t, l, c * P:(c + 1) * P] for l in range(2)], c == 0, c == KC - 1)
                last.then_inc(s_lq, 1)

            def expert_scores(p):
                pe.wait_ge(s_lqs, p + 1)
                for u in (2 * p, 2 * p + 1):
                    last = three_products(
                        pe, ps[5][:, u * L_EXP:(u + 1) * L_EXP],
                        [lqs[:, l, u * P:(u + 1) * P] for l in range(2)],
                        [lkys[:, l, :] for l in range(2)], True, True)
                last.then_inc(s_lsc, 1)

            def bottleneck(t, between=None, after_chunk=1):
                ln_transposed(2, t)
                pe.wait_ge(s_wql, 4 * (2 * KVH + 1))
                for c in range(KC):
                    last = three_products(
                        pe, ps[t][:, :], [xT[:, t, l, c * P:(c + 1) * P] for l in range(2)],
                        [tail[:, A, l, c * GW:(c + 1) * GW] for l in range(2)], c == 0, c == KC - 1)
                    if between and c == after_chunk:
                        between()
                last.then_inc(s_z, 1)

            def z_transposes(t):
                pe.wait_ge(s_zl, t + 1)
                if t >= 2:
                    pe.wait_ge(s_zTc, t - 1)
                transposes(hlr[:, t, :, :], ps[6 + t % 2][:, :], hi_lo_major).then_inc(s_zT, 1)

            queries(0)
            queries(1)
            bottleneck(0)
            ln_transpose(2, 2)
            bottleneck(1, lambda: expert_scores(0))
            ln_transpose(2, 3)
            bottleneck(2, lambda: (queries(2), queries(3)))
            bottleneck(3, lambda: expert_scores(1), 0)
            pe.wait_ge(s_wql, 4 * (2 * KVH + 2))
            for t in range(NT):
                if t == 0:
                    z_transposes(0)
                if t + 1 < NT:
                    z_transposes(t + 1)
                pe.wait_ge(s_zTc, t + 1)
                for c in range(KC):
                    last = three_products(
                        pe, ps[t][:, :], [zT[:, t, l, c * P:(c + 1) * P] for l in range(2)],
                        [tail[:, B, l, c * GW:(c + 1) * GW] for l in range(2)], c == 0, c == KC - 1)
                last.then_inc(s_y, 1)

        @block.scalar
        def _(act):
            for c in range(KC):
                act.wait_ge(s_first[c], 16)
                act.copy(ctxs[:, c, 0, 0:CTX], stage[:, 0, c * CTX:(c + 1) * CTX]).then_inc(s_c0h, 1)
                act.copy(wkvs[:, 0, 0, c * GW:(c + 1) * GW], stage[:, 1, c * GW:(c + 1) * GW]).then_inc(s_v0h, 1)
            act.wait_ge(s_ctx, 16)
            for c in range(KC):
                act.copy(ctxs[:, c, 0, CTX:2 * CTX], kv_land[:, 0, c * CTX:(c + 1) * CTX]).then_inc(s_whi, 1)

            def group_hi(w):
                act.wait_ge(s_kv[w - 1], 16)
                act.copy(wkvs[:, w, 0, :], kv_land[:, w, :]).then_inc(s_whi, 1)

            def ln_hi(n):
                for t in range(NT):
                    act.wait_ge(s_ln, NT * n + t + 1)
                    act.copy(hlr[:, t, 0, :], f32r[:, t, :]).then_inc(s_lnh, 1)

            def ln_copies(n):
                for t in range(1, NT, 2):
                    act.wait_ge(s_lnT, NT * n + t + 1)
                    act.copy(words(xT[:, t, :, :]), ps[t][:, :].rearrange("p (l w) -> p l w", l=2)).then_inc(s_lnTc[1], 1)

            def v_hi(hg, tiles):
                for n in tiles:
                    act.wait_ge(s_vp, NST * hg + n + 1)
                    act.copy(v_sb[:, n, 0, hg * GW:(hg + 1) * GW], v_bank(hg, n)[:, :]).then_inc(s_vh, 1)

            def w12_hi(e, s):
                act.wait_ge(s_e12[s], 8 * (e - s) + 16)
                if not (isinstance(e, int) and e < 2):
                    act.wait_ge(s_up, 2 * e - 2)
                act.copy(wsp[:, s, 0, W12], stage[:, s, W12]).then_inc(s_w12h, 1)

            def w3_hi(e, s):
                act.wait_ge(s_e3[s], 8 * (e - s) + 16)
                if not (isinstance(e, int) and e < 2):
                    act.wait_ge(s_dn, e - 1)
                act.copy(wsp[:, s, 0, W3], stage[:, s, W3]).then_inc(s_w3h, 1)

            v_hi(0, (0, 1, 2, 3))
            group_hi(3)
            group_hi(1)
            v_hi(0, (4, 5, 6, 7))
            act.wait_ge(s_par, 16)
            act.copy(rws[:, 0, :], rw).then_inc(s_rwh, 1)
            for b in range(2):
                act.wait_ge(s_xqT, 2 * b + 2)
                act.copy(words(pT1[:, b, :, :]), ps[4 + b][:, :].rearrange("p (l w) -> p l w", l=2)).then_inc(s_xqTc, 1)
            group_hi(2)
            act.wait_ge(s_nw3, 1)
            for t in range(NT):
                act.activation(f32r[:, t, :], ps[6 + t // 2][:, :], ACT.Identity, bias=nw[:, 3, t:t + 1],
                               scale=scs[:, 9:10]).then_inc(s_corr, 1)
            w12_hi(0, 0)
            w3_hi(0, 0)
            w12_hi(1, 1)
            act.wait_ge(s_b3, 16)
            act.copy(b3[0], b3s[0:E_ROUTED + 1, :]).then_inc(s_b3h, 1)
            ln_hi(0)
            v_hi(1, (0,))
            ln_copies(0)
            v_hi(1, (1, 2, 3))

            act.wait_ge(s_lg, 2)
            act.activation(sml[:, 4:8, :], sml[:, 0:4, :], ACT.Exp).then_inc(s_rex, 1)

            def rms_phase(r0, iters, tiles, scale, bias, copy_out, quarter, beside_last=None):
                def squares(r, j, first):
                    act.wait_ge(s_pj, r + 1)
                    if not first or j >= 2:
                        act.wait_ge(s_ss, r - 1)
                    act.activation(f32r[:, j % 2, :], ps[j % 4][:, :], ACT.Square).then_inc(s_sq, 1)

                def roots(r, j, first):
                    act.wait_ge(s_ss, r + 1)
                    if not first or j >= 2:
                        act.wait_ge(s_rr, r - 1)
                    act.activation(root[:, j % 2, :], ss[:, j % 2, :], ACT.Sqrt, bias=bias, scale=scale).then_inc(s_root, 1)

                def hi(r, j, first):
                    act.wait_ge(s_nrm, r + 1)
                    act.wait_ge(s_tr, r + 1)
                    act.copy(hlr[:, j % 4, 0, :], f32r[:, 2 + j % 2, :]).then_inc(s_nh, 1)

                def copied(i, j, r):
                    act.wait_ge(s_tr, r + 5)
                    copy_out(i, j, ps[6 + j % 2][:, :]).then_inc(s_trc, 1)

                def body(i, first):
                    for j in range(tiles):
                        r = r0 + tiles * i + j
                        squares(r, j, first)
                        if not first or j >= 1:
                            roots(r - 1, (j - 1) % tiles, first and j - 1 < 2)
                        if not first or j >= 2:
                            hi(r - 2, (j - 2) % tiles, first and j - 2 < 4)
                        for c in QUARTERS[j % 4]:
                            quarter(i, j // 4, c)
                        if not first or j >= 4:
                            copied(i if j >= 4 else i - 1, (j - 4) % tiles, r - 4)

                body(0, True)
                with act.Fori(1, iters) as i:
                    body(i, False)
                end = tiles * iters
                roots(r0 + end - 1, tiles - 1, False)
                for j in range(2):
                    hi(r0 + end - 2 + j, tiles - 2 + j, False)
                for j in range(4):
                    copied(iters - 1, tiles - 4 + j, r0 + end - 4 + j)
                    if beside_last and j < 3:
                        beside_last(j)

            k_words = words(k_sb[:, :, :, :])

            def k_out(i, j, bank):
                h0 = (j % 2) * 4
                return act.copy(k_words[:, h0:h0 + 4, :, bass.ds(i * P + (j // 2) * (P // 2), P // 2)],
                                bank.rearrange("p (h l w) -> p h l w", h=4, l=2))

            def q_out(i, j, bank):
                return act.copy(words(q_sb[:, bass.ds(2 * NT * i + j, 1), :, :]), bank)

            rms_phase(0, 4, 4, 1.0 / HD, scs[:, 12:13], k_out, lambda i, g, c: None)

            def gate_load(e, s):
                act.dma_start(gate_bc[s], gates_dram[bass.ds(e, 1), :].partition_broadcast(P)
                              .rearrange("q a t -> q (a t)")).then_inc(s_gload[s], 16)

            def silu(e, s):
                act.wait_ge(s_up, 2 * e + 1)
                if not (isinstance(e, int) and e < 2):
                    act.wait_ge(s_hl, e - 1)
                act.activation(f32r[:, s, :], ps[4 + 2 * s][:, :], ACT.Silu, bias=mb[:, 0, bass.ds(e, 1)]).then_inc(s_silu, 1)

            def hidden_hi(e, s):
                act.wait_ge(s_hg, e + 1)
                if not (isinstance(e, int) and e < 2):
                    act.wait_ge(s_dn, e - 1)
                act.copy(hlr[:, s, 0, :], f32r[:, s, :]).then_inc(s_hh, 1)

            def expert(e, s):
                silu(e, s)
                if not (isinstance(e, int) and e + 2 >= NE):
                    w12_hi(e + 2, s)
                hidden_hi(e, s)
                if not (isinstance(e, int) and e + 2 >= NE):
                    gate_load(e + 2, s)
                if not (isinstance(e, int) and e + 1 >= NE):
                    w3_hi(e + 1, 1 - s)

            act.wait_ge(s_gTc, 1)
            act.copy(gatesT[0], gateT[0:E_ROUTED + 1, :]).then_inc(s_gh, 1)
            act.dma_start(gates_dram, gateT[0:NE, :]).then_inc(s_gst, 16)
            act.wait_ge(s_gst, 16)
            for s in range(2):
                gate_load(s, s)
            for s in range(2):
                expert(s, s)
            with act.Fori(1, NE // 2 - 1) as i:
                for s in range(2):
                    expert(2 * i + s, s)
            for s in range(2):
                expert(NE - 2 + s, s)

            def quarter_hi(slot, c, free=None):
                if free is not None:
                    act.wait_ge(*free)
                act.copy(wsp[:, slot, 0, c * GW:(c + 1) * GW], stage[:, slot, c * GW:(c + 1) * GW]).then_inc(s_wqh, 1)

            act.wait_ge(s_w[0], 16)
            for c in range(4):
                quarter_hi(0, c, (s_dn, NE - 1) if c == 0 else None)
            ln_hi(1)
            ln_copies(1)
            v_hi(1, (4, 5, 6, 7))

            def q_quarter(i, s, c):
                if c == 0:
                    act.wait_ge(s_w[1 - s], 16 * (1 + s) + 16 * i)
                    act.wait_ge(s_pj, 16 + 8 * i + 4 * s)
                quarter_hi(1 - s, c)

            def exponentials(j, k):
                act.wait_ge(s_t, k + 1)
                act.activation(f32r[:, j % 4, :], f32r[:, j % 4, :], ACT.Exp, bias=mneg[:, j % 4:j % 4 + 1], scale=-1.0,
                               accum_out=psum_col[:, j % 4:j % 4 + 1]).then_inc(s_e, 1)

            def prob_copy(j, k, u, wait_values):
                act.wait_ge(s_T, k + 1)
                if wait_values:
                    act.wait_ge(s_pv, u - 1)
                act.copy(words(pT[(j // REP) % 2][:, j % REP, :, :]), ps[4 + j % 2][:, :]
                         .rearrange("p (l w) -> p l w", l=2)).then_inc(s_Tc, 1)

            def o_hi(w, mw):
                act.wait_ge(s_pv, w + 1)
                act.activation(q_sb[:, bass.ds(w, 1), 0, :], ps[6 + mw % 2][:, :], ACT.Copy, scale=1.0 / PSCALE).then_inc(s_oh, 1)

            def attention(g, first):
                for j in range(4 * REP):
                    k = 16 * g + j
                    m, hh = divmod(j, REP)
                    if not first or j >= 3:
                        exponentials(j, k)
                    if not first or j >= 4:
                        prob_copy((j - 4) % 16, k - 4, 4 * g + m - 1, hh == 0 and (not first or m >= 3))
                    if hh == 0 and (not first or m >= 3):
                        o_hi(4 * g + m - 3, (m - 3) % 4)

            rms_phase(16, 4, 2 * NT, 1.0 / 64, scs[:, 13:14], q_out, q_quarter,
                      lambda j: exponentials(j, j))
            attention(0, True)
            with act.Fori(1, KVH) as g:
                attention(g, False)
            o_hi(4 * KVH - 3, 1)
            for j in range(4):
                prob_copy(12 + j, 16 * KVH - 4 + j, 4 * KVH - 1, j == 0)
            o_hi(4 * KVH - 2, 0)

            for dst, src in ((lwq, l_wq), (lky, l_keys)):
                act.dma_start(dst, src).then_inc(s_late, 16)
            act.wait_ge(s_w[1], 16 * (KVH // 2 + 1))
            for c in range(4):
                quarter_hi(1, c)
            o_hi(4 * KVH - 1, 1)
            act.wait_ge(s_late, 32)
            act.copy(lwqs[:, 0, :], lwq.rearrange("p k r -> p (k r)")).then_inc(s_lw, 1)
            act.copy(lkys[:, 0, :], lky).then_inc(s_lw, 1)
            with act.Fori(0, KVH // 2 - 2) as i:
                for s in range(2):
                    act.wait_ge(s_w[s], 16 * (KVH // 2 + 2) + 16 * i)
                    act.wait_ge(s_od, 2 * i + s + 1)
                    for c in range(4):
                        quarter_hi(s, c)
            for n in range(4):
                act.wait_ge(s_w[n % 2], 16 * (KVH + n // 2))
                for c in range(4):
                    at = slice(c * GW, (c + 1) * GW)
                    act.copy(tail[:, n, 0, at], stage[:, n % 2, at]).then_inc(s_wqh, 1)

            def last_ln_hi(t):
                act.wait_ge(s_ln, 2 * NT + t + 1)
                act.copy(hlr[:, t, 0, :], f32r[:, t, :]).then_inc(s_lnh, 1)

            def last_ln_copy(t):
                act.wait_ge(s_lnT, 2 * NT + t + 1)
                act.copy(words(xT[:, t, :, :]), ps[t][:, :].rearrange("p (l w) -> p l w", l=2)).then_inc(s_lnTc[1], 1)

            def queries_hi(p):
                act.wait_ge(s_lq, 2 * p + 2)
                at = slice(2 * p * P, (2 * p + 2) * P)
                act.copy(lqs[:, 0, at], ps[4][0:RD, at]).then_inc(s_lqh, 1)

            def gate_exponentials(p):
                for t in (2 * p, 2 * p + 1):
                    act.wait_ge(s_lng, t + 1)
                    act.activation(lex[:, t, :], lsc[:, t, :], ACT.Exp, bias=lng[:, t:t + 1]).then_inc(s_lex, 1)

            def z_hi(t):
                act.wait_ge(s_zg, t + 1)
                act.copy(hlr[:, t, 0, :], f32r[:, t, :]).then_inc(s_zh, 1)

            def z_copy(t):
                act.wait_ge(s_zT, t + 1)
                act.copy(words(zT[:, t, :, :]), ps[6 + t % 2][:, :].rearrange("p (l w) -> p l w", l=2)).then_inc(s_zTc, 1)

            last_ln_hi(0)
            last_ln_hi(1)
            last_ln_copy(0)
            last_ln_hi(2)
            last_ln_copy(1)
            queries_hi(0)
            last_ln_hi(3)
            last_ln_copy(2)
            gate_exponentials(0)
            last_ln_copy(3)
            queries_hi(1)
            z_hi(0)
            z_hi(1)
            gate_exponentials(1)
            z_copy(0)
            z_copy(1)
            for t in range(2, NT):
                z_hi(t)
            for t in range(2, NT):
                z_copy(t)

        @block.gpsimd
        def _(pool):
            pool.memset(ident[:, :], 0.0).then_inc(s_id, 1)
            pool.memset(lower[:, :, :], 1.0).then_inc(s_id, 1)
            pool.wait_ge(s_id, 2)
            pool.affine_select(out=ident[:, :], in_=ident[:, :], compare_op=ALU.not_equal, fill=1.0, base=0,
                               pattern=[[-1, P]], channel_multiplier=1).then_inc(s_id, 1)
            pool.affine_select(out=lower[:, :, :], in_=lower[:, :, :], compare_op=ALU.is_gt, fill=0.0, base=0,
                               pattern=[[1, E_ROUTED], [-1, E_ROUTED]], channel_multiplier=0).then_inc(s_id, 1)

            def low(dst_lo, src, dst_hi):
                return pool.tensor_tensor(dst_lo, src, dst_hi, ALU.subtract)

            for c in range(KC):
                pool.wait_ge(s_v0h, c + 1)
                at = slice(c * GW, (c + 1) * GW)
                low(wkvs[:, 0, 1, at], stage[:, 1, at], wkvs[:, 0, 0, at]).then_inc(s_v0l, 1)
            for c in range(KC):
                pool.wait_ge(s_whi, c + 1)
                low(ctxs[:, c, 1, CTX:2 * CTX], kv_land[:, 0, c * CTX:(c + 1) * CTX],
                    ctxs[:, c, 0, CTX:2 * CTX]).then_inc(s_wlo, 1)
            pool.wait_ge(s_cn, 16)
            pool.wait_ge(s_dve, 1)
            for b in range(BATCH):
                c32 = cnat[:, b * KC * D:(b + 1) * KC * D]
                pool.tensor_scalar(c32, c32, scs[:, 5:6], scs[:, 3:4], ALU.mult, ALU.add).then_inc(s_c1, 1)
            for n, w in enumerate((3, 1, 2)):
                pool.wait_ge(s_whi, KC + n + 1)
                low(wkvs[:, w, 1, :], kv_land[:, w, :], wkvs[:, w, 0, :]).then_inc(s_wlo, 1)

            def w12_lo(e, s):
                pool.wait_ge(s_w12h, e + 1)
                low(wsp[:, s, 1, W12], stage[:, s, W12], wsp[:, s, 0, W12]).then_inc(s_w12l, 1)

            def w3_lo(e, s):
                pool.wait_ge(s_w3h, e + 1)
                low(wsp[:, s, 1, W3], stage[:, s, W3], wsp[:, s, 0, W3]).then_inc(s_w3l, 1)

            w12_lo(0, 0)
            w3_lo(0, 0)
            w12_lo(1, 1)
            pool.wait_ge(s_b3h, 1)
            low(b3[1], b3s[0:E_ROUTED + 1, :], b3[0]).then_inc(s_b3l, 1)

            def rms_phase(r0, iters, tiles, quarter):
                def tile_low(r, j):
                    pool.wait_ge(s_nh, r + 1)
                    low(hlr[:, j % 4, 1, :], f32r[:, 2 + j % 2, :], hlr[:, j % 4, 0, :]).then_inc(s_nl, 1)

                def body(i, first):
                    for j in range(tiles):
                        if not first or j >= 2:
                            tile_low(r0 + tiles * i + j - 2, (j - 2) % tiles)
                        for c in QUARTERS[j % 4]:
                            quarter(i, j // 4, c)

                body(0, True)
                with pool.Fori(1, iters) as i:
                    body(i, False)
                for j in range(2):
                    tile_low(r0 + tiles * iters - 2 + j, tiles - 2 + j)

            rms_phase(0, 4, 4, lambda i, g, c: None)

            with pool.Fori(0, NE // 2 - 1) as i:
                for s in range(2):
                    w12_lo(2 * i + s + 2, s)
                    w3_lo(2 * i + s + 1, 1 - s)
            w3_lo(NE - 1, 1)

            def quarter_lo(slot, c, q):
                pool.wait_ge(s_wqh, q + 1)
                at = slice(c * GW, (c + 1) * GW)
                low(wsp[:, slot, 1, at], stage[:, slot, at], wsp[:, slot, 0, at]).then_inc(s_wql, 1)

            for c in range(4):
                quarter_lo(0, c, c)
            rms_phase(16, 4, 2 * NT, lambda i, s, c: quarter_lo(1 - s, c, 8 * i + 4 + 4 * s + c))

            def prob_hi(j, k, first):
                summed, freed = k + 1, k - 3
                if not first:
                    summed, freed = pool.to_reg(summed), pool.to_reg(freed)
                pool.wait_ge(s_nl, 16 + NT * KVH)
                pool.wait_ge(s_r0, summed)
                if not first:
                    pool.wait_ge(s_T, freed)
                pool.tensor_scalar(rinv[:, 1, j % 4:j % 4 + 1], rinv[:, 0, j % 4:j % 4 + 1], PSCALE, None, ALU.mult)
                pool.tensor_scalar(hlr[:, j % 4, 0, :], f32r[:, j % 4, :], rinv[:, 0, j % 4:j % 4 + 1], PSCALE,
                                   ALU.mult, ALU.mult).then_inc(s_ph, 1)

            for j in range(4):
                prob_hi(j, j, True)
            with pool.Fori(1, 4 * KVH) as u:
                for j in range(4):
                    prob_hi(j, 4 * u + j, False)

            for c in range(4):
                quarter_lo(1, c, 4 * (KVH + 1) + c)
            with pool.Fori(0, KVH // 2 - 2) as i:
                for s in range(2):
                    for c in range(4):
                        quarter_lo(s, c, 4 * (KVH + 2) + 8 * i + 4 * s + c)
            for n in range(4):
                for c in range(4):
                    pool.wait_ge(s_wqh, 4 * (2 * KVH - 2 + n) + c + 1)
                    at = slice(c * GW, (c + 1) * GW)
                    low(tail[:, n, 1, at], stage[:, n % 2, at], tail[:, n, 0, at]).then_inc(s_wql, 1)
            for t in range(NT):
                pool.wait_ge(s_zh, t + 1)
                low(hlr[:, t, 1, :], f32r[:, t, :], hlr[:, t, 0, :]).then_inc(s_zl, 1)

        @block.vector
        def _(dve):
            linked = [0]

            def link(ins):
                ins.then_inc(s_dve, 1)
                linked[0] += 1
                dve.wait_ge(s_dve, linked[0])

            def spread(ap, n):
                return ap.unsqueeze(len(ap.shape)).to_broadcast(list(ap.shape) + [n])

            def layer_norm(tiles=slice(0, NT)):
                each = range(tiles.start, tiles.stop)
                for t in each:
                    last = dve.bn_stats(st6[:, t, :], x_sb[:, t, :])
                link(last)
                for t in each:
                    last = dve.bn_aggr(mv[:, t, :], st6[:, t, :])
                link(last)
                var, y, tmp = nw[:, 0, tiles], nw[:, 1, tiles], nw[:, 2, tiles]
                link(dve.tensor_scalar(var, mv[:, tiles, 1], EPS, None, ALU.add))
                link(dve.tensor_scalar(y.bitcast(I32), var.bitcast(I32), 1, None, ALU.arith_shift_right))
                link(dve.tensor_scalar(y.bitcast(I32), y.bitcast(I32), -1.0, RSQRT_MAGIC, ALU.mult, ALU.add))
                for _ in range(3):
                    link(dve.scalar_tensor_tensor(out=tmp, in0=y, scalar=-0.5, in1=y, op0=ALU.mult, op1=ALU.mult))
                    link(dve.tensor_tensor(tmp, tmp, var, ALU.mult))
                    link(dve.scalar_tensor_tensor(out=y, in0=tmp, scalar=1.5, in1=y, op0=ALU.add, op1=ALU.mult))

            def normalise(t):
                return dve.tensor_scalar(f32r[:, t, :], x_sb[:, t, :], mv[:, t, 0:1], nw[:, 1, t:t + 1],
                                         ALU.subtract, ALU.mult)

            for c in range(KC):
                dve.wait_ge(s_c0h, c + 1)
                dve.tensor_tensor(ctxs[:, c, 1, 0:CTX], stage[:, 0, c * CTX:(c + 1) * CTX], ctxs[:, c, 0, 0:CTX],
                                  ALU.subtract).then_inc(s_c0l, 1)

            dve.wait_ge(s_par, 16)
            for c in (0, 2):
                last = dve.reciprocal(scs[:, 4 + c // 2:5 + c // 2], scs[:, c:c + 1])
            dve.tensor_tensor(scs[:, 6:7], scs[:, 0:1], scs[:, 2:3], ALU.mult)
            for c in (1, 3):
                dve.tensor_scalar(scs[:, 7 + c // 2:8 + c // 2], scs[:, c:c + 1], -1.0, MID, ALU.mult, ALU.add)
            dve.memset(scs[:, 12:13], EPS)
            dve.memset(scs[:, 13:14], 2 * EPS)
            dve.memset(ones[:, :], 1.0)
            dve.memset(ones128, 1.0)
            for t in range(NT):
                dve.memset(gt[:, t, E_ROUTED:NE], 1.0)
            link(dve.scalar_tensor_tensor(out=wneg, in0=wneg, scalar=-1.0, in1=identf,
                                          op0=ALU.mult, op1=ALU.mult))
            dve.wait_ge(s_id, 4)
            dve.tensor_copy(identf, ident[:, :])
            for c in range(2):
                last = dve.tensor_tensor(scs[:, 9 + c:10 + c], scs[:, 6:7], scs[:, 7 + c:8 + c], ALU.mult)
            link(last)
            link(dve.scalar_tensor_tensor(out=scs[:, 11:12], in0=scs[:, 9:10], scalar=float(D), in1=scs[:, 8:9],
                                          op0=ALU.mult, op1=ALU.mult))
            def v_lo(hg, tiles):
                at = slice(hg * GW, (hg + 1) * GW)
                for n in tiles:
                    dve.wait_ge(s_vh, NST * hg + n + 1)
                    dve.tensor_tensor(v_sb[:, n, 1, at], v_bank(hg, n)[:, :], v_sb[:, n, 0, at],
                                      ALU.subtract).then_inc(s_vfree, 1)

            dve.wait_ge(s_x, 16)
            layer_norm()
            for t in range(NT):
                last = normalise(t)
            link(last)
            for t in range(NT):
                last = dve.tensor_scalar(f32r[:, t, :], f32r[:, t, :], scs[:, 4:5], scs[:, 1:2], ALU.mult, ALU.add)
            link(last)
            for t in range(NT):
                last = dve.tensor_scalar(f32r[:, t, :], f32r[:, t, :], 0.0, QMAX, ALU.max, ALU.min)
            link(last)
            for t in range(NT):
                dve.tensor_scalar(hlr[:, t, 0, :], f32r[:, t, :], ROUND, ROUND + MID, ALU.add, ALU.subtract).then_inc(s_xq, 1)
            v_lo(0, (0, 1))
            half = KC * D
            for b in range(BATCH):
                c32 = cnat[:, b * half:(b + 1) * half]
                dve.wait_ge(s_c1, b + 1)
                link(dve.tensor_scalar(c32, c32, 0.0, QMAX, ALU.max, ALU.min))
                dve.tensor_scalar(cq[:, b * half:(b + 1) * half], c32, ROUND, ROUND + MID, ALU.add, ALU.subtract)\
                   .then_inc(s_cq, 1)
                v_lo(0, ((2, 3), (4, 5, 6, 7))[b])
            dve.wait_ge(s_rwh, 1)
            dve.tensor_tensor(rws[:, 1, :], rw, rws[:, 0, :], ALU.subtract).then_inc(s_rws, 1)
            dve.wait_ge(s_sums, BATCH + 1)
            dve.tensor_scalar(nw[:, 3, :], ps[4][:, 0:NT], scs[:, 10:11], scs[:, 11:12], ALU.mult, ALU.add).then_inc(s_nw3, 1)
            for t in range(NT):
                dve.wait_ge(s_corr, t + 1)
                last = dve.tensor_tensor(x_sb[:, t, :], x_sb[:, t, :], f32r[:, t, :], ALU.add)
            link(last)
            for t in range(NT):
                dve.wait_ge(s_main, t + 1)
                last = dve.scalar_tensor_tensor(out=x_sb[:, t, :], in0=ps[t][:, :], scalar=scs[:, 6:7],
                                                in1=x_sb[:, t, :], op0=ALU.mult, op1=ALU.add)
            link(last)

            def ln_split(n):
                layer_norm()
                for t in range(NT):
                    normalise(t).then_inc(s_ln, 1)
                for t in range(NT):
                    dve.wait_ge(s_lnh, NT * n + t + 1)
                    dve.tensor_tensor(hlr[:, t, 1, :], f32r[:, t, :], hlr[:, t, 0, :], ALU.subtract).then_inc(s_lnl, 1)

            def ln_copies(n):
                for t in range(0, NT, 2):
                    dve.wait_ge(s_lnT, NT * n + t + 1)
                    dve.tensor_copy(words(xT[:, t, :, :]), ps[t][:, :].rearrange("p (l w) -> p l w", l=2)).then_inc(s_lnTc[0], 1)

            ln_split(0)
            v_lo(1, (0,))
            ln_copies(0)
            v_lo(1, (1, 2, 3))

            lg, ex = sml[:, 0:4, :], sml[:, 4:8, :]
            dve.wait_ge(s_rt, 1)
            link(dve.tensor_tensor(lg, ps[4][:, 0:NT * E_ROUTED].rearrange("p (t e) -> p t e", t=NT),
                                   rb[:, 0, :].rearrange("p (t e) -> p t e", t=NT), ALU.add))
            link(dve.tensor_reduce(rstat[:, 0, :], lg, AX_X, ALU.max))
            dve.tensor_tensor(lg, lg, spread(rstat[:, 0, :], E_ROUTED), ALU.subtract).then_inc(s_lg, 2)
            dve.wait_ge(s_rex, 1)
            link(dve.tensor_reduce(rstat[:, 1, :], ex, AX_X, ALU.add))
            link(dve.reciprocal(rstat[:, 2, :], rstat[:, 1, :]))
            link(dve.tensor_tensor(ex, ex, spread(rstat[:, 2, :], E_ROUTED), ALU.mult))
            link(dve.tensor_tensor(ex, ex, rb[:, 1, :].rearrange("p (t e) -> p t e", t=NT), ALU.add))

            def ranks(vals, n, dst):
                gt_, eq_ = (c[:, 0:NT * n * n].rearrange("p (t i j) -> p t i j", t=NT, i=n) for c in (cmp_gt, cmp_eq))
                other = vals.unsqueeze(2).to_broadcast([P, NT, n, n])
                own = spread(vals, n)
                below = lower[:, 0:n, 0:n].unsqueeze(1).to_broadcast([P, NT, n, n])
                dve.tensor_tensor(gt_, other, own, ALU.is_gt)
                link(dve.tensor_tensor(eq_, other, own, ALU.is_equal))
                link(dve.tensor_tensor(eq_, eq_, below, ALU.mult))
                link(dve.tensor_tensor(gt_, gt_, eq_, ALU.add))
                link(dve.tensor_reduce(dst, gt_, AX_X, ALU.add))

            gmax = lg[:, :, 0:GROUPS]
            grank = lg[:, :, GROUPS:2 * GROUPS]
            masked = lg[:, :, :]
            link(dve.tensor_reduce(gmax, ex.rearrange("p t (g e) -> p t g e", g=GROUPS), AX_X, ALU.max))
            ranks(gmax, GROUPS, grank)
            link(dve.tensor_scalar(rstat[:, :, :], grank, float(TOPG), -BIG, ALU.is_ge, ALU.mult))
            link(dve.tensor_tensor(masked.rearrange("p t (g e) -> p t g e", g=GROUPS), ex.rearrange("p t (g e) -> p t g e", g=GROUPS),
                                   spread(rstat[:, :, :], EPG), ALU.add))

            def gates():
                ranks(masked, E_ROUTED, rb[:, 0, :].rearrange("p (t e) -> p t e", t=NT))
                dve.scalar_tensor_tensor(out=gt[:, :, 0:E_ROUTED], in0=rb[:, 0, :].rearrange("p (t e) -> p t e", t=NT),
                                         scalar=float(TOPE), in1=ex, op0=ALU.is_lt, op1=ALU.mult).then_inc(s_gate, 1)

            def rms_phase(r0, iters, tiles, weighted, after_first=None):
                def sums(r, j, first):
                    dve.wait_ge(s_sq, r + 1)
                    if not first or j >= 2:
                        dve.wait_ge(s_root, r - 1)
                    dve.tensor_reduce(ss[:, j % 2, :], f32r[:, j % 2, :].rearrange("p (h d) -> p h d", h=REP),
                                      AX_X, ALU.add).then_inc(s_ss, 1)

                def normed(r, j, first):
                    dve.wait_ge(s_root, r + 1)
                    dve.reciprocal(rrt[:, j % 2, :], root[:, j % 2, :]).then_inc(s_rr, 1)
                    dve.wait_ge(s_rr, r + 1)
                    if not first or j >= 2:
                        dve.wait_ge(s_nl, r - 1)
                    dst, bank = f32r[:, 2 + j % 2, :], ps[j % 4]
                    if weighted:
                        for h in range(REP):
                            at = slice(h * HD, (h + 1) * HD)
                            last = dve.scalar_tensor_tensor(out=dst[:, at], in0=bank[:, at], scalar=rrt[:, j % 2, h:h + 1],
                                                            in1=wneg, op0=ALU.mult, op1=ALU.mult)
                    else:
                        last = dve.tensor_tensor(dst.rearrange("p (h d) -> p h d", h=REP),
                                                 bank[:, :].rearrange("p (h d) -> p h d", h=REP),
                                                 spread(rrt[:, j % 2, :], HD), ALU.mult)
                    last.then_inc(s_nrm, 1)

                def body(i, first):
                    for j in range(tiles):
                        r = r0 + tiles * i + j
                        sums(r, j, first)
                        if not first or j >= 1:
                            normed(r - 1, (j - 1) % tiles, first and j - 1 < 2)

                body(0, True)
                if after_first:
                    after_first()
                with dve.Fori(1, iters) as i:
                    body(i, False)
                normed(r0 + tiles * iters - 1, tiles - 1, False)

            rms_phase(0, 4, 4, True, gates)

            dve.wait_ge(s_mask, 16)
            dve.tensor_scalar(nmask[:, :, :], nmask[:, :, :], -8.0, None, ALU.mult)

            dve.wait_ge(s_gT, 1)
            dve.tensor_copy(gateT[0:NE, :], ps[5][0:NE, :]).then_inc(s_gTc, 1)
            dve.wait_ge(s_gh, 1)
            dve.tensor_tensor(gatesT[1], gateT[0:E_ROUTED + 1, :], gatesT[0], ALU.subtract).then_inc(s_gl, 1)

            def expert(e, s):
                tile, bank = f32r[:, s, :], ps[5 + 2 * s]
                dve.wait_ge(s_silu, e + 1)
                dve.wait_ge(s_up, 2 * e + 2)
                dve.scalar_tensor_tensor(out=tile, in0=bank[:, :], scalar=mb[:, 1, bass.ds(e, 1)], in1=tile,
                                         op0=ALU.add, op1=ALU.mult).then_inc(s_hx, 1)
                dve.wait_ge(s_hx, e + 1)
                dve.wait_ge(s_gload[s], 8 * (e - s) + 16)
                dve.tensor_tensor(tile, tile, gate_bc[s], ALU.mult).then_inc(s_hg, 1)
                dve.wait_ge(s_hh, e + 1)
                dve.tensor_tensor(hlr[:, s, 1, :], tile, hlr[:, s, 0, :], ALU.subtract).then_inc(s_hl, 1)

            with dve.Fori(0, NE // 2) as i:
                for s in range(2):
                    expert(2 * i + s, s)
            dve.wait_ge(s_dn, NE)
            for t in range(NT):
                last = dve.tensor_tensor(x_sb[:, t, :], ps[t][:, :], x_sb[:, t, :], ALU.add)
            link(last)
            ln_split(1)
            ln_copies(1)
            v_lo(1, (4, 5, 6, 7))
            rms_phase(16, 4, 2 * NT, False)

            def masked_scores(j, k, qt, first):
                scored, freed = k + 1, k - 3
                if not first:
                    scored, freed = dve.to_reg(scored), dve.to_reg(freed)
                dve.wait_ge(s_mask, 16)
                dve.wait_ge(s_s, scored)
                if first and 2 <= j < 4:
                    dve.wait_ge(s_nl, 16 + NT * KVH - 3 + j)
                if not first or j >= 4:
                    dve.wait_ge(s_pl, freed)
                dve.tensor_tensor_reduce(f32r[:, j % 4, :], ps[j % 4][:, :], nmask[:, qt, :], 0.125, BIG,
                                         ALU.add, ALU.min, mneg[:, j % 4:j % 4 + 1]).then_inc(s_t, 1)

            def inverse_sum(j, k):
                dve.wait_ge(s_e, k + 1)
                dve.reciprocal(rinv[:, 0, j % 4:j % 4 + 1], psum_col[:, j % 4:j % 4 + 1]).then_inc(s_r0, 1)

            def prob_lo(j, k):
                dve.wait_ge(s_ph, k + 1)
                dve.scalar_tensor_tensor(out=hlr[:, j % 4, 1, :], in0=f32r[:, j % 4, :], scalar=rinv[:, 1, j % 4:j % 4 + 1],
                                         in1=hlr[:, j % 4, 0, :], op0=ALU.mult, op1=ALU.subtract).then_inc(s_pl, 1)

            def o_lo(w, mw):
                dve.wait_ge(s_oh, w + 1)
                dve.scalar_tensor_tensor(out=q_sb[:, bass.ds(w, 1), 1, :], in0=ps[6 + mw % 2][:, :], scalar=1.0 / PSCALE,
                                         in1=q_sb[:, bass.ds(w, 1), 0, :], op0=ALU.mult, op1=ALU.subtract).then_inc(s_ol, 1)

            def attention(g, first):
                for j in range(4 * REP):
                    k = 16 * g + j
                    m, hh = divmod(j, REP)
                    masked_scores(j, k, m % QT_PER_B, first)
                    if not first or j >= 1:
                        inverse_sum((j - 1) % 4, k - 1)
                    if not first or j >= 2:
                        prob_lo((j - 2) % 4, k - 2)
                    if hh == 1 and (not first or m >= 3):
                        o_lo(4 * g + m - 3, (m - 3) % 4)

            attention(0, True)
            with dve.Fori(1, KVH) as g:
                attention(g, False)
            end = 16 * KVH
            inverse_sum(3, end - 1)
            prob_lo(2, end - 2)
            prob_lo(3, end - 1)
            for m in range(3):
                o_lo(4 * KVH - 3 + m, (m + 1) % 4)

            dve.wait_ge(s_lw, 2)
            dve.tensor_tensor(lwqs[:, 1, :], lwq.rearrange("p k r -> p (k r)"), lwqs[:, 0, :], ALU.subtract)
            dve.tensor_tensor(lkys[:, 1, :], lky, lkys[:, 0, :], ALU.subtract).then_inc(s_lwl, 1)
            def queries_lo(p):
                at = slice(2 * p * P, (2 * p + 2) * P)
                dve.wait_ge(s_lqh, p + 1)
                dve.tensor_tensor(lqs[:, 1, at], ps[4][0:RD, at], lqs[:, 0, at], ALU.subtract).then_inc(s_lqs, 1)

            for t in range(NT):
                dve.wait_ge(s_ot, t + 1)
                link(dve.tensor_tensor(x_sb[:, t, :], ps[t][:, :], x_sb[:, t, :], ALU.add))
                layer_norm(slice(t, t + 1))
                if t == NT - 1:
                    queries_lo(0)
                normalise(t).then_inc(s_ln, 1)
                dve.wait_ge(s_lnh, 2 * NT + t + 1)
                dve.tensor_tensor(hlr[:, t, 1, :], f32r[:, t, :], hlr[:, t, 0, :], ALU.subtract).then_inc(s_lnl, 1)

            for p in range(2):
                tiles, own = slice(2 * p, 2 * p + 2), (2 * p, 2 * p + 1)
                if p == 1:
                    queries_lo(1)
                dve.wait_ge(s_lsc, p + 1)
                link(dve.tensor_copy(lsc[:, tiles, :], ps[5][:, 2 * p * L_EXP:(2 * p + 2) * L_EXP]
                                     .rearrange("p (t e) -> p t e", t=2)))
                for t in own:
                    last = dve.max(lm8[:, t, 0, :], lsc[:, t, :])
                link(last)
                for t in own:
                    dve.tensor_scalar(lng[:, t:t + 1], lm8[:, t, 0, 0:1], -1.0, None, ALU.mult).then_inc(s_lng, 1)
                for t in own:
                    last = dve.match_replace(lw1[:, t, :], lm8[:, t, 0, :], lsc[:, t, :], -BIG)
                link(last)
                for t in own:
                    last = dve.max(lm8[:, t, 1, :], lw1[:, t, :])
                link(last)
                for t in own:
                    last = dve.match_replace(lw2[:, t, :], lm8[:, t, 1, :], lw1[:, t, :], -BIG)
                link(last)
                link(dve.tensor_tensor(lw2[:, tiles, :], lw2[:, tiles, :], lsc[:, tiles, :], ALU.not_equal))
                dve.wait_ge(s_lex, 2 * p + 2)
                link(dve.tensor_tensor(lex[:, tiles, :], lex[:, tiles, :], lw2[:, tiles, :], ALU.mult))
                link(dve.tensor_reduce(lsum[:, tiles], lex[:, tiles, :], AX_X, ALU.add))
                inverse = lsum[:, NT + 2 * p:NT + 2 * p + 2]
                link(dve.reciprocal(inverse, lsum[:, tiles]))
                link(dve.tensor_tensor(lex[:, tiles, :], lex[:, tiles, :], spread(inverse, L_EXP), ALU.mult))
                for t in own:
                    dve.wait_ge(s_z, t + 1)
                    dve.tensor_tensor(f32r[:, t, :].rearrange("p (e r) -> p e r", r=RANK),
                                      ps[t][:, :].rearrange("p (e r) -> p e r", r=RANK),
                                      spread(lex[:, t, :], RANK), ALU.mult).then_inc(s_zg, 1)
            for t in range(NT):
                dve.wait_ge(s_y, t + 1)
                dve.scalar_tensor_tensor(out=x_sb[:, t, :], in0=ps[t][:, :], scalar=L_SCALING, in1=x_sb[:, t, :],
                                         op0=ALU.mult, op1=ALU.add).then_inc(s_fin, 1)


def kernel(x, ctx_4096, mask_1x1xSxS2_ff0, L0_xattn_x1_scale, L0_xattn_x1_zp, L0_xattn_x2_scale, L0_xattn_x2_zp,
           L0_ffn_router_w, L0_ffn_router_b, L0_ffn_router_bias, L0_ffn_ew1, L0_ffn_eb1, L0_ffn_ew2, L0_ffn_eb2,
           L0_ffn_ew3, L0_ffn_eb3, L0_ffn_sw1, L0_ffn_sb1, L0_ffn_sw2, L0_ffn_sb2, L0_ffn_sw3, L0_ffn_sb3,
           L1_xattn_q_proj_w, L1_xattn_k_proj_w, L1_xattn_v_proj_w, L1_xattn_o_proj_w, L1_xattn_q_norm_w,
           L1_xattn_k_norm_w, L1_ffn_A_w, L1_ffn_B_w, L1_ffn_Wq_w, L1_ffn_keys):
    import numpy as np
    import concourse.bacc as bacc
    from concourse.bass_utils import run_bass_kernel_spmd

    def a(v):
        return np.asarray(v)

    def chunked(w):
        return w.reshape(KC, P, -1).transpose(1, 0, 2)

    def groups(w):
        return chunked(w).reshape(P, KC, -1, GW).transpose(2, 0, 1, 3).reshape(-1, P, WG)

    def rows(v, n=1):
        return np.tile(v.reshape(1, -1), (P, n))

    ctx = a(ctx_4096)
    ctx_t = chunked(ctx.transpose(2, 0, 1).reshape(D, BATCH * CTX)).reshape(P, KC, BATCH, CTX)
    wk, wv = groups(a(L1_xattn_k_proj_w).T), groups(a(L1_xattn_v_proj_w).T)

    def experts(ew, sw):
        both = np.concatenate([ew, sw.reshape(D, 2, INTER).transpose(1, 0, 2)])
        return both.reshape(NE, KC, P, INTER).transpose(0, 2, 1, 3).reshape(NE, P, KC * INTER)

    moe = np.concatenate([experts(a(L0_ffn_ew1), a(L0_ffn_sw1)), experts(a(L0_ffn_ew2), a(L0_ffn_sw2)),
                          np.concatenate([a(L0_ffn_ew3), a(L0_ffn_sw3).reshape(2, INTER, D)])], axis=2)
    moe_b = np.stack([np.concatenate([a(L0_ffn_eb1), a(L0_ffn_sb1).reshape(2, INTER)]).T,
                      np.concatenate([a(L0_ffn_eb2), a(L0_ffn_sb2).reshape(2, INTER)]).T], axis=1)
    params = np.concatenate([rows(a(L1_xattn_q_norm_w)), rows(a(L1_xattn_k_norm_w)), moe_b.reshape(P, -1),
                             chunked(a(L0_ffn_router_w)).reshape(P, -1), rows(a(L0_ffn_router_b), NT),
                             rows(a(L0_ffn_router_bias), NT)]
                            + [rows(a(v)) for v in (L0_xattn_x1_scale, L0_xattn_x1_zp, L0_xattn_x2_scale,
                                                    L0_xattn_x2_zp)], axis=1)
    arrays = {
        "x_rows": a(x).reshape(TOK, D),
        "ctx_nat": ctx.reshape(BATCH * KC, P, D).transpose(1, 0, 2).reshape(P, -1),
        "first_chunks": np.stack([ctx_t[:, :, 0], wv[0].reshape(P, KC, GW)], axis=2).transpose(1, 0, 2, 3),
        "ctx_t": ctx_t[:, :, 1].reshape(P, WG),
        "params": params,
        "mask": a(mask_1x1xSxS2_ff0).reshape(SEQ, CTX),
        "wkv": np.stack([wk[0], wk[1], wv[1]]),
        "moe": moe,
        "moe_b3": np.concatenate([a(L0_ffn_eb3), a(L0_ffn_sb3).reshape(1, D)]),
        "wq": groups(a(L1_xattn_q_proj_w).T),
        "wo": a(L1_xattn_o_proj_w).T.reshape(KVH, REP, P, D).transpose(0, 2, 1, 3).reshape(KVH, P, WG),
        "a_w": chunked(a(L1_ffn_A_w).T).reshape(P, WG),
        "b_w": chunked(a(L1_ffn_B_w).T).reshape(P, WG),
        "l_wq": chunked(a(L1_ffn_Wq_w).T),
        "l_keys": a(L1_ffn_keys).T,
    }
    nc = bacc.Bacc("TRN2", target_bir_lowering=False, num_devices=1)
    sent, args = {}, {}
    for name, v in arrays.items():
        v = np.ascontiguousarray(v)
        sent["in_" + name] = v
        args[name] = nc.dram_tensor("in_" + name, v.shape, mybir.dt.from_np(v.dtype), kind="ExternalInput").ap()
    out = nc.dram_tensor("out_x", (TOK, D), F32, kind="ExternalOutput").ap()
    xattn_ffn_kernel(nc, out=out, **args)
    r = run_bass_kernel_spmd(nc, [sent], core_ids=[0])
    return r.results[0]["out_x"].reshape(BATCH, SEQ, D)
```
